# Optimizing a Trainium2 kernel written in Bass

```python
import numpy as np
import jax
import jax.numpy as jnp

def _softmax(x, axis=-1):
    return jax.nn.softmax(x, axis=axis)

def _gelu(x):
    return jax.nn.gelu(x, approximate=True)

def _silu(x):
    return jax.nn.silu(x)

def _sigmoid(x):
    return jax.nn.sigmoid(x)

def _layernorm(x, axis=-1, eps=1e-05):
    m = jnp.mean(x, axis=axis, keepdims=True)
    v = jnp.var(x, axis=axis, keepdims=True)
    return (x - m) / jnp.sqrt(v + eps)

def _scatter_add(tgt, idx, src, axis=0):
    return tgt.at[idx].add(src)

def _segment_sum(src, seg, n):
    return jax.ops.segment_sum(src, seg, n)
kernel_name = 'mk_flamingo_gated_d4_seqx_r8_7597c8'

def setup_inputs(seed: int=0):
    np.random.seed(seed)
    _w = jnp.asarray

    def _rec_inputs():
        import jax
        import jax.numpy as jnp
        _rk = jax.random.key(seed)
        x = -0.0003929 + 0.9999 * jax.random.normal(jax.random.fold_in(_rk, 1), (8, 256, 128), jnp.float32)
        _lenS = 256 - jax.random.randint(jax.random.fold_in(_rk, 7), (8,), 0, max(1, 256 // 4) + 1, jnp.int32)
        _lenS2 = 64 - jax.random.randint(jax.random.fold_in(_rk, 8), (8,), 0, max(1, 64 // 4) + 1, jnp.int32)
        _ctx_2048P = jax.random.normal(jax.random.fold_in(_rk, 11), (8, 16, 256), jnp.float32)
        _ctx_2048c = jax.random.dirichlet(jax.random.fold_in(_rk, 511), 0.3 * jnp.ones((16,), jnp.float32), (8, 64))
        _ctx_2048t = jnp.einsum('bsk,bkd->bsd', _ctx_2048c, _ctx_2048P)
        _ctx_2048t = _ctx_2048t * jax.lax.rsqrt(jnp.mean(jnp.square(_ctx_2048t)) + 1e-12) * 0.953939
        ctx_2048 = 4.13588e-05 + 0.999923 * (_ctx_2048t + 0.3 * jax.random.normal(jax.random.fold_in(_rk, 611), (8, 64, 256), jnp.float32))
        _validS = jnp.arange(256)[None, :] < _lenS[:, None]
        _validS2 = jnp.arange(64)[None, :] < _lenS2[:, None]
        _causal = jnp.tril(jnp.ones((256, 256), dtype=bool))
        mask_BxS2_if0 = jnp.where(jnp.ones((8, 64), dtype=bool), 4, 0).astype(jnp.int32)
        mask_BxS2_ik0 = jnp.where(jnp.broadcast_to(_validS2[:, :], (8, 64)), 0, 1).astype(jnp.int32)
        _g = jax.random.normal(jax.random.fold_in(_rk, 9001), (2, 4), jnp.float32)
        _g = jnp.sign(_g) * jnp.maximum(jnp.abs(_g), 1.0) + (_g == 0) * 1.0
        g_xattn = _g[0]
        g_ffn = _g[1]
        return (x, ctx_2048, mask_BxS2_if0, mask_BxS2_ik0, g_xattn, g_ffn)
    x, ctx_2048, mask_BxS2_if0, mask_BxS2_ik0, g_xattn, g_ffn = _rec_inputs()

    def _L0_xattn_setup():
        import jax, jax.numpy as jnp
        import numpy as np
        B, L, P = (4, 512, 128)
        D_MODEL = 128
        D_GLOBAL = 256
        HEADDIM = 32
        EPSILON = 0.001
        RMS_EPS = 1e-05

        def rmsnorm(x, g, eps=RMS_EPS):
            var = jnp.mean(jnp.square(x), axis=-1, keepdims=True)
            return x * jax.lax.rsqrt(var + eps) * g

        def _hnet_depool(h, h_patch_full, patch_lens):
            h_patch = h_patch_full[..., :D_MODEL]
            bsz, plen = (h_patch.shape[0], h_patch.shape[1])
            seqlen = h.shape[1]
            logp = jnp.full((bsz, plen), -EPSILON, dtype=jnp.float32)
            bidx = jnp.cumsum(patch_lens, axis=1) - 1
            boundary_mask = jnp.zeros((bsz, seqlen), dtype=jnp.int32)
            boundary_mask = boundary_mask.at[jnp.arange(bsz)[:, None], bidx].set(1)
            dt = (-jnp.log(-jnp.expm1(logp))).astype(h_patch.dtype)
            x = h_patch / dt[..., None]
            n_heads = D_MODEL // HEADDIM
            A = -jnp.ones((n_heads,), dtype=jnp.float32)
            bcoef = jnp.exp(logp).astype(h_patch.dtype)
            x4 = x.reshape(bsz, plen, n_heads, HEADDIM)
            a = jnp.exp(dt[:, :, None] * A[None, None, :])
            u = (dt * bcoef)[:, :, None, None] * x4
            a_b = jnp.broadcast_to(a[..., None], u.shape)

            def comb(lft, rgt):
                aL, uL = lft
                aR, uR = rgt
                return (aL * aR, uL * aR + uR)
            _, s = jax.lax.associative_scan(comb, (a_b, u), axis=1)
            depool = s.reshape(bsz, plen, D_MODEL)
            plug = jnp.clip(jnp.cumsum(boundary_mask, axis=1) - 1, 0, plen - 1)
            depool_out = depool[jnp.arange(bsz)[:, None], plug]
            return depool_out + h
        key = jax.random.key(seed)
        k1, k2, k3, k4 = jax.random.split(key, 4)
        embeds = jax.random.normal(k1, (B, L, D_MODEL), dtype=jnp.float32)
        patch_embeds = jax.random.normal(k2, (B, P, D_GLOBAL), dtype=jnp.float32)
        patch_lens = jnp.full((B, P), L // P, dtype=jnp.int64)
        W_in = jax.random.normal(k3, (D_MODEL, D_MODEL), dtype=jnp.float32) * 0.02
        b_in = jnp.zeros((D_MODEL,), dtype=jnp.float32)
        g_res = jnp.ones((D_MODEL,), dtype=jnp.float32)
        g_init = jnp.ones((D_GLOBAL,), dtype=jnp.float32)
        return {'embeds': embeds, 'patch_embeds': patch_embeds, 'patch_lens': patch_lens, 'W_in': W_in, 'b_in': b_in, 'g_res': g_res, 'g_init': g_init}
    _L0_xattn_all = _L0_xattn_setup()
    _L0_xattn_in = {k: v for k, v in _L0_xattn_all.items() if k in ('W_in', 'b_in', 'g_res', 'g_init')}
    del _L0_xattn_all

    def _L0_ffn_setup():
        import jax, jax.numpy as jnp
        import numpy as np
        B, S, H = (2, 128, 128)
        DFF = 256
        E = 8
        TOPK = 2

        def _expert_ffn(x, w1, b1, w2, b2, wg, bg, w3, b3):
            x1 = jnp.einsum('bsh,hf->bsf', x, w1) + b1
            x2 = jnp.einsum('bsh,hf->bsf', x, w2) + b2
            z = x1 * x2
            s = jax.nn.silu(jnp.einsum('bsf,fg->bsg', z, wg) + bg)
            return jnp.einsum('bsg,gh->bsh', s, w3) + b3
        key = jax.random.key(seed)
        ks = jax.random.split(key, 12)
        sc = 0.02
        return {'x': jax.random.normal(ks[0], (B, S, H), jnp.float32), 'gate_w': jax.random.normal(ks[1], (H, E), jnp.float32) * sc, 'gate_b': jnp.zeros((E,), jnp.float32), 'w1': jax.random.normal(ks[2], (E, H, DFF), jnp.float32) * sc, 'b1': jnp.zeros((E, DFF), jnp.float32), 'w2': jax.random.normal(ks[3], (E, H, DFF), jnp.float32) * sc, 'b2': jnp.zeros((E, DFF), jnp.float32), 'wg': jax.random.normal(ks[4], (E, DFF, DFF), jnp.float32) * sc, 'bg': jnp.zeros((E, DFF), jnp.float32), 'w3': jax.random.normal(ks[5], (E, DFF, H), jnp.float32) * sc, 'b3': jnp.zeros((E, H), jnp.float32)}
    _L0_ffn_all = _L0_ffn_setup()
    _L0_ffn_in = {k: v for k, v in _L0_ffn_all.items() if k in ('gate_w', 'gate_b', 'w1', 'b1', 'w2', 'b2', 'wg', 'bg', 'w3', 'b3')}
    del _L0_ffn_all

    def _L1_xattn_setup():
        import jax, jax.numpy as jnp
        import numpy as np
        NUM_HEADS = 16
        key = jax.random.key(seed)
        ks = jax.random.split(key, 5)
        dim = 128
        B, N, N_c = (4, 128, 32)
        x = jax.random.normal(ks[0], (B, N, dim), dtype=jnp.float32)
        context = jax.random.normal(ks[1], (B, N_c, 2 * dim), dtype=jnp.float32)
        w_qkv = jax.random.normal(ks[2], (3 * dim, dim), dtype=jnp.float32) * 0.02
        w_proj = jax.random.normal(ks[3], (dim, dim), dtype=jnp.float32) * 0.02
        b_proj = jax.random.normal(ks[4], (dim,), dtype=jnp.float32) * 0.02
        return {'x': x, 'context': context, 'w_qkv': w_qkv, 'w_proj': w_proj, 'b_proj': b_proj}
    _L1_xattn_all = _L1_xattn_setup()
    _L1_xattn_in = {k: v for k, v in _L1_xattn_all.items() if k in ('w_qkv', 'w_proj', 'b_proj')}
    del _L1_xattn_all

    def _L1_ffn_setup():
        import jax, jax.numpy as jnp
        import numpy as np
        H = 16
        E = 8
        EPS = 1e-05

        def _layernorm(x, g, b):
            mu = jnp.mean(x, axis=-1, keepdims=True)
            var = jnp.mean(jnp.square(x - mu), axis=-1, keepdims=True)
            return (x - mu) * jax.lax.rsqrt(var + EPS) * g + b
        key = jax.random.key(seed)
        T, B, C = (128, 8, 128)
        ks = jax.random.split(key, 12)
        s = 0.02
        return {'x': jax.random.normal(ks[0], (T, B, C), jnp.float32), 'in_proj_w': jax.random.normal(ks[1], (3 * C, C), jnp.float32) * s, 'in_proj_b': jnp.zeros((3 * C,), jnp.float32), 'out_w': jax.random.normal(ks[2], (C, C), jnp.float32) * s, 'out_b': jnp.zeros((C,), jnp.float32), 'ln1_g': jnp.ones((C,), jnp.float32), 'ln1_b': jnp.zeros((C,), jnp.float32), 'router_w': jax.random.normal(ks[3], (E, C), jnp.float32) * s, 'router_b': jnp.zeros((E,), jnp.float32), 'w1': jax.random.normal(ks[4], (E, C, C), jnp.float32) * s, 'b1': jnp.zeros((E, C), jnp.float32), 'w2': jax.random.normal(ks[5], (E, C, C), jnp.float32) * s, 'b2': jnp.zeros((E, C), jnp.float32), 'ln2_g': jnp.ones((C,), jnp.float32), 'ln2_b': jnp.zeros((C,), jnp.float32)}
    _L1_ffn_all = _L1_ffn_setup()
    _L1_ffn_in = {k: v for k, v in _L1_ffn_all.items() if k in ('in_proj_w', 'in_proj_b', 'out_w', 'out_b', 'ln1_g', 'ln1_b', 'router_w', 'router_b', 'w1', 'b1', 'w2', 'b2', 'ln2_g', 'ln2_b')}
    del _L1_ffn_all

    def _L2_xattn_setup():
        import jax, jax.numpy as jnp
        import numpy as np
        UNITS = 128
        NUM_HEADS = 8

        def _split_heads(x, n):
            B, S, D = x.shape
            return x.reshape(B, S, n, D // n).transpose(0, 2, 1, 3)
        key = jax.random.key(seed)
        k1, k2, k3 = jax.random.split(key, 3)
        B, S = (8, 128)
        memory = jax.random.normal(k1, (B, S, 2 * UNITS), dtype=jnp.float32)
        query = jax.random.normal(k2, (B, S, UNITS), dtype=jnp.float32)
        seq_mask = jax.random.randint(k3, (B, S), 0, 2, dtype=jnp.int32)
        b = jnp.zeros((1,), dtype=jnp.float32)
        return {'memory': memory, 'query': query, 'seq_mask': seq_mask, 'b': b}
    _L2_xattn_all = _L2_xattn_setup()
    _L2_xattn_in = {k: v for k, v in _L2_xattn_all.items() if k in ('b',)}
    del _L2_xattn_all

    def _L2_ffn_setup():
        import math
        import jax, jax.numpy as jnp
        import numpy as np
        D_MODEL = 128
        D_HIDDEN = 256
        N_EXPERTS = 8
        TOP_K = 2
        CAPACITY_FACTOR = 1.25

        def _moe_forward(x, w_router, w_gate, w_down):
            B, T, D = x.shape
            N = B * T
            xf = x.reshape(N, D)
            logits = xf.astype(jnp.float32) @ w_router.T
            gates = jax.nn.softmax(logits, axis=-1)
            topk_gates, topk_idx = jax.lax.top_k(gates, TOP_K)
            expert_mask = jax.nn.one_hot(topk_idx, N_EXPERTS, dtype=jnp.int32).sum(axis=1)
            capacity = math.ceil(N / N_EXPERTS * CAPACITY_FACTOR)
            position_in_expert = jnp.cumsum(expert_mask, axis=0) - 1
            expert_mask = expert_mask * (position_in_expert < capacity)
            keep = jnp.take_along_axis(expert_mask, topk_idx, axis=1) > 0
            topk_gates = topk_gates * keep
            topk_gates = topk_gates / (topk_gates.sum(axis=-1, keepdims=True) + 1e-06)
            hidden = jax.nn.silu(xf @ w_gate.T)
            combine = (topk_gates[:, :, None] * jax.nn.one_hot(topk_idx, N_EXPERTS, dtype=topk_gates.dtype)).sum(axis=1)
            y = jnp.zeros((N, D), dtype=x.dtype)
            for e in range(N_EXPERTS):
                y = y + combine[:, e:e + 1] * (hidden @ w_down[e].T)
            return y.reshape(B, T, D)
        key = jax.random.key(seed)
        k0, k1, k2, k3 = jax.random.split(key, 4)
        B, T = (2, 256)
        x = jax.random.normal(k0, (B, T, D_MODEL), dtype=jnp.float32)
        w_router = jax.random.normal(k1, (N_EXPERTS, D_MODEL), dtype=jnp.float32) * 0.02
        w_gate = jax.random.normal(k2, (D_HIDDEN, D_MODEL), dtype=jnp.float32) * 0.02
        w_down = jax.random.normal(k3, (N_EXPERTS, D_MODEL, D_HIDDEN), dtype=jnp.float32) * 0.02
        return {'x': x, 'w_router': w_router, 'w_gate': w_gate, 'w_down': w_down}
    _L2_ffn_all = _L2_ffn_setup()
    _L2_ffn_in = {k: v for k, v in _L2_ffn_all.items() if k in ('w_router', 'w_gate', 'w_down')}
    del _L2_ffn_all

    def _L3_xattn_setup():
        import jax, jax.numpy as jnp
        import numpy as np
        B, N, DIM = (8, 512, 128)
        M, CTX = (32, 256)
        HEADS, DH = (16, 64)
        INNER = HEADS * DH
        EPS = 1e-06

        def _split_heads(t):
            b, n, _ = t.shape
            return t.reshape(b, n, HEADS, DH).transpose(0, 2, 1, 3)
        key = jax.random.key(seed)
        ks = jax.random.split(key, 6)
        x = jax.random.normal(ks[0], (B, N, DIM), dtype=jnp.float32)
        context = jax.random.normal(ks[1], (B, M, CTX), dtype=jnp.float32)
        Wq = jax.random.normal(ks[2], (DIM, INNER), dtype=jnp.float32) / np.sqrt(DIM)
        Wkv = jax.random.normal(ks[3], (CTX, 2 * INNER), dtype=jnp.float32) / np.sqrt(CTX)
        null_kv = jax.random.normal(ks[4], (2, DH), dtype=jnp.float32) / np.sqrt(2.0)
        Wout = jax.random.normal(ks[5], (INNER, DIM), dtype=jnp.float32) / np.sqrt(INNER)
        ln_scale = jnp.ones((DIM,), dtype=jnp.float32)
        ln_bias = jnp.zeros((DIM,), dtype=jnp.float32)
        return {'x': x, 'context': context, 'Wq': Wq, 'Wkv': Wkv, 'null_kv': null_kv, 'Wout': Wout, 'ln_scale': ln_scale, 'ln_bias': ln_bias}
    _L3_xattn_all = _L3_xattn_setup()
    _L3_xattn_in = {k: v for k, v in _L3_xattn_all.items() if k in ('Wq', 'Wkv', 'null_kv', 'Wout', 'ln_scale', 'ln_bias')}
    del _L3_xattn_all

    def _L3_ffn_setup():
        import math
        import jax, jax.numpy as jnp
        import numpy as np
        B, S, D, F, E = (8, 256, 128, 512, 8)
        CAPACITY_FACTOR = 1.0
        key = jax.random.key(seed)
        k1, k2, k3, k4 = jax.random.split(key, 4)
        x = jax.random.normal(k1, (B, S, D), dtype=jnp.float32)
        Wr = jax.random.normal(k2, (D, E), dtype=jnp.float32) * (1.0 / math.sqrt(D))
        W1 = jax.random.normal(k3, (E, D, F), dtype=jnp.float32) * (1.0 / math.sqrt(D))
        W2 = jax.random.normal(k4, (E, F, D), dtype=jnp.float32) * (1.0 / math.sqrt(F))
        return {'x': x, 'Wr': Wr, 'W1': W1, 'W2': W2}
    _L3_ffn_all = _L3_ffn_setup()
    _L3_ffn_in = {k: v for k, v in _L3_ffn_all.items() if k in ('Wr', 'W1', 'W2')}
    del _L3_ffn_all
    return {'x': x, 'ctx_2048': ctx_2048, 'mask_BxS2_if0': mask_BxS2_if0, 'mask_BxS2_ik0': mask_BxS2_ik0, 'g_xattn': g_xattn, 'g_ffn': g_ffn, 'L0_xattn_W_in': _L0_xattn_in['W_in'], 'L0_xattn_b_in': _L0_xattn_in['b_in'], 'L0_xattn_g_res': _L0_xattn_in['g_res'], 'L0_xattn_g_init': _L0_xattn_in['g_init'], 'L0_ffn_gate_w': _L0_ffn_in['gate_w'], 'L0_ffn_gate_b': _L0_ffn_in['gate_b'], 'L0_ffn_w1': _L0_ffn_in['w1'], 'L0_ffn_b1': _L0_ffn_in['b1'], 'L0_ffn_w2': _L0_ffn_in['w2'], 'L0_ffn_b2': _L0_ffn_in['b2'], 'L0_ffn_wg': _L0_ffn_in['wg'], 'L0_ffn_bg': _L0_ffn_in['bg'], 'L0_ffn_w3': _L0_ffn_in['w3'], 'L0_ffn_b3': _L0_ffn_in['b3'], 'L1_xattn_w_qkv': _L1_xattn_in['w_qkv'], 'L1_xattn_w_proj': _L1_xattn_in['w_proj'], 'L1_xattn_b_proj': _L1_xattn_in['b_proj'], 'L1_ffn_in_proj_w': _L1_ffn_in['in_proj_w'], 'L1_ffn_in_proj_b': _L1_ffn_in['in_proj_b'], 'L1_ffn_out_w': _L1_ffn_in['out_w'], 'L1_ffn_out_b': _L1_ffn_in['out_b'], 'L1_ffn_ln1_g': _L1_ffn_in['ln1_g'], 'L1_ffn_ln1_b': _L1_ffn_in['ln1_b'], 'L1_ffn_router_w': _L1_ffn_in['router_w'], 'L1_ffn_router_b': _L1_ffn_in['router_b'], 'L1_ffn_w1': _L1_ffn_in['w1'], 'L1_ffn_b1': _L1_ffn_in['b1'], 'L1_ffn_w2': _L1_ffn_in['w2'], 'L1_ffn_b2': _L1_ffn_in['b2'], 'L1_ffn_ln2_g': _L1_ffn_in['ln2_g'], 'L1_ffn_ln2_b': _L1_ffn_in['ln2_b'], 'L2_xattn_b': _L2_xattn_in['b'], 'L2_ffn_w_router': _L2_ffn_in['w_router'], 'L2_ffn_w_gate': _L2_ffn_in['w_gate'], 'L2_ffn_w_down': _L2_ffn_in['w_down'], 'L3_xattn_Wq': _L3_xattn_in['Wq'], 'L3_xattn_Wkv': _L3_xattn_in['Wkv'], 'L3_xattn_null_kv': _L3_xattn_in['null_kv'], 'L3_xattn_Wout': _L3_xattn_in['Wout'], 'L3_xattn_ln_scale': _L3_xattn_in['ln_scale'], 'L3_xattn_ln_bias': _L3_xattn_in['ln_bias'], 'L3_ffn_Wr': _L3_ffn_in['Wr'], 'L3_ffn_W1': _L3_ffn_in['W1'], 'L3_ffn_W2': _L3_ffn_in['W2']}

def reference(x, ctx_2048, mask_BxS2_if0, mask_BxS2_ik0, g_xattn, g_ffn, L0_xattn_W_in, L0_xattn_b_in, L0_xattn_g_res, L0_xattn_g_init, L0_ffn_gate_w, L0_ffn_gate_b, L0_ffn_w1, L0_ffn_b1, L0_ffn_w2, L0_ffn_b2, L0_ffn_wg, L0_ffn_bg, L0_ffn_w3, L0_ffn_b3, L1_xattn_w_qkv, L1_xattn_w_proj, L1_xattn_b_proj, L1_ffn_in_proj_w, L1_ffn_in_proj_b, L1_ffn_out_w, L1_ffn_out_b, L1_ffn_ln1_g, L1_ffn_ln1_b, L1_ffn_router_w, L1_ffn_router_b, L1_ffn_w1, L1_ffn_b1, L1_ffn_w2, L1_ffn_b2, L1_ffn_ln2_g, L1_ffn_ln2_b, L2_xattn_b, L2_ffn_w_router, L2_ffn_w_gate, L2_ffn_w_down, L3_xattn_Wq, L3_xattn_Wkv, L3_xattn_null_kv, L3_xattn_Wout, L3_xattn_ln_scale, L3_xattn_ln_bias, L3_ffn_Wr, L3_ffn_W1, L3_ffn_W2):
    import jax
    import jax.numpy as jnp

    def _L0_xattn_ref(embeds, patch_embeds, patch_lens, W_in, b_in, g_res, g_init):
        import jax, jax.numpy as jnp
        import numpy as np
        B, L, P = (4, 512, 128)
        D_MODEL = 128
        D_GLOBAL = 256
        HEADDIM = 32
        EPSILON = 0.001
        RMS_EPS = 1e-05

        def rmsnorm(x, g, eps=RMS_EPS):
            var = jnp.mean(jnp.square(x), axis=-1, keepdims=True)
            return x * jax.lax.rsqrt(var + eps) * g

        def _hnet_depool(h, h_patch_full, patch_lens):
            h_patch = h_patch_full[..., :D_MODEL]
            bsz, plen = (h_patch.shape[0], h_patch.shape[1])
            seqlen = h.shape[1]
            logp = jnp.full((bsz, plen), -EPSILON, dtype=jnp.float32)
            bidx = jnp.cumsum(patch_lens, axis=1) - 1
            boundary_mask = jnp.zeros((bsz, seqlen), dtype=jnp.int32)
            boundary_mask = boundary_mask.at[jnp.arange(bsz)[:, None], bidx].set(1)
            dt = (-jnp.log(-jnp.expm1(logp))).astype(h_patch.dtype)
            x = h_patch / dt[..., None]
            n_heads = D_MODEL // HEADDIM
            A = -jnp.ones((n_heads,), dtype=jnp.float32)
            bcoef = jnp.exp(logp).astype(h_patch.dtype)
            x4 = x.reshape(bsz, plen, n_heads, HEADDIM)
            a = jnp.exp(dt[:, :, None] * A[None, None, :])
            u = (dt * bcoef)[:, :, None, None] * x4
            a_b = jnp.broadcast_to(a[..., None], u.shape)

            def comb(lft, rgt):
                aL, uL = lft
                aR, uR = rgt
                return (aL * aR, uL * aR + uR)
            _, s = jax.lax.associative_scan(comb, (a_b, u), axis=1)
            depool = s.reshape(bsz, plen, D_MODEL)
            plug = jnp.clip(jnp.cumsum(boundary_mask, axis=1) - 1, 0, plen - 1)
            depool_out = depool[jnp.arange(bsz)[:, None], plug]
            return depool_out + h
        h = rmsnorm(embeds, g_res)
        h = jnp.einsum('bld,ed->ble', h, W_in) + b_in
        h_patch = rmsnorm(patch_embeds, g_init)
        return _hnet_depool(h, h_patch, patch_lens)

    def _L0_ffn_ref(x, gate_w, gate_b, w1, b1, w2, b2, wg, bg, w3, b3):
        import jax, jax.numpy as jnp
        import numpy as np
        B, S, H = (2, 128, 128)
        DFF = 256
        E = 8
        TOPK = 2

        def _expert_ffn(x, w1, b1, w2, b2, wg, bg, w3, b3):
            x1 = jnp.einsum('bsh,hf->bsf', x, w1) + b1
            x2 = jnp.einsum('bsh,hf->bsf', x, w2) + b2
            z = x1 * x2
            s = jax.nn.silu(jnp.einsum('bsf,fg->bsg', z, wg) + bg)
            return jnp.einsum('bsg,gh->bsh', s, w3) + b3
        logits = jnp.einsum('bsh,he->bse', x, gate_w) + gate_b
        topv, topi = jax.lax.top_k(logits, TOPK)
        probs = jax.nn.softmax(topv, axis=-1)
        out = jnp.zeros_like(x)
        for e in range(E):
            we = jnp.sum(probs * (topi == e), axis=-1)
            y = _expert_ffn(x, w1[e], b1[e], w2[e], b2[e], wg[e], bg[e], w3[e], b3[e])
            out = out + we[..., None] * y
        return out

    def _L1_xattn_ref(x, context, w_qkv, w_proj, b_proj):
        import jax, jax.numpy as jnp
        import numpy as np
        NUM_HEADS = 16
        B, N, C = x.shape
        H = NUM_HEADS
        D = C // H
        scale = D ** (-0.5)
        qkv = (x @ w_qkv.T).reshape(B, N, 3, H, D).transpose(2, 0, 3, 1, 4)
        q, k, v = (qkv[0], qkv[1], qkv[2])
        N_c = context.shape[1]
        kv = context.reshape(B, N_c, 2, H, D).transpose(2, 0, 3, 1, 4)
        extra_k, extra_v = (kv[0], kv[1])
        k = jnp.concatenate([extra_k, k], axis=2)
        v = jnp.concatenate([extra_v, v], axis=2)
        dtype = q.dtype
        attn = jnp.einsum('bhnd,bhmd->bhnm', q * scale, k).astype(jnp.float32)
        attn = jax.nn.softmax(attn, axis=-1).astype(dtype)
        out = jnp.einsum('bhnm,bhmd->bhnd', attn, v)
        out = out.transpose(0, 2, 1, 3).reshape(B, N, C)
        return out @ w_proj.T + b_proj

    def _L1_ffn_ref(x, in_proj_w, in_proj_b, out_w, out_b, ln1_g, ln1_b, router_w, router_b, w1, b1, w2, b2, ln2_g, ln2_b):
        import jax, jax.numpy as jnp
        import numpy as np
        H = 16
        E = 8
        EPS = 1e-05

        def _layernorm(x, g, b):
            mu = jnp.mean(x, axis=-1, keepdims=True)
            var = jnp.mean(jnp.square(x - mu), axis=-1, keepdims=True)
            return (x - mu) * jax.lax.rsqrt(var + EPS) * g + b
        T, B, C = x.shape
        D = C // H
        qkv = x @ in_proj_w.T + in_proj_b
        q, k, v = jnp.split(qkv, 3, axis=-1)
        q = q.reshape(T, B, H, D)
        k = k.reshape(T, B, H, D)
        v = v.reshape(T, B, H, D)
        scale = 1.0 / np.sqrt(D).astype(np.float32)
        scores = jnp.einsum('tbhd,sbhd->bhts', q, k) * scale
        attn = jax.nn.softmax(scores, axis=-1)
        ctx = jnp.einsum('bhts,sbhd->tbhd', attn, v).reshape(T, B, C)
        attn_out = ctx @ out_w.T + out_b
        h = _layernorm(x + attn_out, ln1_g, ln1_b)
        flat = h.reshape(-1, C)
        logits = flat @ router_w.T + router_b
        probs = jax.nn.softmax(logits, axis=-1)
        _, top_i = jax.lax.top_k(probs, 2)
        assign = jnp.max(top_i, axis=-1)
        out = jnp.zeros_like(flat)
        for e in range(E):
            he = jax.nn.gelu(flat @ w1[e].T + b1[e], approximate=False)
            oe = he @ w2[e].T + b2[e]
            out = jnp.where((assign == e)[:, None], oe, out)
        moe_out = out.reshape(T, B, C)
        return _layernorm(h + moe_out, ln2_g, ln2_b)

    def _L2_xattn_ref(memory, query, seq_mask, b):
        import jax, jax.numpy as jnp
        import numpy as np
        UNITS = 128
        NUM_HEADS = 8

        def _split_heads(x, n):
            B, S, D = x.shape
            return x.reshape(B, S, n, D // n).transpose(0, 2, 1, 3)
        H = NUM_HEADS
        depth = UNITS // H
        Q = _split_heads(query, H) * depth ** (-0.5)
        k_mem, v_mem = jnp.split(memory, 2, axis=2)
        K = _split_heads(k_mem, H)
        V = _split_heads(v_mem, H)
        logits = jnp.einsum('bhqd,bhkd->bhqk', Q, K) + b[0]
        mask = seq_mask.astype(jnp.float32)[:, None, None, :]
        logits = logits + -1e+30 * (1.0 - mask)
        weights = jax.nn.softmax(logits, axis=-1)
        out = jnp.einsum('bhqk,bhkd->bhqd', weights, V)
        B, _, S, _ = out.shape
        return out.transpose(0, 2, 1, 3).reshape(B, S, UNITS)

    def _L2_ffn_ref(x, w_router, w_gate, w_down):
        import math
        import jax, jax.numpy as jnp
        import numpy as np
        D_MODEL = 128
        D_HIDDEN = 256
        N_EXPERTS = 8
        TOP_K = 2
        CAPACITY_FACTOR = 1.25

        def _moe_forward(x, w_router, w_gate, w_down):
            B, T, D = x.shape
            N = B * T
            xf = x.reshape(N, D)
            logits = xf.astype(jnp.float32) @ w_router.T
            gates = jax.nn.softmax(logits, axis=-1)
            topk_gates, topk_idx = jax.lax.top_k(gates, TOP_K)
            expert_mask = jax.nn.one_hot(topk_idx, N_EXPERTS, dtype=jnp.int32).sum(axis=1)
            capacity = math.ceil(N / N_EXPERTS * CAPACITY_FACTOR)
            position_in_expert = jnp.cumsum(expert_mask, axis=0) - 1
            expert_mask = expert_mask * (position_in_expert < capacity)
            keep = jnp.take_along_axis(expert_mask, topk_idx, axis=1) > 0
            topk_gates = topk_gates * keep
            topk_gates = topk_gates / (topk_gates.sum(axis=-1, keepdims=True) + 1e-06)
            hidden = jax.nn.silu(xf @ w_gate.T)
            combine = (topk_gates[:, :, None] * jax.nn.one_hot(topk_idx, N_EXPERTS, dtype=topk_gates.dtype)).sum(axis=1)
            y = jnp.zeros((N, D), dtype=x.dtype)
            for e in range(N_EXPERTS):
                y = y + combine[:, e:e + 1] * (hidden @ w_down[e].T)
            return y.reshape(B, T, D)
        return _moe_forward(x, w_router, w_gate, w_down)

    def _L3_xattn_ref(x, context, Wq, Wkv, null_kv, Wout, ln_scale, ln_bias):
        import jax, jax.numpy as jnp
        import numpy as np
        B, N, DIM = (8, 512, 128)
        M, CTX = (32, 256)
        HEADS, DH = (16, 64)
        INNER = HEADS * DH
        EPS = 1e-06

        def _split_heads(t):
            b, n, _ = t.shape
            return t.reshape(b, n, HEADS, DH).transpose(0, 2, 1, 3)
        scale = DH ** (-0.5)
        b = x.shape[0]
        q = _split_heads(jnp.einsum('bnd,df->bnf', x, Wq))
        kv = jnp.einsum('bmc,cf->bmf', context, Wkv)
        k, v = jnp.split(kv, 2, axis=-1)
        k, v = (_split_heads(k), _split_heads(v))
        nk = jnp.broadcast_to(null_kv[0], (b, HEADS, 1, DH))
        nv = jnp.broadcast_to(null_kv[1], (b, HEADS, 1, DH))
        k = jnp.concatenate((nk, k), axis=-2)
        v = jnp.concatenate((nv, v), axis=-2)
        q = q * scale
        sim = jnp.einsum('bhid,bhjd->bhij', q, k)
        attn = jax.nn.softmax(sim, axis=-1)
        out = jnp.einsum('bhij,bhjd->bhid', attn, v)
        out = out.transpose(0, 2, 1, 3).reshape(b, -1, INNER)
        out = jnp.einsum('bnf,fd->bnd', out, Wout)
        mu = jnp.mean(out, axis=-1, keepdims=True)
        var = jnp.var(out, axis=-1, keepdims=True)
        out = (out - mu) * jax.lax.rsqrt(var + EPS) * ln_scale + ln_bias
        return out

    def _L3_ffn_ref(x, Wr, W1, W2):
        import math
        import jax, jax.numpy as jnp
        import numpy as np
        B, S, D, F, E = (8, 256, 128, 512, 8)
        CAPACITY_FACTOR = 1.0
        b, s, d = x.shape
        t = b * s
        cap = max(math.ceil(t * CAPACITY_FACTOR / E), 1)
        xf = x.reshape(t, d)
        probs = jax.nn.softmax(xf.astype(jnp.float32) @ Wr, axis=-1)
        eidx = jnp.argmax(probs, axis=-1)
        p_tok = jnp.take_along_axis(probs, eidx[:, None], axis=1)[:, 0]
        onehot = jax.nn.one_hot(eidx, E, dtype=jnp.int32)
        rank_all = jnp.cumsum(onehot, axis=0) - onehot
        rank = jnp.take_along_axis(rank_all, eidx[:, None], axis=1)[:, 0]
        keep = rank < cap
        slot = jnp.where(keep, rank, cap)
        dispatch = jnp.zeros((E, cap + 1), dtype=jnp.int32).at[eidx, slot].set(jnp.arange(t, dtype=jnp.int32))
        valid = jnp.zeros((E, cap + 1), dtype=bool).at[eidx, slot].set(keep)
        dispatch = dispatch[:, :cap]
        valid = valid[:, :cap]
        xe = xf[dispatch]
        h = jnp.maximum(jnp.einsum('ecd,edf->ecf', xe, W1), 0.0)
        ye = jnp.einsum('ecf,efd->ecd', h, W2)
        pe = p_tok[dispatch]
        ye = ye * (pe * valid.astype(ye.dtype))[:, :, None]
        y = jnp.zeros((t, d), dtype=x.dtype).at[dispatch.reshape(-1)].add(ye.reshape(E * cap, d).astype(x.dtype))
        return y.reshape(b, s, d)
    x = x + jnp.tanh(g_xattn[0]) * _L0_xattn_ref(_layernorm(x, axis=-1), ctx_2048, mask_BxS2_if0, L0_xattn_W_in, L0_xattn_b_in, L0_xattn_g_res, L0_xattn_g_init)
    x = x + jnp.tanh(g_ffn[0]) * _L0_ffn_ref(_layernorm(x, axis=-1), L0_ffn_gate_w, L0_ffn_gate_b, L0_ffn_w1, L0_ffn_b1, L0_ffn_w2, L0_ffn_b2, L0_ffn_wg, L0_ffn_bg, L0_ffn_w3, L0_ffn_b3)
    x = x + jnp.tanh(g_xattn[1]) * _L1_xattn_ref(_layernorm(x, axis=-1), ctx_2048, L1_xattn_w_qkv, L1_xattn_w_proj, L1_xattn_b_proj)
    x = x + jnp.tanh(g_ffn[1]) * _L1_ffn_ref(_layernorm(x, axis=-1), L1_ffn_in_proj_w, L1_ffn_in_proj_b, L1_ffn_out_w, L1_ffn_out_b, L1_ffn_ln1_g, L1_ffn_ln1_b, L1_ffn_router_w, L1_ffn_router_b, L1_ffn_w1, L1_ffn_b1, L1_ffn_w2, L1_ffn_b2, L1_ffn_ln2_g, L1_ffn_ln2_b)
    x = x + jnp.tanh(g_xattn[2]) * _L2_xattn_ref(ctx_2048, _layernorm(x, axis=-1), mask_BxS2_ik0, L2_xattn_b)
    x = x + jnp.tanh(g_ffn[2]) * _L2_ffn_ref(_layernorm(x, axis=-1), L2_ffn_w_router, L2_ffn_w_gate, L2_ffn_w_down)
    x = x + jnp.tanh(g_xattn[3]) * _L3_xattn_ref(_layernorm(x, axis=-1), ctx_2048, L3_xattn_Wq, L3_xattn_Wkv, L3_xattn_null_kv, L3_xattn_Wout, L3_xattn_ln_scale, L3_xattn_ln_bias)
    x = x + jnp.tanh(g_ffn[3]) * _L3_ffn_ref(_layernorm(x, axis=-1), L3_ffn_Wr, L3_ffn_W1, L3_ffn_W2)
    return x

_drawn_inputs = setup_inputs


def setup_inputs(seed=0):
    import zlib

    import numpy as np

    out = dict(_drawn_inputs(seed))
    spreads = {'L0_xattn_b_in': (0.0, 0.1),
     'L0_xattn_g_res': (1.0, 0.2),
     'L0_xattn_g_init': (1.0, 0.2),
     'L0_ffn_gate_b': (0.0, 0.1),
     'L0_ffn_b1': (0.0, 0.8),
     'L0_ffn_b2': (0.0, 0.8),
     'L0_ffn_bg': (0.0, 0.8),
     'L0_ffn_b3': (0.0, 0.471),
     'L1_ffn_in_proj_b': (0.0, 0.383),
     'L1_ffn_out_b': (0.0, 0.282),
     'L1_ffn_ln1_g': (1.0, 0.2),
     'L1_ffn_ln1_b': (0.0, 0.1),
     'L1_ffn_router_b': (0.0, 0.1),
     'L1_ffn_b1': (0.0, 0.8),
     'L1_ffn_b2': (0.0, 0.401),
     'L1_ffn_ln2_g': (1.0, 0.534),
     'L1_ffn_ln2_b': (0.0, 0.336),
     'L3_xattn_ln_scale': (1.0, 0.6),
     'L3_xattn_ln_bias': (0.0, 0.8)}
    factors = {'g_ffn': 25.856,
     'L0_ffn_w1': 8.0,
     'L0_ffn_w2': 8.0,
     'L0_ffn_wg': 8.0,
     'L0_ffn_w3': 5.81,
     'L1_xattn_w_qkv': 15.027,
     'L1_xattn_b_proj': 9.332,
     'L1_ffn_in_proj_w': 5.223,
     'L1_ffn_out_w': 3.07,
     'L1_ffn_w1': 4.298,
     'L1_ffn_w2': 3.869,
     'L2_ffn_w_router': 5.667,
     'L2_ffn_w_gate': 6.112,
     'L2_ffn_w_down': 6.234,
     'L3_xattn_null_kv': 4.6,
     'L1_xattn_w_proj': 3.378,
     'L3_ffn_W1': 2.757}
    for name, (base, spread) in spreads.items():
        noise = np.random.default_rng([zlib.crc32(name.encode()), seed]).standard_normal(out[name].shape)
        drawn = base * np.exp(spread * noise) if base else spread * noise
        out[name] = jnp.asarray(drawn.astype(out[name].dtype))
    for name, factor in factors.items():
        out[name] = (out[name] * factor).astype(out[name].dtype)
    return out
```

```python
import math
from contextlib import ExitStack

import concourse.bass as bass
from concourse import mybir

F32 = mybir.dt.float32
I32 = mybir.dt.int32
ALU = mybir.AluOpType
ACT = mybir.ActivationFunctionType
AX = mybir.AxisListType

P = 128
B, S, D = 8, 256, 128
NT = B * S // P
SC, DC = 64, 256
E = 8
GROUP = 4
NG = NT // GROUP
CHUNK = GROUP * P
EPS = 1e-5

SMALL_STEP = 0.001
DECAY = -math.expm1(-SMALL_STEP)
KEEP = math.exp(-SMALL_STEP)


def bc(ap, shape):
    return ap.to_broadcast(list(shape))


class Arena:

    def __init__(self, tensor, size):
        self.tensor, self.size, self.at = tensor, size, 0

    def take(self, n):
        a = self.at
        self.at += n
        assert self.at <= self.size, (self.at, self.size)
        return self.tensor[:, a:a + n]


class Core:

    def __init__(self, nc, ctx, d):
        self.nc, self.ctx, self.d = nc, ctx, d
        self.psum = ctx.enter_context(nc.psum_tensor("psum", [P, 8, 512], F32))
        self.bank = [self.psum[:, i, :] for i in range(8)]
        self.X = self.sb("X", [P, NT, D])
        self.XN = self.sb("XN", [P, NT, D])
        self.XT = self.sb("XT", [P, NT * P])
        self.stats = self.sb("stats", [P, NT, 6])
        self.moments = self.sb("moments", [P, NT, 2])
        self.veps = self.sb("veps", [P, NT])
        self.rstd = self.sb("rstd", [P, NT])
        self.gates = self.sb("gates", [P, 8])
        self.scratch_tensor = self.sb("scratch", [P, 12544])
        self.C = self.sb("C", [P, 4, DC])
        self.CT = self.sb("CT", [P, 2, B * SC])
        self.C2 = self.sb("C2", [P, B, DC])

        self.norms = self.turns = 0
        self.stats_done, self.moments_done = self.sem("stats_done"), self.sem("moments_done")
        self.veps_done, self.rstd_done = self.sem("veps_done"), self.sem("rstd_done")
        self.normed, self.transposed = self.sem("normed"), self.sem("transposed")
        self.turned_done = self.sem("turned_done")
        self.routers, self.spreads = 0, 0
        self.logits_done, self.shift_done = self.sem("logits_done"), self.sem("shift_done")
        self.exp_done = self.sem("exp_done")
        self.rows_turned, self.rows_copied = self.sem("rows_turned"), self.sem("rows_copied")
        self.bias_products = self.sem("bias_products")
        self.dve_chain, self.pool_chain = Chain(self, "dve_chain"), Chain(self, "pool_chain")

    def scratch(self):
        return Arena(self.scratch_tensor, 12544)

    def signals(self, prefix, names):
        return {n: self.sem(prefix + "_" + n) for n in names.split()}

    def sb(self, name, shape, dt=F32):
        return self.ctx.enter_context(self.nc.sbuf_tensor(name, shape, dt))

    def sem(self, name):
        return self.ctx.enter_context(self.nc.semaphore(name))


class Chain:

    def __init__(self, c, name):
        self.sem, self.n = c.sem(name), 0

    def link(self, eng, ins):
        self.n += 1
        ins.then_inc(self.sem, 1)
        eng.wait_ge(self.sem, self.n)


class Norm:

    def __init__(self, c, src, dst, mul=1.0, add=EPS, turned=None):
        self.c, self.src, self.dst, self.mul, self.add = c, src, dst, mul, add
        self.tiles_before, self.groups_before = NT * c.norms, NG * c.norms
        c.norms += 1
        self.turn = Turn(c, dst, turned, c.normed, GROUP, self.tiles_before) if turned is not None else None

    def dve(self, v, ready=None):
        c, before = self.c, self.tiles_before

        def normalize(g):
            v.wait_ge(c.rstd_done, self.groups_before + g + 1)
            for j in range(GROUP * g, GROUP * g + GROUP):
                v.tensor_scalar(self.dst[:, j, :], self.src[:, j, :], c.moments[:, j, 0:1],
                                c.rstd[:, j:j + 1], ALU.subtract, ALU.mult).then_inc(c.normed, 1)

        for g in range(NG):
            for j in range(GROUP * g, GROUP * g + GROUP):
                if ready is not None:
                    v.wait_ge(ready, j + 1)
                v.bn_stats(c.stats[:, j, :], self.src[:, j, :]).then_inc(c.stats_done, 1)
            for j in range(GROUP * g, GROUP * g + GROUP):
                v.wait_ge(c.stats_done, before + j + 1)
                v.bn_aggr(c.moments[:, j, :], c.stats[:, j, :]).then_inc(c.moments_done, 1)
            if g:
                normalize(g - 1)
        normalize(NG - 1)

    def wait_normed(self, eng, tiles):
        eng.wait_ge(self.c.normed, self.tiles_before + tiles)

    def pool(self, g_):
        c = self.c
        for g in range(NG):
            a, b = GROUP * g, GROUP * g + GROUP
            g_.wait_ge(c.moments_done, self.tiles_before + b)
            g_.tensor_scalar(c.veps[:, a:b], c.moments[:, a:b, 1], self.mul, self.add,
                             ALU.mult, ALU.add).then_inc(c.veps_done, 1)
            g_.wait_ge(c.veps_done, self.groups_before + g + 1)
            g_.tensor_tensor(c.rstd[:, a:b], c.veps[:, a:b], c.minus_half[:, a:b],
                             ALU.pow).then_inc(c.rstd_done, 1)

    def pe(self, t):
        self.turn.pe(t)

    def act(self, a):
        self.turn.act(a)


class Turn:

    def __init__(self, c, src, dst, ready, per_group, base=0, banks=(6, 7)):
        self.c, self.src, self.dst, self.ready, self.per_group = c, src, dst, ready, per_group
        self.base, self.banks, self.before = base, banks, NG * c.turns
        c.turns += 1

    def wait(self, eng, groups):
        eng.wait_ge(self.c.turned_done, self.before + groups)

    def pe(self, t):
        c = self.c
        for g in range(NG):
            t.wait_ge(self.ready, self.base + self.per_group * (g + 1))
            if g >= 2:
                self.wait(t, g - 1)
            for i in range(GROUP):
                last = t.transpose(c.bank[self.banks[g % 2]][:, i * P:(i + 1) * P],
                                   self.src[:, GROUP * g + i, :], c.ident[:])
            last.then_inc(c.transposed, 1)

    def act(self, a):
        c = self.c
        for g in range(NG):
            a.wait_ge(c.transposed, self.before + g + 1)
            a.activation(self.dst[:, g * CHUNK:(g + 1) * CHUNK], c.bank[self.banks[g % 2]][:, :],
                         ACT.Copy).then_inc(c.turned_done, 1)


class Load:

    def __init__(self, c, name):
        self.sem, self.parts = c.sem(name + "_loaded"), []

    def add(self, dst, src):
        self.parts.append((dst, src))
        return self

    def issue(self, eng):
        for dst, src in self.parts:
            eng.dma_start(dst, src).then_inc(self.sem, 16)

    def wait(self, eng):
        eng.wait_ge(self.sem, 16 * len(self.parts))


class Constants:

    def __init__(self, c):
        self.c = c
        c.ident = c.sb("ident", [P, P])
        c.ones = c.sb("ones", [P, P])
        c.half_ones = c.sb("half_ones", [P, P])
        c.half_upto = c.sb("half_upto", [P, P])
        c.before = c.sb("before", [P, P])
        c.minus_half = c.sb("minus_half", [P, NT])
        c.expert_m8 = c.sb("expert_m8", [P, E])
        c.column = c.sb("column", [P, S])
        c.row64 = c.sb("row64", [P, 1])
        c.head16 = c.sb("head16", [P, 8])
        c.parity = c.sb("parity", [P, 8])
        c.decay = c.sb("decay", [P, P])
        c.decayT = c.sb("decayT", [P, P])
        self.own = c.pool_chain
        c.constants_done = c.sem("constants_done")

    def pool(self, g):
        c, own = self.c, self.own

        def select(t, pattern, base, mult, op=ALU.is_ge, fill=0.0):
            own.link(g, g.affine_select(out=t, in_=t, compare_op=op, fill=fill, base=base,
                                        pattern=pattern, channel_multiplier=mult))

        own.link(g, g.memset(c.ident[:], 0.0))
        select(c.ident[:], [[-1, P]], 0, 1, ALU.not_equal, 1.0)
        g.memset(c.minus_half[:], -0.5)
        g.memset(c.decay[:], DECAY)
        own.link(g, g.memset(c.ones[:], 1.0))
        own.link(g, g.memset(c.before[:], 1.0))
        select(c.before[:], [[1, P]], -1, -1)
        own.link(g, g.memset(c.half_upto[:], 1.0))
        select(c.half_upto[:], [[1, P]], 0, -1)
        own.link(g, g.memset(c.half_upto[0:64, 64:128], 0.0))
        own.link(g, g.memset(c.half_ones[:], 1.0))
        own.link(g, g.memset(c.half_ones[0:64, 64:128], 0.0))
        own.link(g, g.memset(c.half_ones[64:128, 0:64], 0.0))
        own.link(g, g.memset(c.head16[:], 1.0))
        select(c.head16[:], [[-16, 8]], 0, 1)
        select(c.head16[:], [[16, 8]], 15, -1)
        par = c.parity[:, :].rearrange("p (k a) -> p k a", a=2)
        own.link(g, g.memset(c.parity[:], 0.0))
        g.memset(par[0:64, :, 0], 1.0)
        own.link(g, g.memset(par[64:128, :, 1], 1.0))
        own.link(g, g.iota(c.expert_m8[:], pattern=[[1, E]], base=-E, channel_multiplier=0,
               allow_small_or_imprecise_dtypes=True))
        own.link(g, g.iota(c.column[:], pattern=[[1, S]], base=0, channel_multiplier=0,
               allow_small_or_imprecise_dtypes=True))
        own.link(g, g.iota(c.row64[0:64, :], pattern=[[0, 1]], base=0, channel_multiplier=1,
               allow_small_or_imprecise_dtypes=True))
        g.iota(c.row64[64:128, :], pattern=[[0, 1]], base=0, channel_multiplier=1,
               allow_small_or_imprecise_dtypes=True).then_inc(c.constants_done, 1)


class DepoolStage:

    def __init__(self, c, after):
        self.c, self.after = c, after
        sc, d = c.scratch(), c.d
        self.norm = Norm(c, c.X, c.XN, 1.0 + EPS, EPS * EPS, c.XT)
        self.WinT = c.sb("WinT", [P, D])
        self.Wg = c.sb("Wg", [P, D])
        self.g_res = c.sb("g_res", [P, 1])
        self.b_in = c.sb("b_in", [1, D])
        self.lens = c.sb("lens", [P, 4], I32)
        self.small = c.sb("a_small", [P, 7, 4])
        self.g_init = sc.take(D)
        self.square = sc.take(DC)
        self.hp = sc.take(4 * D).rearrange("p (a d) -> p a d", a=4)
        self.states = sc.take(4 * D).rearrange("p (a d) -> p a d", a=4)
        self.hit = sc.take(4 * S).rearrange("p (a t) -> p a t", a=4)
        self.count = sc.take(4 * S).rearrange("p (a t) -> p a t", a=4)
        self.zeros = sc.take(S)
        self.pick = sc.take(4 * S).rearrange("p (a t) -> p a t", a=4)
        self.all_added = NT
        self.load = (Load(c, "a").add(c.C[:], d["ctx_pairs"])
                     .add(self.lens[:], d["patch_lens"])
                     .add(self.g_init, d["L0_xattn_g_init"][0:D].partition_broadcast(P))
                     .add(self.g_res[:], d["L0_xattn_g_res"])
                     .add(self.WinT[:], d["L0_xattn_W_in"])
                     .add(self.b_in[:], d["L0_xattn_b_in"][None, :]))
        self.own = c.dve_chain
        self.s = c.signals("a", "mean_square patch_eps patch_rstd patches scanned states lengths ends "
                                "hits counted picks product added")

    def dve(self, v):
        c, s, own, sm = self.c, self.s, self.own, self.small
        v.wait_ge(c.constants_done, 1)
        own.link(v, v.tensor_scalar(c.decayT[:], c.ident[:], KEEP, None, ALU.mult))
        own.link(v, v.tensor_tensor_scan(c.decayT[:], c.decay[:], c.decayT[:], 0.0, ALU.mult, ALU.add))
        own.link(v, v.memset(c.decayT[0:64, 64:128], 0.0))
        self.load.wait(v)
        own.link(v, v.tensor_copy(sm[:, 0, :], self.lens[:]))
        v.tensor_scalar(self.Wg[:], self.WinT[:], self.g_res[:, 0:1], None, ALU.mult) \
            .then_inc(s["lengths"], 1)
        v.wait_ge(s["patch_rstd"], 1)
        for a in range(4):
            v.scalar_tensor_tensor(self.hp[:, a, :], c.C[:, a, 0:D], sm[:, 6, a:a + 1], self.g_init,
                                   ALU.mult, ALU.mult).then_inc(s["patches"], 1)
        v.wait_ge(s["ends"], 1)
        own.link(v, v.tensor_scalar(sm[:, 1, :], c.bank[4][:, 0:4], -1.0, None, ALU.add))
        own.link(v, v.tensor_scalar(sm[:, 2, :], sm[:, 1, :], 0.0, float(S), ALU.is_lt, ALU.mult))
        own.link(v, v.tensor_tensor(sm[:, 3, :], sm[:, 1, :], sm[:, 2, :], ALU.add))
        for a in range(4):
            v.tensor_scalar(self.hit[:, a, :], c.column[:], sm[:, 3, a:a + 1], None, ALU.is_equal) \
                .then_inc(s["hits"], 1)
        own.link(v, v.memset(self.zeros, 0.0))
        v.wait_ge(s["counted"], 1)
        for k in range(2):
            own.link(v, v.tensor_scalar(self.count[:, 2 * k:2 * k + 2, :].rearrange("p a t -> p (a t)"),
                                        c.bank[4 + k][:, :], 1.0, None, ALU.min))
        for a in range(4):
            own.link(v, v.tensor_tensor_scan(self.count[:, a, :], self.count[:, a, :], self.zeros, 0.0,
                                             ALU.add, ALU.add))
        own.link(v, v.tensor_scalar(self.count[:, :, :], self.count[:, :, :], -1.0, 0.0, ALU.add, ALU.max))
        v.tensor_scalar(self.pick[:, :, :], self.count[:, :, :], float(SC - 1), c.row64[:, 0:1],
                        ALU.min, ALU.is_equal).then_inc(s["picks"], 1)
        self.norm.dve(v, self.after)
        for j in range(NT):
            v.wait_ge(s["product"], j // 2 + 1)
            v.scalar_tensor_tensor(c.X[:, j, :], c.bank[j // 2 % 4][:, (j % 2) * D:(j % 2 + 1) * D],
                                   c.gates[:, 0:1], c.X[:, j, :], ALU.mult, ALU.add) \
                .then_inc(s["added"], 1)

    def pool(self, g):
        c, s, sm = self.c, self.s, self.small
        g.wait_ge(s["mean_square"], 4)
        g.tensor_scalar(sm[:, 5, :], sm[:, 4, :], 1.0 / DC, EPS, ALU.mult, ALU.add) \
            .then_inc(s["patch_eps"], 1)
        g.wait_ge(s["patch_eps"], 1)
        g.tensor_tensor(sm[:, 6, :], sm[:, 5, :], c.minus_half[:, 0:4], ALU.pow) \
            .then_inc(s["patch_rstd"], 1)
        self.norm.pool(g)

    def act(self, a):
        c, s, sm = self.c, self.s, self.small
        c.gate_load.wait(a)
        a.activation(c.gates[:], c.gates_in[:], ACT.Tanh).then_inc(c.gates_done, 1)
        self.load.wait(a)
        for k in range(4):
            if k:
                a.wait_ge(s["mean_square"], k)
            a.activation(self.square, c.C[:, k, :], ACT.Square, accum_out=sm[:, 4, k:k + 1]) \
                .then_inc(s["mean_square"], 1)
        a.wait_ge(s["scanned"], 1)
        a.activation(self.states[:, :, :].rearrange("p a d -> p (a d)"), c.bank[5][:, :], ACT.Copy) \
            .then_inc(s["states"], 1)
        self.norm.act(a)

    def pe(self, t):
        c, s = self.c, self.s
        t.wait_ge(c.constants_done, 1)
        t.wait_ge(s["lengths"], 1)
        t.matmul(c.bank[4][:, 0:4], c.half_upto[:], self.small[:, 0, :], start=True, stop=True) \
            .then_inc(s["ends"], 1)
        t.wait_ge(s["patches"], 4)
        t.matmul(c.bank[5][:, :], c.decayT[:], self.hp[:, :, :].rearrange("p a d -> p (a d)"),
                 start=True, stop=True).then_inc(s["scanned"], 1)
        t.wait_ge(s["states"], 1)
        t.wait_ge(s["hits"], 4)
        for k in range(2):
            last = t.matmul(c.bank[4 + k][:, :], c.half_ones[:],
                            self.hit[:, 2 * k:2 * k + 2, :].rearrange("p a t -> p (a t)"),
                            start=True, stop=True)
        last.then_inc(s["counted"], 1)
        self.norm.pe(t)
        t.wait_ge(s["picks"], 1)
        for b in range(B):
            h = slice(64 * (b % 2), 64 * (b % 2) + 64)
            self.norm.turn.wait(t, b // 2 + 1)
            if b >= 4:
                t.wait_ge(s["added"], 2 * (b - 4) + 2)
            for i in range(2):
                j = 2 * b + i
                out = c.bank[b % 4][:, i * D:(i + 1) * D]
                t.matmul(out, c.XT[:, j * P:(j + 1) * P], self.Wg[:], start=True, stop=False)
                t.matmul(out, c.ones[0:1, :], self.b_in[0:1, :], start=False, stop=False)
                last = t.matmul(out, self.pick[h, b // 2, i * P:(i + 1) * P], self.states[h, b // 2, :],
                                start=False, stop=True)
            last.then_inc(s["product"], 1)


class Routing:

    def __init__(self, c):
        self.c = c
        self.small = c.sb("routing_small", [P, 16, NT])
        self.wide = c.sb("routing_wide", [P, 8, NT, E])

    def rows(self, k):
        return self.small[:, k, :]

    def table(self, k):
        return self.wide[:, k, :, :]

    def first(self, v, own, values, biggest, onehot, index):
        c, shape, tmp = self.c, (P, NT, E), self.table(7)
        place = bc(c.expert_m8[:, None, :], shape)
        own.link(v, v.tensor_reduce(biggest, values, AX.X, ALU.max))
        own.link(v, v.tensor_tensor(tmp, values, bc(biggest[:, :, None], shape), ALU.is_ge))
        own.link(v, v.tensor_tensor(tmp, tmp, place, ALU.mult))
        own.link(v, v.tensor_reduce(index, tmp, AX.X, ALU.min))
        own.link(v, v.tensor_tensor(onehot, place, bc(index[:, :, None], shape), ALU.is_equal))

    def hide(self, v, own, values, onehot, left):
        own.link(v, v.scalar_tensor_tensor(left, onehot, -3.0e38, values, ALU.mult, ALU.add))


class Router:

    def __init__(self, c):
        c.routers += 1
        self.c, self.n = c, c.routers

    def pe(self, t, weights):
        c = self.c
        for j in range(NT):
            last = t.matmul(c.bank[0][:, j * E:(j + 1) * E], c.XT[:, j * P:(j + 1) * P], weights,
                            start=True, stop=True)
        last.then_inc(c.logits_done, 1)

    def logits(self, v):
        v.wait_ge(self.c.logits_done, self.n)
        return self.c.bank[0][:, 0:NT * E].rearrange("p (j e) -> p j e", e=E)

    def softmax(self, v, logits, prob, top):
        c, own, shape = self.c, self.c.dve_chain, (P, NT, E)
        own.link(v, v.tensor_reduce(top, logits, AX.X, ALU.max))
        v.tensor_tensor(prob, logits, bc(top[:, :, None], shape), ALU.subtract).then_inc(c.shift_done, 1)
        v.wait_ge(c.exp_done, self.n)
        own.link(v, v.tensor_reduce(top, prob, AX.X, ALU.add))
        own.link(v, v.reciprocal(top, top))
        own.link(v, v.tensor_tensor(prob, prob, bc(top[:, :, None], shape), ALU.mult))

    def act(self, a, values):
        a.wait_ge(self.c.shift_done, self.n)
        a.activation(values, values, ACT.Exp).then_inc(self.c.exp_done, 1)


class ExpertBias:

    def __init__(self, c, table, turned, bias):
        self.c, self.table, self.turned, self.bias = c, table, turned, bias
        self.before = NG * c.spreads
        c.spreads += 1

    def pe(self, t):
        c = self.c
        for q in range(NG):
            if q >= 2:
                t.wait_ge(c.rows_copied, self.before + q - 1)
            for i in range(GROUP):
                last = t.transpose(c.bank[4 + q % 2][0:E, i * P:(i + 1) * P], self.table[:, GROUP * q + i, :],
                                   c.ident[:])
            last.then_inc(c.rows_turned, 1)
        for q in range(NG):
            t.wait_ge(c.rows_copied, self.before + q + 1)
            for i in range(GROUP):
                j = GROUP * q + i
                last = t.matmul(c.bank[q][:, i * D:(i + 1) * D], self.turned[:, j * P:(j + 1) * P],
                                self.bias, start=True, stop=True)
            last.then_inc(c.bias_products, 1)

    def act(self, a):
        c = self.c
        for q in range(NG):
            a.wait_ge(c.rows_turned, self.before + q + 1)
            a.activation(self.turned[:, q * CHUNK:(q + 1) * CHUNK], c.bank[4 + q % 2][0:E, :], ACT.Copy) \
                .then_inc(c.rows_copied, 1)

    def dve(self, v, rows, done):
        c = self.c
        for q in range(NG):
            v.wait_ge(c.bias_products, self.before + q + 1)
            j = GROUP * q
            v.tensor_tensor(rows[:, j:j + GROUP, :], rows[:, j:j + GROUP, :],
                            c.bank[q][:, :].rearrange("p (j d) -> p j d", d=D), ALU.add).then_inc(done, 1)


class ExpertPairStage:

    def __init__(self, c, after):
        self.c, self.after = c, after
        sc, d = c.scratch(), c.d
        self.norm = Norm(c, c.X, c.XN, 1.0, EPS, c.XT)
        ar = Arena(c.arena_tensor, 10240)
        self.w1 = ar.take(E * 256).rearrange("p (e f) -> p e f", e=E)
        self.w2 = ar.take(E * 256).rearrange("p (e f) -> p e f", e=E)
        self.wg = ar.take(E * 512).rearrange("p (e k f) -> p e k f", e=E, k=2)
        self.w3 = ar.take(E * 256).rearrange("p (e k f) -> p e k f", e=E, k=2)
        self.gate_w = c.sb("b_gate_w", [P, E])
        self.gate_b = c.sb("b_gate_b", [P, E])
        self.bias = c.sb("b_bias", [P, 3, 2 * E])
        self.b3 = c.sb("b_b3", [E, D])
        self.all_added = NG + E * NT
        self.load = (Load(c, "b").add(self.gate_w[:], d["L0_ffn_gate_w"])
                     .add(self.gate_b[:], d["L0_ffn_gate_b"].partition_broadcast(P))
                     .add(self.bias[:, 0, :], d["L0_ffn_b1"]).add(self.bias[:, 1, :], d["L0_ffn_b2"])
                     .add(self.bias[:, 2, :], d["L0_ffn_bg"]).add(self.b3[:], d["L0_ffn_b3"]))
        self.expert_load = [Load(c, f"b_experts{q}")
                            .add(self.w1[:, 2 * q:2 * q + 2], d["L0_ffn_w1"][2 * q:2 * q + 2].rearrange("e h f -> h e f"))
                            .add(self.w2[:, 2 * q:2 * q + 2], d["L0_ffn_w2"][2 * q:2 * q + 2].rearrange("e h f -> h e f"))
                            .add(self.wg[:, 2 * q], d["L0_ffn_wg"][2 * q].rearrange("(k h) f -> h k f", k=2))
                            .add(self.wg[:, 2 * q + 1], d["L0_ffn_wg"][2 * q + 1].rearrange("(k h) f -> h k f", k=2))
                            .add(self.w3[:, 2 * q], d["L0_ffn_w3"][2 * q].rearrange("(k h) f -> h k f", k=2))
                            .add(self.w3[:, 2 * q + 1], d["L0_ffn_w3"][2 * q + 1].rearrange("(k h) f -> h k f", k=2))
                            for q in range(4)]
        self.x2 = sc.take(2 * 1024).rearrange("p (u k n) -> p u k n", u=2, k=2)
        self.z = sc.take(2 * 1024).rearrange("p (u k n) -> p u k n", u=2, k=2)
        self.act_out = sc.take(2 * 1024).rearrange("p (u k n) -> p u k n", u=2, k=2)
        self.weightT = sc.take(NT * P)[0:E, :]
        self.own = c.dve_chain
        self.s = c.signals("b", "weights added second second_copied z third silu result")
        self.router = Router(c)
        self.bias_sum = ExpertBias(c, c.routing.table(2), self.weightT, self.b3[:])

    def dve(self, v):
        c, s, own, r = self.c, self.s, self.own, self.c.routing
        self.norm.dve(v, self.after)
        products = self.router.logits(v)
        self.load.wait(v)
        logits, left, one, two = r.table(0), r.table(1), r.table(2), r.table(3)
        m1, m2, idx, gap, w1, w2 = (r.rows(k) for k in range(6))
        own.link(v, v.tensor_tensor(logits, products, bc(self.gate_b[:, None, :], (P, NT, E)), ALU.add))
        r.first(v, own, logits, m1, one, idx)
        r.hide(v, own, logits, one, left)
        r.first(v, own, left, m2, two, idx)
        v.tensor_tensor(gap, m2, m1, ALU.subtract).then_inc(c.shift_done, 1)
        v.wait_ge(c.exp_done, self.router.n)
        own.link(v, v.tensor_scalar(w1, gap, 1.0, None, ALU.add))
        own.link(v, v.reciprocal(w1, w1))
        own.link(v, v.tensor_tensor(w2, gap, w1, ALU.mult))
        own.link(v, v.tensor_tensor(one, one, bc(w1[:, :, None], (P, NT, E)), ALU.mult))
        own.link(v, v.tensor_tensor(two, two, bc(w2[:, :, None], (P, NT, E)), ALU.mult))
        own.link(v, v.tensor_tensor(one, one, two, ALU.add))
        v.tensor_scalar(one, one, c.gates[:, 4:5], None, ALU.mult).then_inc(s["weights"], 1)
        v.wait_ge(s["weights"], 1)
        self.bias_sum.dve(v, c.X, s["added"])

        def multiply(n):
            e = n // NG
            for k in range(2):
                v.wait_ge(s["second_copied"], 2 * n + k + 1)
                if n >= 2:
                    v.wait_ge(s["third"], n - 1)
                v.scalar_tensor_tensor(self.z[:, n % 2, k, :], c.bank[k][:, :],
                                       self.bias[:, 0, 2 * e + k:2 * e + k + 1], self.x2[:, n % 2, k, :],
                                       ALU.add, ALU.mult).then_inc(s["z"], 1)

        def add(n):
            e, q = n // NG, n % NG
            v.wait_ge(s["result"], n + 1)
            v.wait_ge(s["added"], NG + max(GROUP * (n - NG + 1), 0))
            for i in range(GROUP):
                j = GROUP * q + i
                v.scalar_tensor_tensor(c.X[:, j, :], c.bank[6 + n % 2][:, i * D:(i + 1) * D],
                                       one[:, j, e:e + 1], c.X[:, j, :], ALU.mult, ALU.add) \
                    .then_inc(s["added"], 1)

        for n in range(E * NG):
            multiply(n)
            if n:
                add(n - 1)
        add(E * NG - 1)

    def pool(self, g):
        self.norm.pool(g)

    def act(self, a):
        c, s = self.c, self.s
        self.norm.act(a)
        self.router.act(a, c.routing.rows(3))
        self.bias_sum.act(a)
        self.load.wait(a)

        def copy_second(n):
            e = n // NG
            if n >= 2:
                a.wait_ge(s["z"], 2 * (n - 1))
            for k in range(2):
                a.wait_ge(s["second"], 2 * n + k + 1)
                a.activation(self.x2[:, n % 2, k, :], c.bank[2 + k][:, :], ACT.Identity,
                             bias=self.bias[:, 1, 2 * e + k:2 * e + k + 1]).then_inc(s["second_copied"], 1)

        def silu(n):
            e = n // NG
            if n >= 2:
                a.wait_ge(s["result"], n - 1)
            a.wait_ge(s["third"], n + 1)
            for k in range(2):
                a.activation(self.act_out[:, n % 2, k, :], c.bank[4 + k][:, :], ACT.Silu,
                             bias=self.bias[:, 2, 2 * e + k:2 * e + k + 1]).then_inc(s["silu"], 1)

        for n in range(E * NG):
            copy_second(n)
            silu(n)

    def pe(self, t):
        c, s = self.c, self.s
        self.norm.pe(t)
        self.load.wait(t)
        self.norm.turn.wait(t, NG)
        self.router.pe(t, self.gate_w[:])
        t.wait_ge(s["weights"], 1)
        self.bias_sum.pe(t)

        def project(n):
            e, x = n // NG, c.XT[:, (n % NG) * CHUNK:(n % NG + 1) * CHUNK]
            if n % (2 * NG) == 0:
                self.expert_load[e // 2].wait(t)
            if n == 0:
                t.wait_ge(s["added"], NG)
            else:
                t.wait_ge(s["z"], 2 * n)
            for k in range(2):
                t.matmul(c.bank[k][:, :], self.w1[:, e, k * P:(k + 1) * P], x, start=True, stop=True)
                t.matmul(c.bank[2 + k][:, :], self.w2[:, e, k * P:(k + 1) * P], x, start=True, stop=True) \
                    .then_inc(s["second"], 1)

        def third(n):
            e = n // NG
            t.wait_ge(s["z"], 2 * n + 2)
            if n:
                t.wait_ge(s["silu"], 2 * n)
            for k in range(2):
                for q in range(2):
                    last = t.matmul(c.bank[4 + k][:, :], self.wg[:, e, q, k * P:(k + 1) * P],
                                    self.z[:, n % 2, q, :], start=(q == 0), stop=(q == 1))
            last.then_inc(s["third"], 1)

        def last_product(n):
            e = n // NG
            t.wait_ge(s["silu"], 2 * n + 2)
            if n >= 2:
                t.wait_ge(s["added"], NG + GROUP * (n - 1))
            for i in range(GROUP):
                for k in range(2):
                    last = t.matmul(c.bank[6 + n % 2][:, i * D:(i + 1) * D],
                                    self.act_out[:, n % 2, k, i * P:(i + 1) * P], self.w3[:, e, k, :],
                                    start=(k == 0), stop=(k == 1))
            last.then_inc(s["result"], 1)

        project(0)
        for n in range(E * NG):
            third(n)
            if n + 1 < E * NG:
                project(n + 1)
            last_product(n)


class HeadsStage:

    H, DH = 16, 8
    SCALE = 8 ** -0.5

    def __init__(self, c, after):
        self.c, self.after, self.all_added = c, after, NT
        sc, d = c.scratch(), c.d
        self.norm = Norm(c, c.X, c.XN, 1.0, EPS, c.XT)
        self.Wqkv = c.sb("c_Wqkv", [P, 3 * D])
        self.Wproj = c.sb("c_Wproj", [P, D])
        self.b_proj = c.sb("c_b_proj", [1, D])
        self.load = (Load(c, "c").add(self.Wqkv[:], d["L1_xattn_w_qkv"]).add(self.Wproj[:], d["L1_xattn_w_proj"])
                     .add(self.b_proj[:], d["L1_xattn_b_proj"][None, :]))
        self.Q = sc.take(1024).rearrange("p (i h c) -> p i h c", i=2, h=16)
        self.K = sc.take(1024).rearrange("p (i h c) -> p i h c", i=2, h=16)
        self.KC = sc.take(2 * 512)[0:64, :].rearrange("p (u h c) -> p u h c", u=2, h=16)
        self.V = sc.take(2 * 288).rearrange("p (u i h c) -> p u i h c", u=2, i=2, h=16)
        self.VC = sc.take(B * 144).rearrange("p (b h c) -> p b h c", b=B, h=16)
        self.QT = sc.take(1024).rearrange("p (g t) -> p g t", g=4)
        self.KT = sc.take(1280).rearrange("p (g t) -> p g t", g=4)
        self.prob = sc.take(4 * 512).rearrange("p (u k t) -> p u k t", u=4, k=2)
        self.prob_c = sc.take(2 * 512).rearrange("p (u k t) -> p u k t", u=2, k=2)
        self.rz = sc.take(32).rearrange("p (i h) -> p i h", i=2)
        self.O = sc.take(256).rearrange("p (i n) -> p i n", i=2)
        self.OT = sc.take(256)
        self.s = c.signals("c", "clear ones_set values keys_c qkv split q_t k_t q_turned k_turned scores maxed "
                                "st exp st_c exp_c av rz heads o_t o_turned product added")

    def pool(self, g):
        c, s = self.c, self.s
        self.norm.pool(g)
        c.c2_load.wait(g)
        for n, t in enumerate((self.Q, self.K, self.KC)):
            g.memset(t, 0.0).then_inc(s["clear"], 1)
        g.wait_ge(s["clear"], 3)
        g.memset(self.K[:, :, :, 8], 1.0).then_inc(s["ones_set"], 1)
        g.memset(self.KC[:, :, :, 8], 1.0).then_inc(s["ones_set"], 1)
        g.memset(self.V[:, :, :, :, 8], 1.0).then_inc(s["ones_set"], 1)
        g.memset(self.VC[:, :, :, 8], 1.0).then_inc(s["ones_set"], 1)
        g.wait_ge(s["ones_set"], 4)
        for b in range(B):
            g.tensor_copy(self.VC[:, b, :, 0:8], c.C2[:, b, D:2 * D].rearrange("p (h c) -> p h c", c=8)) \
                .then_inc(s["values"], 1)
        for b in range(B):
            if b >= 2:
                g.wait_ge(s["k_t"], 3 * (b - 1))
            g.tensor_copy(self.KC[:, b % 2, :, 0:8],
                          c.C2[0:64, b, 0:D].rearrange("p (h c) -> p h c", c=8)).then_inc(s["keys_c"], 1)

    def pe(self, t):
        c, s = self.c, self.s
        self.norm.pe(t)
        self.load.wait(t)
        bank = c.bank

        def project(b):
            self.norm.turn.wait(t, b // 2 + 1)
            if b:
                t.wait_ge(s["exp_c"], 4 * b)
            for i in range(2):
                j = 2 * b + i
                t.matmul(bank[i][:, 0:3 * D], c.XT[:, j * P:(j + 1) * P], self.Wqkv[:], start=True,
                         stop=True).then_inc(s["qkv"], 1)

        def turn_rows(b):
            t.wait_ge(s["split"], 6 * b + 6)
            t.wait_ge(s["keys_c"], b + 1)
            if b:
                t.wait_ge(s["exp"], 16 * b)
            for i in range(2):
                for g in range(4):
                    last = t.transpose(bank[2 + i][:, g * P:(g + 1) * P],
                                       self.Q[:, i, 4 * g:4 * g + 4, :].rearrange("p h c -> p (h c)"), c.ident[:])
                last.then_inc(s["q_t"], 1)
            for i in range(2):
                for g in range(4):
                    last = t.transpose(bank[i][:, g * P:(g + 1) * P],
                                       self.K[:, i, 4 * g:4 * g + 4, :].rearrange("p h c -> p (h c)"), c.ident[:])
                last.then_inc(s["k_t"], 1)
            for g in range(4):
                last = t.transpose(bank[4][:, g * 64:(g + 1) * 64],
                                   self.KC[:, b % 2, 4 * g:4 * g + 4, :].rearrange("p h c -> p (h c)"),
                                   c.ident[0:64, 0:64])
            last.then_inc(s["k_t"], 1)

        def scores(b):
            t.wait_ge(s["q_turned"], 4 * b + 2)
            t.wait_ge(s["k_turned"], 3 * b + 3)
            for n in range(16):
                i = n // 8
                if n >= 2:
                    t.wait_ge(s["maxed"], 16 * b + n - 1)
                for q in range(2):
                    h = 2 * (n % 8) + q
                    g, r = h // 4, 32 * (h % 4)
                    last = t.matmul(bank[2 * (n % 2) + q][:, 0:320], self.QT[r:r + 8, g, i * P:(i + 1) * P],
                                    self.KT[r:r + 8, g, :], start=True, stop=True)
                last.then_inc(s["scores"], 1)

        def turn_again(b):
            t.wait_ge(s["maxed"], 16 * b + 16)
            for i in range(2):
                for g in range(4):
                    last = t.transpose(bank[i][:, g * P:(g + 1) * P],
                                       self.Q[:, i, 4 * g:4 * g + 4, :].rearrange("p h c -> p (h c)"), c.ident[:])
                last.then_inc(s["q_t"], 1)

        def keys_major(b, g):
            n = 4 * b + g
            if n:
                t.wait_ge(s["exp_c"], n)
            for r in range(4):
                last = t.matmul(bank[r // 2][64 * (r % 2):64 * (r % 2) + 64, 0:S],
                                self.KT[32 * r:32 * r + 9, g, S:S + 64], self.QT[32 * r:32 * r + 9, g, :],
                                start=True, stop=True)
            last.then_inc(s["st_c"], 1)

        def keys_major_own(b, h):
            n, g, r = 16 * b + h, h // 4, 32 * (h % 4)
            if n >= 4:
                t.wait_ge(s["exp"], n - 3)
            for k in range(2):
                last = t.matmul(bank[2 + n % 4][:, k * S:(k + 1) * S], self.KT[r:r + 9, g, k * P:(k + 1) * P],
                                self.QT[r:r + 9, g, :], start=True, stop=True)
            last.then_inc(s["st"], 1)

        def values(b, h):
            n, g, r = 16 * b + h, h // 4, h % 4
            t.wait_ge(s["exp_c"], 4 * b + g + 1)
            t.wait_ge(s["exp"], n + 1)
            half = slice(64 * (r % 2), 64 * (r % 2) + 64)
            for i in range(2):
                at = i * 72 + 9 * (h // 2)
                out = bank[7 - h % 2][:, at:at + 9]
                for k in range(2):
                    t.matmul(out, self.prob[:, n % 4, k, i * P:(i + 1) * P], self.V[:, b % 2, k, h, :],
                             start=(k == 0), stop=False)
                last = t.matmul(out, self.prob_c[half, (4 * b + g) % 2, r // 2, i * P:(i + 1) * P],
                                self.VC[half, b, h, :], start=False, stop=True)
            last.then_inc(s["av"], 1)

        def turn_out(b):
            t.wait_ge(s["heads"], 2 * b + 2)
            for i in range(2):
                last = t.transpose(bank[6][:, i * P:(i + 1) * P], self.O[:, i, :], c.ident[:])
            last.then_inc(s["o_t"], 1)

        def project_out(b):
            t.wait_ge(s["o_turned"], b + 1)
            for i in range(2):
                out = bank[6][:, 256 + i * P:256 + (i + 1) * P]
                t.matmul(out, self.OT[:, i * P:(i + 1) * P], self.Wproj[:], start=True, stop=False)
                last = t.matmul(out, c.ones[0:1, :], self.b_proj[0:1, :], start=False, stop=True)
            last.then_inc(s["product"], 1)

        t.wait_ge(s["ones_set"], 4)
        for b in range(B):
            project(b)
            if b:
                turn_out(b - 1)
            turn_rows(b)
            if b:
                project_out(b - 1)
            scores(b)
            turn_again(b)
            t.wait_ge(s["q_turned"], 4 * b + 4)
            if b:
                t.wait_ge(s["added"], 2 * b)
                t.wait_ge(s["heads"], 2 * b)
            else:
                t.wait_ge(s["values"], B)
            keys_major(b, 0)
            keys_major_own(b, 0)
            for h in range(16):
                if h + 1 < 16:
                    if (h + 1) % 4 == 0:
                        keys_major(b, (h + 1) // 4)
                    keys_major_own(b, h + 1)
                values(b, h)
        turn_out(B - 1)
        project_out(B - 1)

    def act(self, a):
        c, s = self.c, self.s
        self.norm.act(a)
        bank = c.bank
        a.wait_ge(s["ones_set"], 4)

        def split(b):
            for i in range(2):
                a.wait_ge(s["qkv"], 2 * b + i + 1)
                if b:
                    a.wait_ge(s["q_t"], 4 * b)
                    a.wait_ge(s["k_t"], 3 * b)
                if b >= 2:
                    a.wait_ge(s["av"], 16 * (b - 1))
                rows = [bank[i][:, k * D:(k + 1) * D].rearrange("p (h c) -> p h c", c=8) for k in range(3)]
                a.activation(self.Q[:, i, :, 0:8], rows[0], ACT.Copy, scale=self.SCALE).then_inc(s["split"], 1)
                a.activation(self.K[:, i, :, 0:8], rows[1], ACT.Copy).then_inc(s["split"], 1)
                a.activation(self.V[:, b % 2, i, :, 0:8], rows[2], ACT.Copy).then_inc(s["split"], 1)

        def copy_keys(b):
            if b:
                a.wait_ge(s["av"], 16 * b)
            for i in range(2):
                a.wait_ge(s["k_t"], 3 * b + i + 1)
                a.activation(self.KT[:, :, i * P:(i + 1) * P],
                             bank[i][:, :].rearrange("p (g t) -> p g t", g=4), ACT.Copy).then_inc(s["k_turned"], 1)
            a.wait_ge(s["k_t"], 3 * b + 3)
            a.activation(self.KT[:, :, S:S + 64], bank[4][:, 0:256].rearrange("p (g t) -> p g t", g=4),
                         ACT.Copy).then_inc(s["k_turned"], 1)

        def copy_out(b):
            a.wait_ge(s["o_t"], b + 1)
            a.activation(self.OT, bank[6][:, 0:256], ACT.Copy).then_inc(s["o_turned"], 1)

        def exp_context(b, g):
            n = 4 * b + g
            a.wait_ge(s["st_c"], n + 1)
            if n >= 2:
                a.wait_ge(s["av"], 4 * (n - 1))
            a.activation(self.prob_c[:, n % 2, :, :], c.psum[:, 0:2, 0:S], ACT.Exp) \
                .then_inc(s["exp_c"], 1)

        def exp_own(b, h):
            n = 16 * b + h
            a.wait_ge(s["st"], n + 1)
            if n >= 4:
                a.wait_ge(s["av"], n - 3)
            a.activation(self.prob[:, n % 4, :, :].rearrange("p k t -> p (k t)"), bank[2 + n % 4][:, :],
                         ACT.Exp).then_inc(s["exp"], 1)

        for b in range(B):
            split(b)
            if b:
                copy_out(b - 1)
            copy_keys(b)
            for h in range(16):
                if h % 4 == 0:
                    exp_context(b, h // 4)
                exp_own(b, h)
        copy_out(B - 1)

    def dve(self, v):
        c, s = self.c, self.s
        self.norm.dve(v, self.after)
        bank = c.bank

        def copy_queries(b, again):
            for i in range(2):
                v.wait_ge(s["q_t"], 4 * b + 2 * again + i + 1)
                v.tensor_copy(self.QT[:, :, i * P:(i + 1) * P],
                              bank[i if again else 2 + i][:, :].rearrange("p (g t) -> p g t", g=4)) \
                    .then_inc(s["q_turned"], 1)

        def maxima(b):
            for n in range(16):
                v.wait_ge(s["scores"], 16 * b + n + 1)
                k, h = 2 * (n % 2), 2 * (n % 8)
                v.tensor_reduce(self.Q[:, n // 8, h:h + 2, 8], c.psum[:, k:k + 2, 0:320], AX.X, ALU.max,
                                negate=True).then_inc(s["maxed"], 1)

        def heads(b):
            v.wait_ge(s["av"], 16 * b + 16)
            if b:
                v.wait_ge(s["o_t"], b)
            for a in range(2):
                av = bank[7 - a][:, 0:144].rearrange("p (n c) -> p n c", c=9)
                v.reciprocal(self.rz[:, a, :], av[:, :, 8]).then_inc(s["rz"], 1)
            for a in range(2):
                av = bank[7 - a][:, 0:144].rearrange("p (n c) -> p n c", c=9)
                out = self.O[:, :, :].rearrange("p i (k a c) -> p (i k) a c", a=2, c=8)[:, :, a, :]
                v.wait_ge(s["rz"], 2 * b + a + 1)
                v.tensor_tensor(out, av[:, :, 0:8], bc(self.rz[:, a, :][:, :, None], (P, 16, 8)), ALU.mult) \
                    .then_inc(s["heads"], 1)

        def add(b):
            v.wait_ge(s["product"], b + 1)
            for i in range(2):
                j = 2 * b + i
                v.scalar_tensor_tensor(c.X[:, j, :], bank[6][:, 256 + i * P:256 + (i + 1) * P],
                                       c.gates[:, 1:2], c.X[:, j, :], ALU.mult, ALU.add).then_inc(s["added"], 1)

        for b in range(B):
            copy_queries(b, 0)
            if b:
                add(b - 1)
            maxima(b)
            copy_queries(b, 1)
            heads(b)
        add(B - 1)


class AcrossStage:

    HEADS, DH, T = 16, 8, 8
    SCALE = 8 ** -0.5

    def __init__(self, c, after):
        self.c, self.after, self.all_added = c, after, NG
        sc, d = c.scratch(), c.d
        self.norm = Norm(c, c.X, c.XN, 1.0, EPS, c.XT)
        self.Win = c.sb("d_Win", [P, 3 * D])
        self.Wout = c.sb("d_Wout", [P, D])
        self.b_in = c.sb("d_b_in", [1, 3 * D])
        self.b_out = c.sb("d_b_out", [1, D])
        self.affine = c.sb("d_affine", [P, 4, D])
        self.router_w = c.sb("d_router_w", [P, E])
        self.router_b = c.sb("d_router_b", [P, E])
        self.b1 = c.sb("d_b1", [P, E])
        self.b2 = c.sb("d_b2", [E, D])
        self.w1 = c.late[:, 0:1024].rearrange("p (e n) -> p e n", e=E)
        self.w2 = c.late[:, 1024:2048].rearrange("p (e n) -> p e n", e=E)
        self.load = (Load(c, "d").add(self.Win[:], d["L1_ffn_in_proj_w"]).add(self.Wout[:], d["L1_ffn_out_w"])
                     .add(self.b_in[:], d["L1_ffn_in_proj_b"][None, :]).add(self.b_out[:], d["L1_ffn_out_b"][None, :])
                     .add(self.affine[:, 0, :], d["L1_ffn_ln1_g"].partition_broadcast(P))
                     .add(self.affine[:, 1, :], d["L1_ffn_ln1_b"].partition_broadcast(P))
                     .add(self.affine[:, 2, :], d["L1_ffn_ln2_g"].partition_broadcast(P))
                     .add(self.affine[:, 3, :], d["L1_ffn_ln2_b"].partition_broadcast(P))
                     .add(self.router_w[:], d["L1_ffn_router_w"])
                     .add(self.router_b[:], d["L1_ffn_router_b"].partition_broadcast(P))
                     .add(self.b1[:], d["L1_ffn_b1"]).add(self.b2[:], d["L1_ffn_b2"])
                     .add(self.w1, d["L1_ffn_w1"]).add(self.w2, d["L1_ffn_w2"]))
        self.qkv = sc.take(8 * 384).rearrange("p (t n) -> p t n", t=8)
        self.prod = sc.take(4 * 1024).rearrange("p (u n) -> p u n", u=4)
        self.score = sc.take(1024).rearrange("p (t s h) -> p t s h", t=8, s=8)
        self.top = sc.take(128).rearrange("p (t h) -> p t h", t=8)
        self.mixed = sc.take(NT * D).rearrange("p (j d) -> p j d", j=NT)
        sc2 = c.scratch()
        self.hidden = sc2.take(2 * 512).rearrange("p (u n) -> p u n", u=2)
        self.pickT = sc2.take(NT * P)[0:E, :]
        self.own = c.dve_chain
        self.s = c.signals("d", "qkv qkv_copied prod scored shifted exp attn prod_v summed out residual "
                                "h_norm h_affine pick "
                                "hidden gelu result moe moe_affine added")
        self.out_turn = Turn(c, self.mixed, c.XT, self.s["summed"], 2, 8)
        self.ln1 = Norm(c, c.XN, c.XN)
        self.h_turn = Turn(c, c.XN, c.XT, self.s["h_affine"], 1)
        self.router = Router(c)
        self.bias_sum = ExpertBias(c, c.routing.table(2), self.pickT, self.b2[:])
        self.ln2 = Norm(c, c.XN, c.XN)

    def products(self, eng, m, t, kind):
        s = self.s
        n = 8 * m + t
        if kind == "scores":
            done, used = s["prod"], s["scored"]
            if n >= 2:
                eng.wait_ge(used, n - 1)
            q = bc(self.qkv[:, t, 0:D][:, None, :], (P, 8, D))
            eng.tensor_tensor(self.prod[:, n % 2, :].rearrange("p (s n) -> p s n", s=8), q,
                              self.qkv[:, :, D:2 * D], ALU.mult).then_inc(done, 1)
        else:
            if n >= 2:
                eng.wait_ge(s["summed"], n - 1)
            w = bc(self.score[:, t, :, :][:, :, :, None], (P, 8, 16, 8))
            eng.tensor_tensor(self.prod[:, 2 + n % 2, :].rearrange("p (s h c) -> p s h c", s=8, c=8), w,
                              self.qkv[:, :, 2 * D:3 * D].rearrange("p s (h c) -> p s h c", c=8),
                              ALU.mult).then_inc(s["prod_v"], 1)

    def pool(self, g):
        c, s = self.c, self.s
        self.norm.pool(g)
        for m in range(2):
            g.wait_ge(s["qkv_copied"], 16 * m + 16)
            for t in range(8):
                self.products(g, m, t, "scores")
            g.wait_ge(s["attn"], m + 1)
            for t in range(8):
                self.products(g, m, t, "values")
        self.ln1.pool(g)
        self.ln2.pool(g)

    def dve(self, v):
        c, s, own, r = self.c, self.s, self.own, self.c.routing
        self.norm.dve(v, self.after)
        for m in range(2):
            for t in range(8):
                n = 8 * m + t
                v.wait_ge(s["prod"], n + 1)
                if m and t == 0:
                    v.wait_ge(s["prod_v"], 8)
                v.tensor_reduce(self.score[:, t, :, :].rearrange("p s h -> p (s h)"),
                                self.prod[:, n % 2, :].rearrange("p (n c) -> p n c", c=8), AX.X, ALU.add) \
                    .then_inc(s["scored"], 1)
            v.wait_ge(s["scored"], 8 * m + 8)
            over_s = self.score[:, :, :, :].rearrange("p t s h -> p t h s")
            spread = bc(self.top[:, :, None, :], (P, 8, 8, 16))
            own.link(v, v.tensor_reduce(self.top, over_s, AX.X, ALU.max))
            v.tensor_tensor(self.score, self.score, spread, ALU.subtract).then_inc(s["shifted"], 1)
            v.wait_ge(s["exp"], m + 1)
            own.link(v, v.tensor_reduce(self.top, over_s, AX.X, ALU.add))
            own.link(v, v.reciprocal(self.top, self.top))
            v.tensor_tensor(self.score, self.score, spread, ALU.mult).then_inc(s["attn"], 1)
            for t in range(8):
                n = 8 * m + t
                v.wait_ge(s["prod_v"], n + 1)
                v.tensor_reduce(self.mixed[:, 2 * t + m, :],
                                self.prod[:, 2 + n % 2, :].rearrange("p (s n) -> p n s", s=8), AX.X, ALU.add) \
                    .then_inc(s["summed"], 1)
        for j in range(NT):
            v.wait_ge(s["out"], j + 1)
            v.tensor_tensor(c.XN[:, j, :], c.XN[:, j, :], c.bank[j % 4][:, 0:D], ALU.add) \
                .then_inc(s["residual"], 1)
        self.ln1.dve(v, s["residual"])
        self.scale_shift(v, self.ln1, 0, s["h_affine"])

        products = self.router.logits(v)
        logits, left, one, two = (r.table(k) for k in range(4))
        m1, m2, i1, i2 = (r.rows(k) for k in range(4))
        shape = (P, NT, E)
        own.link(v, v.tensor_tensor(logits, products, bc(self.router_b[:, None, :], shape), ALU.add))
        self.router.softmax(v, logits, logits, m1)
        r.first(v, own, logits, m1, one, i1)
        r.hide(v, own, logits, one, left)
        r.first(v, own, left, m2, two, i2)
        own.link(v, v.tensor_tensor(i1, i1, i2, ALU.max))
        v.tensor_tensor(one, bc(c.expert_m8[:, None, :], shape), bc(i1[:, :, None], shape), ALU.is_equal) \
            .then_inc(s["pick"], 1)
        v.wait_ge(s["pick"], 1)
        self.bias_sum.dve(v, c.XN, s["moe"])
        for n in range(E * NG):
            e, q = n // NG, n % NG
            v.wait_ge(s["result"], n + 1)
            v.wait_ge(s["moe"], NG + max(GROUP * (n - NG + 1), 0))
            for i in range(GROUP):
                j = GROUP * q + i
                v.scalar_tensor_tensor(c.XN[:, j, :], c.bank[2 + n % 2][:, i * D:(i + 1) * D],
                                       one[:, j, e:e + 1], c.XN[:, j, :], ALU.mult, ALU.add) \
                    .then_inc(s["moe"], 1)
        v.wait_ge(s["moe"], NG + E * NT)
        self.ln2.dve(v)
        self.scale_shift(v, self.ln2, 2, s["moe_affine"])
        for q in range(NG):
            v.wait_ge(s["moe_affine"], q + 1)
            tiles = slice(GROUP * q, GROUP * q + GROUP)
            v.scalar_tensor_tensor(c.X[:, tiles, :], c.XN[:, tiles, :], c.gates[:, 5:6], c.X[:, tiles, :],
                                   ALU.mult, ALU.add).then_inc(s["added"], 1)

    def scale_shift(self, v, norm, k, done):
        c = self.c
        for q in range(NG):
            tiles = c.XN[:, GROUP * q:GROUP * q + GROUP, :]
            norm.wait_normed(v, GROUP * q + GROUP)
            self.own.link(v, v.tensor_tensor(tiles, tiles, bc(self.affine[:, k, :][:, None, :], (P, GROUP, D)),
                                             ALU.mult))
            v.tensor_tensor(tiles, tiles, bc(self.affine[:, k + 1, :][:, None, :], (P, GROUP, D)),
                            ALU.add).then_inc(done, 1)

    def act(self, a):
        c, s = self.c, self.s
        self.norm.act(a)
        for m in range(2):
            if m:
                a.wait_ge(s["scored"], 8)
                a.wait_ge(s["prod_v"], 8)
            for t in range(8):
                n = 8 * m + t
                a.wait_ge(s["qkv"], n + 1)
                a.activation(self.qkv[:, t, 0:D], c.bank[n % 4][:, 0:D], ACT.Copy, scale=self.SCALE) \
                    .then_inc(s["qkv_copied"], 1)
                a.activation(self.qkv[:, t, D:3 * D], c.bank[n % 4][:, D:3 * D], ACT.Copy) \
                    .then_inc(s["qkv_copied"], 1)
            a.wait_ge(s["shifted"], m + 1)
            a.activation(self.score, self.score, ACT.Exp).then_inc(s["exp"], 1)
        self.out_turn.act(a)
        self.h_turn.act(a)
        self.router.act(a, c.routing.table(0))
        self.bias_sum.act(a)
        for n in range(E * NG):
            if n >= 2:
                a.wait_ge(s["result"], n - 1)
            a.wait_ge(s["hidden"], n + 1)
            a.activation(self.hidden[:, n % 2, :], c.bank[4 + n % 2][:, :], ACT.Gelu,
                         bias=self.b1[:, n // NG:n // NG + 1]).then_inc(s["gelu"], 1)

    def pe(self, t):
        c, s = self.c, self.s
        self.norm.pe(t)
        self.load.wait(t)
        self.norm.turn.wait(t, NG)
        for n in range(NT):
            j = 2 * (n % 8) + n // 8
            if n >= 4:
                t.wait_ge(s["qkv_copied"], 2 * (n - 3))
            out = c.bank[n % 4][:, 0:3 * D]
            t.matmul(out, c.XT[:, j * P:(j + 1) * P], self.Win[:], start=True, stop=False)
            t.matmul(out, c.ones[0:1, :], self.b_in[0:1, :], start=False, stop=True).then_inc(s["qkv"], 1)
        self.out_turn.pe(t)
        for j in range(NT):
            self.out_turn.wait(t, j // GROUP + 1)
            if j >= 4:
                t.wait_ge(s["residual"], j - 3)
            out = c.bank[j % 4][:, 0:D]
            t.matmul(out, c.XT[:, j * P:(j + 1) * P], self.Wout[:], start=True, stop=False)
            t.matmul(out, c.ones[0:1, :], self.b_out[0:1, :], start=False, stop=True).then_inc(s["out"], 1)
        self.h_turn.pe(t)
        self.h_turn.wait(t, NG)
        self.router.pe(t, self.router_w[:])
        t.wait_ge(s["pick"], 1)
        self.bias_sum.pe(t)

        def first(n):
            e, x = n // NG, c.XT[:, (n % NG) * CHUNK:(n % NG + 1) * CHUNK]
            if n >= 2:
                t.wait_ge(s["gelu"], n - 1)
            t.matmul(c.bank[4 + n % 2][:, :], self.w1[:, e, :], x, start=True, stop=True) \
                .then_inc(s["hidden"], 1)

        def second(n):
            e = n // NG
            t.wait_ge(s["gelu"], n + 1)
            t.wait_ge(s["moe"], NG + GROUP * max(n - 1, 0))
            for i in range(GROUP):
                last = t.matmul(c.bank[2 + n % 2][:, i * D:(i + 1) * D],
                                self.hidden[:, n % 2, i * P:(i + 1) * P], self.w2[:, e, :],
                                start=True, stop=True)
            last.then_inc(s["result"], 1)

        first(0)
        for n in range(E * NG):
            if n + 1 < E * NG:
                first(n + 1)
            second(n)


class MaskedStage:

    H, DH = 8, 16
    SCALE = 16 ** -0.5

    def __init__(self, c, after):
        self.c, self.after, self.all_added = c, after, NT
        sc, d = c.scratch(), c.d
        self.norm = Norm(c, c.X, c.XN, 1.0, EPS, c.XT)
        self.shift = c.sb("e_shift", [P, 1])
        self.mask_in = c.sb("e_mask_in", [P, B * SC], I32)
        self.load = (Load(c, "e").add(self.shift[:], d["L2_xattn_b"].partition_broadcast(P))
                     .add(self.mask_in[:], d["seq_mask"].partition_broadcast(P))
                     .add(c.CT[:], d["ctx_T"]))
        self.keys = sc.take(B * 512).rearrange("p (b h k) -> p b h k", b=B, h=8)
        self.vals = sc.take(B * 136).rearrange("p (b h n) -> p b h n", b=B, h=8)
        self.mask = sc.take(B * SC)
        self.prob = sc.take(2 * 512).rearrange("p (u n) -> p u n", u=2)
        self.probT = sc.take(2 * 512).rearrange("p (u n) -> p u n", u=2)
        self.top = sc.take(2 * 8).rearrange("p (u h) -> p u h", u=2)
        self.rz = sc.take(8)
        self.part = sc.take(D)
        self.head = sc.take(8)
        self.own, self.own_pool = c.dve_chain, c.pool_chain
        self.s = c.signals("e", "operands scores biased topped shifted exp p_t p_turned av rz added")

    def pool(self, g):
        c, s, own = self.c, self.s, self.own_pool
        self.norm.pool(g)
        self.load.wait(g)
        c.c2_load.wait(g)
        own.link(g, g.tensor_scalar(self.head, c.head16[:], self.SCALE, None, ALU.mult))
        own.link(g, g.tensor_copy(self.mask, self.mask_in[:]))
        own.link(g, g.tensor_scalar(self.mask, self.mask, -1.0, 1.0e30, ALU.add, ALU.mult))
        for b in range(B):
            own.link(g, g.tensor_tensor(self.keys[:, b, :, :], bc(c.CT[:, 0, b * SC:(b + 1) * SC][:, None, :], (P, 8, SC)),
                                        bc(self.head[:, :, None], (P, 8, SC)), ALU.mult))
            own.link(g, g.tensor_tensor(self.vals[:, b, :, 0:16],
                                        c.C2[:, b, D:2 * D].rearrange("p (h n) -> p h n", h=8),
                                        bc(c.parity[:, :, None], (P, 8, 16)), ALU.mult))
            g.tensor_copy(self.vals[:, b, :, 16], c.parity[:]).then_inc(s["operands"], 1)

    def dve(self, v):
        c, s, own = self.c, self.s, self.own
        self.norm.dve(v, self.after)
        v.wait_ge(s["operands"], B)
        self.load.wait(v)

        def softmax(j):
            u, b = j % 2, j // 2
            tile = self.prob[:, u, :].rearrange("p (h k) -> p h k", h=8)
            v.wait_ge(s["scores"], j + 1)
            if j >= 2:
                v.wait_ge(s["p_t"], j - 1)
            v.scalar_tensor_tensor(tile, c.bank[u][:, :].rearrange("p (h k) -> p h k", h=8), self.shift[:, 0:1],
                                   bc(self.mask[:, b * SC:(b + 1) * SC][:, None, :], (P, 8, SC)),
                                   ALU.add, ALU.add).then_inc(s["biased"], 1)
            v.wait_ge(s["biased"], j + 1)
            v.tensor_reduce(self.top[:, u, :], tile, AX.X, ALU.max).then_inc(s["topped"], 1)
            v.wait_ge(s["topped"], j + 1)
            v.tensor_tensor(tile, tile, bc(self.top[:, u, :][:, :, None], (P, 8, SC)), ALU.subtract) \
                .then_inc(s["shifted"], 1)

        def finish(j):
            v.wait_ge(s["av"], j + 1)
            av = c.bank[4 + j % 2][:, 0:136].rearrange("p (h n) -> p h n", h=8)
            own.link(v, v.reciprocal(self.rz, av[:, :, 16]))
            own.link(v, v.tensor_scalar(self.rz, self.rz, c.gates[:, 2:3], None, ALU.mult))
            own.link(v, v.tensor_tensor(self.part.rearrange("p (h n) -> p h n", h=8), av[:, :, 0:16],
                                        bc(self.rz[:, :, None], (P, 8, 16)), ALU.mult))
            v.tensor_tensor(c.X[:, j, :], c.X[:, j, :], self.part, ALU.add).then_inc(s["added"], 1)

        for j in range(NT):
            softmax(j)
            if j:
                finish(j - 1)
        finish(NT - 1)

    def act(self, a):
        c, s = self.c, self.s
        self.norm.act(a)
        for j in range(NT):
            u = j % 2
            a.wait_ge(s["shifted"], j + 1)
            a.activation(self.prob[:, u, :], self.prob[:, u, :], ACT.Exp).then_inc(s["exp"], 1)
            a.wait_ge(s["p_t"], j + 1)
            if j >= 2:
                a.wait_ge(s["av"], j - 1)
            a.activation(self.probT[:, u, :], c.bank[2 + u][:, :], ACT.Copy).then_inc(s["p_turned"], 1)

    def pe(self, t):
        c, s = self.c, self.s
        self.norm.pe(t)
        self.norm.turn.wait(t, NG)

        def scores(j):
            t.wait_ge(s["operands"], j // 2 + 1)
            if j >= 2:
                t.wait_ge(s["biased"], j - 1)
            t.matmul(c.bank[j % 2][:, :], c.XT[:, j * P:(j + 1) * P],
                     self.keys[:, j // 2, :, :].rearrange("p h k -> p (h k)"), start=True, stop=True) \
                .then_inc(s["scores"], 1)

        def turn(j):
            u = j % 2
            t.wait_ge(s["exp"], j + 1)
            if j >= 2:
                t.wait_ge(s["p_turned"], j - 1)
            for k in range(4):
                last = t.transpose(c.bank[2 + u][:, k * P:(k + 1) * P], self.prob[:, u, k * P:(k + 1) * P],
                                   c.ident[:])
            last.then_inc(s["p_t"], 1)

        def values(j):
            u = j % 2
            t.wait_ge(s["p_turned"], j + 1)
            if j >= 2:
                t.wait_ge(s["added"], j - 1)
            for k in range(4):
                last = t.matmul(c.bank[4 + u][:, k * 34:(k + 1) * 34], self.probT[:, u, k * P:(k + 1) * P],
                                self.vals[:, j // 2, 2 * k:2 * k + 2, :].rearrange("p h n -> p (h n)"),
                                start=True, stop=True)
            last.then_inc(s["av"], 1)

        scores(0)
        for j in range(NT):
            if j + 1 < NT:
                scores(j + 1)
            turn(j)
            values(j)


class Ranks:

    def __init__(self, c, name):
        self.c = c
        self.counted = c.sem(name + "_rank_products")
        self.own = c.dve_chain

    def pe(self, t, chosen):
        c = self.c
        t.matmul(c.bank[1][:, 0:NT * E], c.before[:], chosen, start=True, stop=True)
        t.matmul(c.bank[2][:, 0:NT * E], c.ones[:], chosen, start=True, stop=True).then_inc(self.counted, 1)

    def dve(self, v, ranks, totals, running, zeros):
        c, own = self.c, self.own
        own.link(v, v.memset(zeros, 0.0))
        v.wait_ge(self.counted, 1)
        own.link(v, v.tensor_copy(totals, c.bank[2][:, 0:NT * E].rearrange("p (j e) -> p j e", e=E)))
        for e in range(E):
            last = v.tensor_tensor_scan(running[:, :, e], totals[:, :, e], zeros, 0.0, ALU.add, ALU.add)
        own.link(v, last)
        own.link(v, v.tensor_tensor(running, running, totals, ALU.subtract))
        own.link(v, v.tensor_tensor(ranks, c.bank[1][:, 0:NT * E].rearrange("p (j e) -> p j e", e=E), running,
                                    ALU.add))


class CapacityStage:

    CAPACITY = math.ceil(B * S / E * 1.25)

    def __init__(self, c, after):
        self.c, self.after, self.all_added = c, after, NT * E
        sc, d = c.scratch(), c.d
        self.norm = Norm(c, c.X, c.XN, 1.0, EPS, c.XT)
        self.router_w = c.sb("f_router_w", [P, E])
        self.w_gate = c.sb("f_w_gate", [P, 256])
        self.w_down = c.late[:, 2048:4096].rearrange("p (k n) -> p k n", k=2)
        self.load = (Load(c, "f").add(self.router_w[:], d["L2_ffn_w_router"]).add(self.w_gate[:], d["L2_ffn_w_gate"])
                     .add(self.w_down, d["L2_ffn_w_down"]))
        self.hidden = sc.take(2 * NT * P).rearrange("p (k n) -> p k n", k=2)
        self.own = c.dve_chain
        self.router = Router(c)
        self.ranks = Ranks(c, "f")
        self.s = c.signals("f", "chosen hidden_in hidden result combine added")

    def dve(self, v):
        c, s, own, r = self.c, self.s, self.own, self.c.routing
        self.norm.dve(v, self.after)
        shape = (P, NT, E)
        prob, left, one, two, chosen, ranks, totals, running = (r.table(k) for k in range(8))
        m1, m2, i1, i2, zeros, total = (r.rows(k) for k in range(6))
        self.router.softmax(v, self.router.logits(v), prob, m1)
        r.first(v, own, prob, m1, one, i1)
        r.hide(v, own, prob, one, left)
        r.first(v, own, left, m2, two, i2)
        v.tensor_tensor(chosen, one, two, ALU.add).then_inc(s["chosen"], 1)
        v.wait_ge(s["chosen"], 1)
        self.ranks.dve(v, ranks, totals, running, zeros)
        own.link(v, v.tensor_scalar(ranks, ranks, float(self.CAPACITY), None, ALU.is_lt))
        own.link(v, v.tensor_tensor(one, one, bc(m1[:, :, None], shape), ALU.mult))
        own.link(v, v.tensor_tensor(two, two, bc(m2[:, :, None], shape), ALU.mult))
        own.link(v, v.tensor_tensor(one, one, two, ALU.add))
        own.link(v, v.tensor_tensor(one, one, ranks, ALU.mult))
        own.link(v, v.tensor_reduce(total, one, AX.X, ALU.add))
        own.link(v, v.tensor_scalar(total, total, 1.0e-6, None, ALU.add))
        own.link(v, v.reciprocal(total, total))
        own.link(v, v.tensor_tensor(one, one, bc(total[:, :, None], shape), ALU.mult))
        v.tensor_scalar(one, one, c.gates[:, 6:7], None, ALU.mult).then_inc(s["combine"], 1)
        v.wait_ge(s["combine"], 1)
        n = 0
        for q in range(NT // 2):
            v.wait_ge(s["result"], q + 1)
            for e in range(E):
                for i in range(2):
                    j = 2 * q + i
                    if e:
                        v.wait_ge(s["added"], n - 1)
                    bank = c.bank[4 * (q % 2) + 2 * i + e // 4]
                    v.scalar_tensor_tensor(c.X[:, j, :], bank[:, (e % 4) * D:(e % 4 + 1) * D],
                                           one[:, j, e:e + 1], c.X[:, j, :], ALU.mult, ALU.add) \
                        .then_inc(s["added"], 1)
                    n += 1

    def pool(self, g):
        self.norm.pool(g)

    def act(self, a):
        c, s = self.c, self.s
        self.norm.act(a)
        self.router.act(a, c.routing.table(0))
        for n in range(2 * NG):
            k, q = n % 2, n // 2
            a.wait_ge(s["hidden_in"], n + 1)
            a.activation(self.hidden[:, k, q * CHUNK:(q + 1) * CHUNK], c.bank[4 + n % 4][:, :], ACT.Silu) \
                .then_inc(s["hidden"], 1)

    def pe(self, t):
        c, s = self.c, self.s
        self.norm.pe(t)
        self.load.wait(t)
        self.norm.turn.wait(t, NG)
        self.router.pe(t, self.router_w[:])
        for n in range(2 * NG):
            k, q = n % 2, n // 2
            if n >= 4:
                t.wait_ge(s["hidden"], n - 3)
            t.matmul(c.bank[4 + n % 4][:, :], self.w_gate[:, k * P:(k + 1) * P],
                     c.XT[:, q * CHUNK:(q + 1) * CHUNK], start=True, stop=True).then_inc(s["hidden_in"], 1)
        t.wait_ge(s["chosen"], 1)
        self.ranks.pe(t, c.routing.table(4).rearrange("p j e -> p (j e)"))
        t.wait_ge(s["combine"], 1)
        t.wait_ge(s["hidden"], 2 * NG)
        for q in range(NT // 2):
            if q >= 2:
                t.wait_ge(s["added"], 2 * E * (q - 1))
            for i in range(2):
                j = 2 * q + i
                for half in range(2):
                    for k in range(2):
                        last = t.matmul(c.bank[4 * (q % 2) + 2 * i + half][:, :],
                                        self.hidden[:, k, j * P:(j + 1) * P],
                                        self.w_down[:, k, half * 512:(half + 1) * 512],
                                        start=(k == 0), stop=(k == 1))
            last.then_inc(s["result"], 1)


class NullStage:

    H, DH = 16, 64
    SCALE = 64 ** -0.5

    def __init__(self, c, after):
        self.c, self.after, self.all_added = c, after, NG
        sc, d = c.scratch(), c.d
        ar = Arena(c.arena_tensor, 10240)
        self.norm = Norm(c, c.X, c.XN, 1.0, EPS, c.XT)
        self.Wq = c.sb("g_Wq", [P, 8, D])
        self.Wkv = c.wide[:, :].rearrange("p (k n) -> p k n", k=2)
        self.Wout = c.sb("g_Wout", [P, 8, D])
        self.affine = c.sb("g_affine", [P, 2, D])
        self.null = c.sb("g_null", [P, 2])
        self.load = (Load(c, "g").add(self.Wq[:], d["L3_xattn_Wq"]).add(self.Wkv, d["L3_xattn_Wkv"])
                     .add(self.Wout[:], d["L3_xattn_Wout"])
                     .add(self.affine[:, 0, :], d["L3_xattn_ln_scale"].partition_broadcast(P))
                     .add(self.affine[:, 1, :], d["L3_xattn_ln_bias"].partition_broadcast(P))
                     .add(self.null[0:64, :], d["L3_xattn_null_kv"]).add(self.null[64:128, :], d["L3_xattn_null_kv"]))
        self.keys = ar.take(B * 1024).rearrange("p (b n) -> p b n", b=B)
        self.null_rows = ar.take(2 * 128).rearrange("p (k n) -> p k n", k=2)
        self.null_keys = ar.take(16)
        self.null_vals = ar.take(D)[0:16, :]
        self.null_probT = ar.take(2 * P)[0:16, :].rearrange("p (u n) -> p u n", u=2)
        self.top = ar.take(2 * 16).rearrange("p (u h) -> p u h", u=2)
        self.sums = ar.take(2 * 16).rearrange("p (u h) -> p u h", u=2)
        self.vals = sc.take(B * 1024).rearrange("p (b k d) -> p b k d", b=B, k=8)
        self.kv = sc.take(2 * 512).rearrange("p (u n) -> p u n", u=2)
        self.prob = sc.take(2 * 1040).rearrange("p (u n) -> p u n", u=2)
        self.probT = sc.take(1024)
        self.own = c.dve_chain
        self.post = Norm(c, c.XN, c.XN, 1.0, 1.0e-6)
        self.s = c.signals("g", "zeroed null_set nulls nulls_copied kv kv_copied folded_a folded_b copied_a copied_b "
                                "vals vals_copied scores raised shifted exp summed divided p_t p_turned out "
                                "out_copied affine added")

    def pool(self, g):
        c, s = self.c, self.s
        self.load.wait(g)
        g.memset(self.null_rows, 0.0).then_inc(s["zeroed"], 1)
        g.wait_ge(s["zeroed"], 1)
        for k in range(2):
            g.tensor_copy(self.null_rows[0:64, k, 0:P:18], bc(self.null[0:64, k:k + 1], (64, 8))) \
                .then_inc(s["null_set"], 1)
            g.tensor_copy(self.null_rows[64:128, k, 1:P:18], bc(self.null[64:128, k:k + 1], (64, 8))) \
                .then_inc(s["null_set"], 1)
        self.norm.pool(g)
        for j in range(NT):
            g.wait_ge(s["summed"], 2 * (j + 1))
            main = self.prob[:, j % 2, 0:1024].rearrange("p (h k) -> p h k", h=16)
            g.tensor_tensor(main, main, bc(self.sums[:, j % 2, :][:, :, None], (P, 16, 64)), ALU.mult) \
                .then_inc(s["divided"], 1)
            g.tensor_tensor(self.prob[:, j % 2, 1024:1040], self.prob[:, j % 2, 1024:1040],
                            self.sums[:, j % 2, :], ALU.mult).then_inc(s["divided"], 1)
        self.post.pool(g)

    def pe(self, t):
        c, s, bank = self.c, self.s, self.c.bank
        self.load.wait(t)
        t.wait_ge(self.before.s["added"], self.before.all_added)
        t.wait_ge(s["null_set"], 4)
        for k in range(8):
            t.matmul(bank[0][:, 0:16], self.Wq[:, k, :], self.null_rows[:, 0, 16 * k:16 * k + 16],
                     start=(k == 0), stop=(k == 7))
        for k in range(8):
            last = t.matmul(bank[1][0:16, 0:D], self.null_rows[:, 1, 16 * k:16 * k + 16], self.Wout[:, k, :],
                            start=(k == 0), stop=(k == 7))
        last.then_inc(s["nulls"], 1)
        for n in range(16):
            if n >= 2:
                t.wait_ge(s["kv_copied"], n - 1)
            for k in range(2):
                last = t.matmul(bank[2 + n % 2][:, :], self.Wkv[:, k, n * P:(n + 1) * P], c.CT[:, k, :],
                                start=(k == 0), stop=(k == 1))
            last.then_inc(s["kv"], 1)
            t.wait_ge(s["kv_copied"], n + 1)
            k = n % 8
            if n < 8:
                if n:
                    t.wait_ge(s["copied_a"], n)
                    t.wait_ge(s["copied_b"], n)
                t.matmul(bank[4][:, :], self.Wq[0:64, k, :], self.kv[0:64, n % 2, :], start=True, stop=True) \
                    .then_inc(s["folded_a"], 1)
                t.matmul(bank[5][:, :], self.Wq[64:128, k, :], self.kv[64:128, n % 2, :], start=True,
                         stop=True).then_inc(s["folded_b"], 1)
            else:
                if n == 8:
                    t.wait_ge(s["copied_b"], 8)
                for q in range(2):
                    m = 2 * k + q
                    if m >= 2:
                        t.wait_ge(s["vals_copied"], m - 1)
                    for b in range(4 * q, 4 * q + 4):
                        for a in range(2):
                            half = slice(64 * a, 64 * a + 64)
                            last = t.matmul(bank[6 + m % 2][half, (b % 4) * D:(b % 4 + 1) * D],
                                            self.kv[half, n % 2, b * SC:(b + 1) * SC], self.Wout[half, k, :],
                                            start=True, stop=True)
                    last.then_inc(s["vals"], 1)
        t.wait_ge(s["vals_copied"], 16)
        self.norm.pe(t)
        self.norm.turn.wait(t, NG)
        t.wait_ge(s["nulls_copied"], 2)

        def scores(j):
            u = j % 2
            x = c.XT[:, j * P:(j + 1) * P]
            if j >= 2:
                t.wait_ge(s["shifted"], 2 * (j - 1))
                t.wait_ge(s["out_copied"], j - 1)
            for half in range(2):
                t.matmul(bank[3 * u + half][:, :], x, self.keys[:, j // 2, half * 512:(half + 1) * 512],
                         start=True, stop=True)
            t.matmul(bank[3 * u + 2][:, 0:16], x, self.null_keys, start=True, stop=True) \
                .then_inc(s["scores"], 1)

        def turn(j):
            u = j % 2
            t.wait_ge(s["divided"], 2 * j + 2)
            if j:
                t.wait_ge(s["p_turned"], 3 * j)
            for k in range(8):
                last = t.transpose(bank[6 + k // 4][:, (k % 4) * P:(k % 4 + 1) * P],
                                   self.prob[:, u, k * P:(k + 1) * P], c.ident[:])
                if k == 3:
                    last.then_inc(s["p_t"], 1)
            last.then_inc(s["p_t"], 1)
            t.transpose(bank[3 * u + 2][0:16, P:2 * P], self.prob[:, u, 1024:1040], c.ident[:]) \
                .then_inc(s["p_t"], 1)

        def values(j):
            u = j % 2
            t.wait_ge(s["p_turned"], 3 * j + 3)
            out = bank[3 * u + 2][:, 256:256 + D]
            for k in range(8):
                t.matmul(out, self.probT[:, k * P:(k + 1) * P], self.vals[:, j // 2, k, :], start=(k == 0),
                         stop=False)
            t.matmul(out, self.null_probT[:, u, :], self.null_vals, start=False, stop=True) \
                .then_inc(s["out"], 1)

        scores(0)
        for j in range(NT):
            if j + 1 < NT:
                scores(j + 1)
            turn(j)
            values(j)

    def act(self, a):
        c, s, bank = self.c, self.s, self.c.bank
        a.wait_ge(s["nulls"], 1)
        a.activation(self.null_keys, bank[0][:, 0:16], ACT.Copy, scale=self.SCALE).then_inc(s["nulls_copied"], 1)
        a.activation(self.null_vals, bank[1][0:16, 0:D], ACT.Copy).then_inc(s["nulls_copied"], 1)
        for n in range(16):
            k = n % 8
            a.wait_ge(s["kv"], n + 1)
            if 2 <= n < 9:
                a.wait_ge(s["folded_b"], n - 1)
            elif n == 9:
                a.wait_ge(s["folded_b"], 8)
            elif n > 9:
                a.wait_ge(s["vals"], 2 * (n - 9))
            a.activation(self.kv[:, n % 2, :], bank[2 + n % 2][:, :], ACT.Copy).then_inc(s["kv_copied"], 1)
            if n < 8:
                a.wait_ge(s["folded_a"], n + 1)
                a.activation(self.keys[:, :, 2 * k * 64:2 * k * 64 + 64],
                             bank[4][:, :].rearrange("p (b n) -> p b n", b=B), ACT.Copy, scale=self.SCALE) \
                    .then_inc(s["copied_a"], 1)
            else:
                for q in range(2):
                    a.wait_ge(s["vals"], 2 * k + q + 1)
                    a.activation(self.vals[:, 4 * q:4 * q + 4, k, :],
                                 bank[6 + q][:, :].rearrange("p (b d) -> p b d", b=4), ACT.Copy) \
                        .then_inc(s["vals_copied"], 1)
        self.norm.act(a)

        def finish(j):
            u = j % 2
            for k in range(2):
                a.wait_ge(s["p_t"], 3 * j + k + 1)
                if j:
                    a.wait_ge(s["out"], j)
                a.activation(self.probT[:, k * 512:(k + 1) * 512], bank[6 + k][:, :], ACT.Copy) \
                    .then_inc(s["p_turned"], 1)
            a.wait_ge(s["p_t"], 3 * j + 3)
            a.activation(self.null_probT[:, u, :], bank[3 * u + 2][0:16, P:2 * P], ACT.Copy) \
                .then_inc(s["p_turned"], 1)
            a.wait_ge(s["out"], j + 1)
            a.activation(c.XN[:, j, :], bank[3 * u + 2][:, 256:256 + D], ACT.Copy).then_inc(s["out_copied"], 1)

        for j in range(NT):
            a.wait_ge(s["shifted"], 2 * j + 2)
            a.activation(self.prob[:, j % 2, :], self.prob[:, j % 2, :], ACT.Exp).then_inc(s["exp"], 1)
            finish(j)

    def dve(self, v):
        c, s, own, bank = self.c, self.s, self.own, self.c.bank
        for k in range(8):
            v.wait_ge(s["folded_b"], k + 1)
            v.tensor_scalar(self.keys[:, :, (2 * k + 1) * 64:(2 * k + 2) * 64],
                            bank[5][:, :].rearrange("p (b n) -> p b n", b=B), self.SCALE, None, ALU.mult) \
                .then_inc(s["copied_b"], 1)
        self.norm.dve(v, self.after)

        def softmax(j):
            u = j % 2
            main_in = c.psum[:, 3 * u:3 * u + 2, :].rearrange("p k (h n) -> p (k h) n", n=64)
            null_in = bank[3 * u + 2][:, 0:16]
            main = self.prob[:, u, 0:1024].rearrange("p (h n) -> p h n", n=64)
            null = self.prob[:, u, 1024:1040]
            top, sums = self.top[:, u, :], self.sums[:, u, :]
            v.wait_ge(s["scores"], j + 1)
            own.link(v, v.tensor_reduce(top, main_in, AX.X, ALU.max))
            own.link(v, v.tensor_tensor(top, null_in, top, ALU.max))
            if j >= 2:
                v.wait_ge(s["p_t"], 3 * (j - 1))
            v.tensor_tensor(main, main_in, bc(top[:, :, None], (P, 16, 64)), ALU.subtract) \
                .then_inc(s["shifted"], 1)
            v.tensor_tensor(null, null_in, top, ALU.subtract).then_inc(s["shifted"], 1)

        def sums(j):
            u = j % 2
            total = self.sums[:, u, :]
            main = self.prob[:, u, 0:1024].rearrange("p (h n) -> p h n", n=64)
            v.wait_ge(s["exp"], j + 1)
            if j >= 2:
                v.wait_ge(s["divided"], 2 * (j - 1))
            own.link(v, v.tensor_reduce(total, main, AX.X, ALU.add))
            v.tensor_tensor(total, total, self.prob[:, u, 1024:1040], ALU.add).then_inc(s["summed"], 1)
            v.wait_ge(s["summed"], 2 * j + 1)
            v.reciprocal(total, total).then_inc(s["summed"], 1)

        softmax(0)
        for j in range(NT):
            if j + 1 < NT:
                softmax(j + 1)
            sums(j)
        self.post.dve(v, s["out_copied"])
        for q in range(NG):
            tiles = slice(GROUP * q, GROUP * q + GROUP)
            self.post.wait_normed(v, GROUP * q + GROUP)
            own.link(v, v.tensor_tensor(c.XN[:, tiles, :], c.XN[:, tiles, :],
                                        bc(self.affine[:, 0, :][:, None, :], (P, GROUP, D)), ALU.mult))
            own.link(v, v.tensor_tensor(c.XN[:, tiles, :], c.XN[:, tiles, :],
                                        bc(self.affine[:, 1, :][:, None, :], (P, GROUP, D)), ALU.add))
            v.scalar_tensor_tensor(c.X[:, tiles, :], c.XN[:, tiles, :], c.gates[:, 3:4], c.X[:, tiles, :],
                                   ALU.mult, ALU.add).then_inc(s["added"], 1)


class DispatchStage:

    CAPACITY = math.ceil(B * S * 1.0 / E)
    SLOTS = E * CAPACITY
    TILES = CAPACITY // P

    def __init__(self, c, after):
        self.c, self.after, self.all_added = c, after, NT
        sc, d = c.scratch(), c.d
        assert self.CAPACITY == self.TILES * P
        self.norm = Norm(c, c.X, c.XN, 1.0, EPS, c.XT)
        self.router_w = c.sb("h_router_w", [P, E])
        self.w1 = c.wide[:, :].rearrange("p (e n) -> p e n", e=E)
        self.w2 = c.late[:, :].rearrange("p (e k d) -> p e k d", e=E, k=4)
        self.load = Load(c, "h").add(self.router_w[:], d["L3_ffn_Wr"])
        self.expert_load = Load(c, "h_experts").add(self.w1, d["L3_ffn_W1"].rearrange("e d f -> d e f"))
        for e in range(E):
            self.expert_load.add(self.w2[:, e], d["L3_ffn_W2"][e].rearrange("(k f) d -> f k d", k=4))
        self.taken = c.nc.dram_tensor("slots_in", (self.SLOTS, D), F32).ap()
        self.given = c.nc.dram_tensor("slots_out", (self.SLOTS, D), F32).ap()
        self.rows = sc.take(NT * D).rearrange("p (j d) -> p j d", j=NT)
        self.hidden = sc.take(2 * 1024).rearrange("p (u k n) -> p u k n", u=2, k=4)
        self.results = sc.take(NT * D).rearrange("p (j d) -> p j d", j=NT)
        self.scatter_at = c.sb("h_scatter_at", [P, NT], I32)
        self.gather_at = c.sb("h_gather_at", [P, NT], I32)
        self.own = c.dve_chain
        self.router = Router(c)
        self.ranks = Ranks(c, "h")
        self.s = c.signals("h", "cleared chosen slots scattered fetched hidden_in hidden_a "
                                "hidden_v result copied stored gathered added")
        self.slot_turn = Turn(c, self.rows, c.XT, self.s["fetched"], 0, 16 * NG)

    def clear(self, sp):
        c = self.c
        sp.wait_ge(c.zeroed, 1)
        for j in range(NT):
            sp.dma_start(self.taken[j * P:(j + 1) * P, :], c.zero_tile[:]).then_inc(self.s["cleared"], 16)

    def pool(self, g):
        c, s = self.c, self.s
        self.norm.pool(g)
        g.wait_ge(s["slots"], 1)
        g.wait_ge(s["cleared"], 16 * NT)
        for j in range(NT):
            g.indirect_dma_start(self.taken, bass.IndirectOffsetOnAxis(ap=self.scatter_at[:, j:j + 1], axis=0),
                                 c.XN[:, j, :], None, bounds_check=self.SLOTS - 1, oob_is_err=False) \
                .then_inc(s["scattered"], 16)
        g.wait_ge(s["stored"], 16 * E)
        for j in range(NT):
            g.indirect_dma_start(self.rows[:, j, :], None, self.given,
                                 bass.IndirectOffsetOnAxis(ap=self.gather_at[:, j:j + 1], axis=0),
                                 bounds_check=self.SLOTS - 1, oob_is_err=False) \
                .then_inc(s["gathered"], 16)

    def sync(self, sp):
        s = self.s
        sp.wait_ge(s["scattered"], 16 * NT)
        for q in range(NG):
            sp.dma_start(self.rows[:, GROUP * q:GROUP * q + GROUP, :],
                         self.taken.rearrange("(j p) d -> p j d", p=P)[:, GROUP * q:GROUP * q + GROUP, :]) \
                .then_inc(s["fetched"], 16)
        for e in range(E):
            j = self.TILES * e
            sp.wait_ge(s["copied"], e + 1)
            sp.dma_start(self.given.rearrange("(j p) d -> p j d", p=P)[:, j:j + self.TILES, :],
                         self.results[:, j:j + self.TILES, :]).then_inc(s["stored"], 16)

    def dve(self, v):
        c, s, own, r = self.c, self.s, self.own, self.c.routing
        self.norm.dve(v, self.after)
        shape = (P, NT, E)
        prob, tmp, one, chosen_at, ranks, totals, running = (r.table(k) for k in range(7))
        m1, i1, zeros, rank, kept, slot, weight = (r.rows(k) for k in range(7))
        self.router.softmax(v, self.router.logits(v), prob, m1)
        r.first(v, own, prob, m1, one, i1)
        v.tensor_copy(chosen_at, one).then_inc(s["chosen"], 1)
        self.ranks.dve(v, ranks, totals, running, zeros)
        own.link(v, v.tensor_tensor(ranks, ranks, one, ALU.mult))
        own.link(v, v.tensor_reduce(rank, ranks, AX.X, ALU.add))
        own.link(v, v.tensor_scalar(kept, rank, float(self.CAPACITY), None, ALU.is_lt))
        own.link(v, v.tensor_scalar(slot, i1, float(E), float(self.CAPACITY), ALU.add, ALU.mult))
        own.link(v, v.tensor_tensor(slot, slot, rank, ALU.add))
        own.link(v, v.tensor_tensor(slot, slot, kept, ALU.mult))
        own.link(v, v.tensor_copy(self.gather_at[:], slot))
        own.link(v, v.tensor_scalar(rank, kept, -float(2 * self.SLOTS), float(2 * self.SLOTS), ALU.mult, ALU.add))
        own.link(v, v.tensor_tensor(slot, slot, rank, ALU.add))
        own.link(v, v.tensor_tensor(weight, m1, kept, ALU.mult))
        own.link(v, v.tensor_scalar(weight, weight, c.gates[:, 7:8], None, ALU.mult))
        v.tensor_copy(self.scatter_at[:], slot).then_inc(s["slots"], 1)
        for e in range(E):
            v.wait_ge(s["hidden_in"], 2 * e + 2)
            if e >= 2:
                v.wait_ge(s["result"], e - 1)
            v.tensor_scalar(self.hidden[:, e % 2, 2:4, :].rearrange("p k n -> p (k n)"),
                            c.bank[2 * (e % 2) + 1][:, :], 0.0, None, ALU.max).then_inc(s["hidden_v"], 1)
        for j in range(NT):
            v.wait_ge(s["gathered"], 16 * NT)
            v.scalar_tensor_tensor(c.X[:, j, :], self.rows[:, j, :], weight[:, j:j + 1], c.X[:, j, :],
                                   ALU.mult, ALU.add).then_inc(s["added"], 1)

    def act(self, a):
        c, s = self.c, self.s
        self.norm.act(a)
        self.router.act(a, c.routing.table(0))
        self.slot_turn.act(a)

        def copy(e):
            a.wait_ge(s["result"], e + 1)
            a.activation(self.results[:, self.TILES * e:self.TILES * (e + 1), :].rearrange("p j d -> p (j d)"),
                         c.bank[4 + e % 2][:, 0:self.TILES * D], ACT.Copy).then_inc(s["copied"], 1)

        for e in range(E):
            a.wait_ge(s["hidden_in"], 2 * e + 1)
            if e >= 2:
                a.wait_ge(s["result"], e - 1)
            a.activation(self.hidden[:, e % 2, 0:2, :].rearrange("p k n -> p (k n)"),
                         c.bank[2 * (e % 2)][:, :], ACT.Relu).then_inc(s["hidden_a"], 1)
            if e:
                copy(e - 1)
        copy(E - 1)

    def pe(self, t):
        c, s = self.c, self.s
        self.norm.pe(t)
        self.load.wait(t)
        self.norm.turn.wait(t, NG)
        self.router.pe(t, self.router_w[:])
        t.wait_ge(s["chosen"], 1)
        self.ranks.pe(t, c.routing.table(3).rearrange("p j e -> p (j e)"))
        self.slot_turn.pe(t)
        self.expert_load.wait(t)
        t.wait_ge(s["slots"], 1)
        n = self.CAPACITY

        def first(e):
            self.slot_turn.wait(t, e // 2 + 1)
            if e >= 2:
                t.wait_ge(s["hidden_a"], e - 1)
                t.wait_ge(s["hidden_v"], e - 1)
            for k in range(4):
                last = t.matmul(c.bank[2 * (e % 2) + k // 2][:, (k % 2) * n:(k % 2 + 1) * n],
                                self.w1[:, e, k * P:(k + 1) * P], c.XT[:, e * n:(e + 1) * n], start=True, stop=True)
                if k % 2:
                    last.then_inc(s["hidden_in"], 1)

        def second(e):
            t.wait_ge(s["hidden_a"], e + 1)
            t.wait_ge(s["hidden_v"], e + 1)
            if e >= 2:
                t.wait_ge(s["copied"], e - 1)
            for i in range(self.TILES):
                for k in range(4):
                    last = t.matmul(c.bank[4 + e % 2][:, i * D:(i + 1) * D],
                                    self.hidden[:, e % 2, k, i * P:(i + 1) * P], self.w2[:, e, k, :],
                                    start=(k == 0), stop=(k == 3))
            last.then_inc(s["result"], 1)

        first(0)
        for e in range(E):
            if e + 1 < E:
                first(e + 1)
            second(e)


KINDS = (DepoolStage, ExpertPairStage, HeadsStage, AcrossStage, MaskedStage, CapacityStage, NullStage, DispatchStage,)


STAGES = 8


def build(nc, d, out):
    with ExitStack() as ctx:
        c = Core(nc, ctx, d)
        constants = Constants(c)
        c.arena_tensor = c.sb("arena", [P, 10240])
        c.late = c.sb("late", [P, 4096])
        c.wide = c.sb("wide", [P, 4096])
        c.routing = Routing(c)
        c.gates_in = c.sb("gates_in", [P, 8])
        c.gates_done = c.sem("gates_done")
        c.gate_load = (Load(c, "gates").add(c.gates_in[:, 0:4], d["g_xattn"].partition_broadcast(P))
                       .add(c.gates_in[:, 4:8], d["g_ffn"].partition_broadcast(P)))
        x_tiles = d["x"].rearrange("b (i p) d -> p (b i) d", p=P)
        x_load = Load(c, "x")
        for g in range(2):
            x_load.add(c.X[:, 8 * g:8 * g + 8, :], x_tiles[:, 8 * g:8 * g + 8, :])
        c2_load = (Load(c, "context").add(c.C2[0:64], d["ctx_2048"].rearrange("b s d -> s b d"))
                   .add(c.C2[64:128], d["ctx_2048"].rearrange("b s d -> s b d")))
        c.c2_load = c2_load
        stored = c.sem("stored")
        c.zero_tile, c.zeroed = c.sb("zero_tile", [P, D]), c.sem("zero_tile")
        stages = []
        for kind in KINDS[:STAGES]:
            stages.append(kind(c, None))
            stages[-1].before = stages[-2] if len(stages) > 1 else None
        block = ctx.enter_context(nc.Block())

        dispatch = [st for st in stages if isinstance(st, DispatchStage)]

        @block.sync
        def _(sp):
            c.gate_load.issue(sp)
            x_load.issue(sp)
            for n, st in enumerate(stages):
                if n == 2:
                    c2_load.issue(sp)
                st.load.issue(sp)
                if isinstance(st, ExpertPairStage):
                    for q in range(4):
                        st.expert_load[q].issue(sp)
            for st in dispatch:
                st.clear(sp)
                if st.before is not None:
                    sp.wait_ge(st.before.before.s["result"], NT // 2)
                    sp.wait_ge(st.before.s["kv"], 16)
                st.expert_load.issue(sp)
                st.sync(sp)
            for g in range(NG):
                sp.wait_ge(stages[-1].s["added"], stages[-1].all_added)
                sp.dma_start(out.rearrange("b (i p) d -> p (b i) d", p=P)[:, GROUP * g:GROUP * g + GROUP, :],
                             c.X[:, GROUP * g:GROUP * g + GROUP, :]).then_inc(stored, 16)
            sp.wait_ge(stored, 16 * NG)

        @block.gpsimd
        def _(g):
            constants.pool(g)
            g.wait_ge(c.constants_done, 1)
            g.memset(c.zero_tile[:], 0.0).then_inc(c.zeroed, 1)
            for st in stages:
                st.pool(g)

        @block.scalar
        def _(a):
            for st in stages:
                st.act(a)

        @block.vector
        def _(v):
            x_load.wait(v)
            v.wait_ge(c.gates_done, 1)
            for n, st in enumerate(stages):
                if n:
                    v.wait_ge(stages[n - 1].s["added"], stages[n - 1].all_added)
                st.dve(v)

        @block.tensor
        def _(t):
            for st in stages:
                st.pe(t)


def kernel(**inputs):
    import numpy as np
    import concourse.bacc as bacc
    from concourse.bass_utils import run_bass_kernel_spmd

    given = {n: np.asarray(a) for n, a in inputs.items()}
    T = lambda n: given[n].T
    lay = {
        "x": given["x"],
        "ctx_pairs": given["ctx_2048"].reshape(4, 2, SC, DC).transpose(1, 2, 0, 3).reshape(P, 4, DC),
        "ctx_T": given["ctx_2048"].reshape(B * SC, 2, P).transpose(2, 1, 0),
        "ctx_2048": given["ctx_2048"],
        "patch_lens": given["mask_BxS2_if0"].reshape(4, P).T,
        "seq_mask": given["mask_BxS2_ik0"].reshape(B * SC),
        "g_xattn": given["g_xattn"], "g_ffn": given["g_ffn"],
        "L0_xattn_g_res": given["L0_xattn_g_res"].reshape(D, 1),
        "L0_xattn_W_in": T("L0_xattn_W_in"),
        "L0_ffn_b1": given["L0_ffn_b1"].reshape(2 * E, P).T,
        "L0_ffn_b2": given["L0_ffn_b2"].reshape(2 * E, P).T,
        "L0_ffn_bg": given["L0_ffn_bg"].reshape(2 * E, P).T,
        "L1_xattn_w_qkv": T("L1_xattn_w_qkv"), "L1_xattn_w_proj": T("L1_xattn_w_proj"),
        "L1_ffn_in_proj_w": T("L1_ffn_in_proj_w"), "L1_ffn_out_w": T("L1_ffn_out_w"),
        "L1_ffn_router_w": T("L1_ffn_router_w"), "L1_ffn_b1": T("L1_ffn_b1"),
        "L1_ffn_w1": given["L1_ffn_w1"].transpose(2, 0, 1), "L1_ffn_w2": given["L1_ffn_w2"].transpose(2, 0, 1),
        "L2_ffn_w_router": T("L2_ffn_w_router"), "L2_ffn_w_gate": T("L2_ffn_w_gate"),
        "L2_ffn_w_down": given["L2_ffn_w_down"].transpose(2, 0, 1).reshape(2, P, E * D).transpose(1, 0, 2),
        "L3_xattn_null_kv": T("L3_xattn_null_kv"),
        "L3_xattn_Wq": given["L3_xattn_Wq"].T.reshape(8, P, D).transpose(1, 0, 2),
        "L3_xattn_Wkv": given["L3_xattn_Wkv"].reshape(2, P, 2048).transpose(1, 0, 2),
        "L3_xattn_Wout": given["L3_xattn_Wout"].reshape(8, P, D).transpose(1, 0, 2),
    }
    for n in ("L0_xattn_b_in L0_xattn_g_init L0_ffn_gate_w L0_ffn_gate_b L0_ffn_w1 L0_ffn_w2 "
              "L0_ffn_wg L0_ffn_w3 L0_ffn_b3 L1_xattn_b_proj L1_ffn_in_proj_b L1_ffn_out_b L1_ffn_ln1_g "
              "L1_ffn_ln1_b L1_ffn_router_b L1_ffn_b2 L1_ffn_ln2_g L1_ffn_ln2_b L2_xattn_b "
              "L3_xattn_ln_scale L3_xattn_ln_bias L3_ffn_Wr L3_ffn_W1 L3_ffn_W2").split():
        lay[n] = given[n]
    nc = bacc.Bacc("TRN2", target_bir_lowering=False, num_devices=1)
    arrays, d = {}, {}
    for n, a in lay.items():
        a = np.ascontiguousarray(a)
        arrays["in_" + n] = a
        d[n] = nc.dram_tensor("in_" + n, a.shape, mybir.dt.from_np(a.dtype), kind="ExternalInput").ap()
    out = nc.dram_tensor("out_x", (B, S, D), F32, kind="ExternalOutput").ap()
    build(nc, d, out)
    r = run_bass_kernel_spmd(nc, [arrays], core_ids=[0])
    return r.results[0]["out_x"]
```

```python
import math
from contextlib import ExitStack

import concourse.bass as bass
from concourse import mybir

F32 = mybir.dt.float32
I32 = mybir.dt.int32
ALU = mybir.AluOpType
ACT = mybir.ActivationFunctionType
AX = mybir.AxisListType

P = 128
B, S, D = 8, 256, 128
NT = B * S // P
SC, DC = 64, 256
E = 8
GROUP = 4
NG = NT // GROUP
CHUNK = GROUP * P
EPS = 1e-5

SMALL_STEP = 0.001
DECAY = -math.expm1(-SMALL_STEP)
KEEP = math.exp(-SMALL_STEP)


def bc(ap, shape):
    return ap.to_broadcast(list(shape))


class Arena:

    def __init__(self, tensor, size):
        self.tensor, self.size, self.at = tensor, size, 0

    def take(self, n):
        a = self.at
        self.at += n
        assert self.at <= self.size, (self.at, self.size)
        return self.tensor[:, a:a + n]


class Core:

    def __init__(self, nc, ctx, d):
        self.nc, self.ctx, self.d = nc, ctx, d
        self.psum = ctx.enter_context(nc.psum_tensor("psum", [P, 8, 512], F32))
        self.bank = [self.psum[:, i, :] for i in range(8)]
        self.X = self.sb("X", [P, NT, D])
        self.XN = self.sb("XN", [P, NT, D])
        self.XT = self.sb("XT", [P, NT * P])
        self.stats = self.sb("stats", [P, NT, 6])
        self.moments = self.sb("moments", [P, NT, 2])
        self.veps = self.sb("veps", [P, NT])
        self.rstd = self.sb("rstd", [P, NT])
        self.gates = self.sb("gates", [P, 8])
        self.scratch_tensor = self.sb("scratch", [P, 12544])
        self.C = self.sb("C", [P, 4, DC])
        self.CT = self.sb("CT", [P, 2, B * SC])
        self.C2 = self.sb("C2", [P, B, DC])

        self.norms = self.turns = 0
        self.stats_done, self.moments_done = self.sem("stats_done"), self.sem("moments_done")
        self.veps_done, self.rstd_done = self.sem("veps_done"), self.sem("rstd_done")
        self.normed, self.transposed = self.sem("normed"), self.sem("transposed")
        self.turned_done = self.sem("turned_done")
        self.routers, self.spreads = 0, 0
        self.logits_done, self.shift_done = self.sem("logits_done"), self.sem("shift_done")
        self.exp_done = self.sem("exp_done")
        self.rows_turned, self.rows_copied = self.sem("rows_turned"), self.sem("rows_copied")
        self.bias_products = self.sem("bias_products")
        self.dve_chain, self.pool_chain = Chain(self, "dve_chain"), Chain(self, "pool_chain")

    def scratch(self):
        return Arena(self.scratch_tensor, 12544)

    def signals(self, prefix, names):
        return {n: self.sem(prefix + "_" + n) for n in names.split()}

    def sb(self, name, shape, dt=F32):
        return self.ctx.enter_context(self.nc.sbuf_tensor(name, shape, dt))

    def sem(self, name):
        return self.ctx.enter_context(self.nc.semaphore(name))


class Chain:

    def __init__(self, c, name):
        self.sem, self.n = c.sem(name), 0

    def link(self, eng, ins):
        self.n += 1
        ins.then_inc(self.sem, 1)
        eng.wait_ge(self.sem, self.n)


class Norm:

    def __init__(self, c, src, dst, mul=1.0, add=EPS, turned=None):
        self.c, self.src, self.dst, self.mul, self.add = c, src, dst, mul, add
        self.tiles_before, self.groups_before = NT * c.norms, NG * c.norms
        c.norms += 1
        self.turn = Turn(c, dst, turned, c.normed, GROUP, self.tiles_before) if turned is not None else None

    def dve(self, v, ready=None):
        c, before = self.c, self.tiles_before

        def normalize(g):
            v.wait_ge(c.rstd_done, self.groups_before + g + 1)
            for j in range(GROUP * g, GROUP * g + GROUP):
                v.tensor_scalar(self.dst[:, j, :], self.src[:, j, :], c.moments[:, j, 0:1],
                                c.rstd[:, j:j + 1], ALU.subtract, ALU.mult).then_inc(c.normed, 1)

        for g in range(NG):
            for j in range(GROUP * g, GROUP * g + GROUP):
                if ready is not None:
                    v.wait_ge(ready, j + 1)
                v.bn_stats(c.stats[:, j, :], self.src[:, j, :]).then_inc(c.stats_done, 1)
            for j in range(GROUP * g, GROUP * g + GROUP):
                v.wait_ge(c.stats_done, before + j + 1)
                v.bn_aggr(c.moments[:, j, :], c.stats[:, j, :]).then_inc(c.moments_done, 1)
            if g:
                normalize(g - 1)
        normalize(NG - 1)

    def wait_normed(self, eng, tiles):
        eng.wait_ge(self.c.normed, self.tiles_before + tiles)

    def pool(self, g_):
        c = self.c
        for g in range(NG):
            a, b = GROUP * g, GROUP * g + GROUP
            g_.wait_ge(c.moments_done, self.tiles_before + b)
            g_.tensor_scalar(c.veps[:, a:b], c.moments[:, a:b, 1], self.mul, self.add,
                             ALU.mult, ALU.add).then_inc(c.veps_done, 1)
            g_.wait_ge(c.veps_done, self.groups_before + g + 1)
            g_.tensor_tensor(c.rstd[:, a:b], c.veps[:, a:b], c.minus_half[:, a:b],
                             ALU.pow).then_inc(c.rstd_done, 1)

    def pe(self, t):
        self.turn.pe(t)

    def act(self, a):
        self.turn.act(a)


class Turn:

    def __init__(self, c, src, dst, ready, per_group, base=0, banks=(6, 7)):
        self.c, self.src, self.dst, self.ready, self.per_group = c, src, dst, ready, per_group
        self.base, self.banks, self.before = base, banks, NG * c.turns
        c.turns += 1

    def wait(self, eng, groups):
        eng.wait_ge(self.c.turned_done, self.before + groups)

    def pe(self, t):
        c = self.c
        for g in range(NG):
            t.wait_ge(self.ready, self.base + self.per_group * (g + 1))
            if g >= 2:
                self.wait(t, g - 1)
            for i in range(GROUP):
                last = t.transpose(c.bank[self.banks[g % 2]][:, i * P:(i + 1) * P],
                                   self.src[:, GROUP * g + i, :], c.ident[:])
            last.then_inc(c.transposed, 1)

    def act(self, a):
        c = self.c
        for g in range(NG):
            a.wait_ge(c.transposed, self.before + g + 1)
            a.activation(self.dst[:, g * CHUNK:(g + 1) * CHUNK], c.bank[self.banks[g % 2]][:, :],
                         ACT.Copy).then_inc(c.turned_done, 1)


class Load:

    def __init__(self, c, name):
        self.sem, self.parts = c.sem(name + "_loaded"), []

    def add(self, dst, src):
        self.parts.append((dst, src))
        return self

    def issue(self, eng):
        for dst, src in self.parts:
            eng.dma_start(dst, src).then_inc(self.sem, 16)

    def wait(self, eng):
        eng.wait_ge(self.sem, 16 * len(self.parts))


class Constants:

    def __init__(self, c):
        self.c = c
        c.ident = c.sb("ident", [P, P])
        c.ones = c.sb("ones", [P, P])
        c.half_ones = c.sb("half_ones", [P, P])
        c.half_upto = c.sb("half_upto", [P, P])
        c.before = c.sb("before", [P, P])
        c.minus_half = c.sb("minus_half", [P, NT])
        c.expert_m8 = c.sb("expert_m8", [P, E])
        c.column = c.sb("column", [P, S])
        c.row64 = c.sb("row64", [P, 1])
        c.head16 = c.sb("head16", [P, 8])
        c.parity = c.sb("parity", [P, 8])
        c.decay = c.sb("decay", [P, P])
        c.decayT = c.sb("decayT", [P, P])
        self.own = c.pool_chain
        c.constants_done = c.sem("constants_done")

    def pool(self, g):
        c, own = self.c, self.own

        def select(t, pattern, base, mult, op=ALU.is_ge, fill=0.0):
            own.link(g, g.affine_select(out=t, in_=t, compare_op=op, fill=fill, base=base,
                                        pattern=pattern, channel_multiplier=mult))

        own.link(g, g.memset(c.ident[:], 0.0))
        select(c.ident[:], [[-1, P]], 0, 1, ALU.not_equal, 1.0)
        g.memset(c.minus_half[:], -0.5)
        g.memset(c.decay[:], DECAY)
        own.link(g, g.memset(c.ones[:], 1.0))
        own.link(g, g.memset(c.before[:], 1.0))
        select(c.before[:], [[1, P]], -1, -1)
        own.link(g, g.memset(c.half_upto[:], 1.0))
        select(c.half_upto[:], [[1, P]], 0, -1)
        own.link(g, g.memset(c.half_upto[0:64, 64:128], 0.0))
        own.link(g, g.memset(c.half_ones[:], 1.0))
        own.link(g, g.memset(c.half_ones[0:64, 64:128], 0.0))
        own.link(g, g.memset(c.half_ones[64:128, 0:64], 0.0))
        own.link(g, g.memset(c.head16[:], 1.0))
        select(c.head16[:], [[-16, 8]], 0, 1)
        select(c.head16[:], [[16, 8]], 15, -1)
        par = c.parity[:, :].rearrange("p (k a) -> p k a", a=2)
        own.link(g, g.memset(c.parity[:], 0.0))
        g.memset(par[0:64, :, 0], 1.0)
        own.link(g, g.memset(par[64:128, :, 1], 1.0))
        own.link(g, g.iota(c.expert_m8[:], pattern=[[1, E]], base=-E, channel_multiplier=0,
               allow_small_or_imprecise_dtypes=True))
        own.link(g, g.iota(c.column[:], pattern=[[1, S]], base=0, channel_multiplier=0,
               allow_small_or_imprecise_dtypes=True))
        own.link(g, g.iota(c.row64[0:64, :], pattern=[[0, 1]], base=0, channel_multiplier=1,
               allow_small_or_imprecise_dtypes=True))
        g.iota(c.row64[64:128, :], pattern=[[0, 1]], base=0, channel_multiplier=1,
               allow_small_or_imprecise_dtypes=True).then_inc(c.constants_done, 1)


class DepoolStage:

    def __init__(self, c, after):
        self.c, self.after = c, after
        sc, d = c.scratch(), c.d
        self.norm = Norm(c, c.X, c.XN, 1.0 + EPS, EPS * EPS, c.XT)
        self.WinT = c.sb("WinT", [P, D])
        self.Wg = c.sb("Wg", [P, D])
        self.g_res = c.sb("g_res", [P, 1])
        self.b_in = c.sb("b_in", [1, D])
        self.lens = c.sb("lens", [P, 4], I32)
        self.small = c.sb("a_small", [P, 7, 4])
        self.g_init = sc.take(D)
        self.square = sc.take(DC)
        self.hp = sc.take(4 * D).rearrange("p (a d) -> p a d", a=4)
        self.states = sc.take(4 * D).rearrange("p (a d) -> p a d", a=4)
        self.hit = sc.take(4 * S).rearrange("p (a t) -> p a t", a=4)
        self.count = sc.take(4 * S).rearrange("p (a t) -> p a t", a=4)
        self.zeros = sc.take(S)
        self.pick = sc.take(4 * S).rearrange("p (a t) -> p a t", a=4)
        self.all_added = NT
        self.load = (Load(c, "a").add(c.C[:], d["ctx_pairs"])
                     .add(self.lens[:], d["patch_lens"])
                     .add(self.g_init, d["L0_xattn_g_init"][0:D].partition_broadcast(P))
                     .add(self.g_res[:], d["L0_xattn_g_res"])
                     .add(self.WinT[:], d["L0_xattn_W_in"])
                     .add(self.b_in[:], d["L0_xattn_b_in"][None, :]))
        self.own = c.dve_chain
        self.s = c.signals("a", "mean_square patch_eps patch_rstd patches scanned states lengths ends "
                                "hits counted picks product added")

    def dve(self, v):
        c, s, own, sm = self.c, self.s, self.own, self.small
        v.wait_ge(c.constants_done, 1)
        own.link(v, v.tensor_scalar(c.decayT[:], c.ident[:], KEEP, None, ALU.mult))
        own.link(v, v.tensor_tensor_scan(c.decayT[:], c.decay[:], c.decayT[:], 0.0, ALU.mult, ALU.add))
        own.link(v, v.memset(c.decayT[0:64, 64:128], 0.0))
        self.load.wait(v)
        own.link(v, v.tensor_copy(sm[:, 0, :], self.lens[:]))
        v.tensor_scalar(self.Wg[:], self.WinT[:], self.g_res[:, 0:1], None, ALU.mult) \
            .then_inc(s["lengths"], 1)
        v.wait_ge(s["patch_rstd"], 1)
        for a in range(4):
            v.scalar_tensor_tensor(self.hp[:, a, :], c.C[:, a, 0:D], sm[:, 6, a:a + 1], self.g_init,
                                   ALU.mult, ALU.mult).then_inc(s["patches"], 1)
        v.wait_ge(s["ends"], 1)
        own.link(v, v.tensor_scalar(sm[:, 1, :], c.bank[4][:, 0:4], -1.0, None, ALU.add))
        own.link(v, v.tensor_scalar(sm[:, 2, :], sm[:, 1, :], 0.0, float(S), ALU.is_lt, ALU.mult))
        own.link(v, v.tensor_tensor(sm[:, 3, :], sm[:, 1, :], sm[:, 2, :], ALU.add))
        for a in range(4):
            v.tensor_scalar(self.hit[:, a, :], c.column[:], sm[:, 3, a:a + 1], None, ALU.is_equal) \
                .then_inc(s["hits"], 1)
        own.link(v, v.memset(self.zeros, 0.0))
        v.wait_ge(s["counted"], 1)
        for k in range(2):
            own.link(v, v.tensor_scalar(self.count[:, 2 * k:2 * k + 2, :].rearrange("p a t -> p (a t)"),
                                        c.bank[4 + k][:, :], 1.0, None, ALU.min))
        for a in range(4):
            own.link(v, v.tensor_tensor_scan(self.count[:, a, :], self.count[:, a, :], self.zeros, 0.0,
                                             ALU.add, ALU.add))
        own.link(v, v.tensor_scalar(self.count[:, :, :], self.count[:, :, :], -1.0, 0.0, ALU.add, ALU.max))
        v.tensor_scalar(self.pick[:, :, :], self.count[:, :, :], float(SC - 1), c.row64[:, 0:1],
                        ALU.min, ALU.is_equal).then_inc(s["picks"], 1)
        self.norm.dve(v, self.after)
        for j in range(NT):
            v.wait_ge(s["product"], j // 2 + 1)
            v.scalar_tensor_tensor(c.X[:, j, :], c.bank[j // 2 % 4][:, (j % 2) * D:(j % 2 + 1) * D],
                                   c.gates[:, 0:1], c.X[:, j, :], ALU.mult, ALU.add) \
                .then_inc(s["added"], 1)

    def pool(self, g):
        c, s, sm = self.c, self.s, self.small
        g.wait_ge(s["mean_square"], 4)
        g.tensor_scalar(sm[:, 5, :], sm[:, 4, :], 1.0 / DC, EPS, ALU.mult, ALU.add) \
            .then_inc(s["patch_eps"], 1)
        g.wait_ge(s["patch_eps"], 1)
        g.tensor_tensor(sm[:, 6, :], sm[:, 5, :], c.minus_half[:, 0:4], ALU.pow) \
            .then_inc(s["patch_rstd"], 1)
        self.norm.pool(g)

    def act(self, a):
        c, s, sm = self.c, self.s, self.small
        c.gate_load.wait(a)
        a.activation(c.gates[:], c.gates_in[:], ACT.Tanh).then_inc(c.gates_done, 1)
        self.load.wait(a)
        for k in range(4):
            if k:
                a.wait_ge(s["mean_square"], k)
            a.activation(self.square, c.C[:, k, :], ACT.Square, accum_out=sm[:, 4, k:k + 1]) \
                .then_inc(s["mean_square"], 1)
        a.wait_ge(s["scanned"], 1)
        a.activation(self.states[:, :, :].rearrange("p a d -> p (a d)"), c.bank[5][:, :], ACT.Copy) \
            .then_inc(s["states"], 1)
        self.norm.act(a)

    def pe(self, t):
        c, s = self.c, self.s
        t.wait_ge(c.constants_done, 1)
        t.wait_ge(s["lengths"], 1)
        t.matmul(c.bank[4][:, 0:4], c.half_upto[:], self.small[:, 0, :], start=True, stop=True) \
            .then_inc(s["ends"], 1)
        t.wait_ge(s["patches"], 4)
        t.matmul(c.bank[5][:, :], c.decayT[:], self.hp[:, :, :].rearrange("p a d -> p (a d)"),
                 start=True, stop=True).then_inc(s["scanned"], 1)
        t.wait_ge(s["states"], 1)
        t.wait_ge(s["hits"], 4)
        for k in range(2):
            last = t.matmul(c.bank[4 + k][:, :], c.half_ones[:],
                            self.hit[:, 2 * k:2 * k + 2, :].rearrange("p a t -> p (a t)"),
                            start=True, stop=True)
        last.then_inc(s["counted"], 1)
        self.norm.pe(t)
        t.wait_ge(s["picks"], 1)
        for b in range(B):
            h = slice(64 * (b % 2), 64 * (b % 2) + 64)
            self.norm.turn.wait(t, b // 2 + 1)
            if b >= 4:
                t.wait_ge(s["added"], 2 * (b - 4) + 2)
            for i in range(2):
                j = 2 * b + i
                out = c.bank[b % 4][:, i * D:(i + 1) * D]
                t.matmul(out, c.XT[:, j * P:(j + 1) * P], self.Wg[:], start=True, stop=False)
                t.matmul(out, c.ones[0:1, :], self.b_in[0:1, :], start=False, stop=False)
                last = t.matmul(out, self.pick[h, b // 2, i * P:(i + 1) * P], self.states[h, b // 2, :],
                                start=False, stop=True)
            last.then_inc(s["product"], 1)


class Routing:

    def __init__(self, c):
        self.c = c
        self.small = c.sb("routing_small", [P, 16, NT])
        self.wide = c.sb("routing_wide", [P, 8, NT, E])

    def rows(self, k):
        return self.small[:, k, :]

    def table(self, k):
        return self.wide[:, k, :, :]

    def first(self, v, own, values, biggest, onehot, index):
        c, shape, tmp = self.c, (P, NT, E), self.table(7)
        place = bc(c.expert_m8[:, None, :], shape)
        own.link(v, v.tensor_reduce(biggest, values, AX.X, ALU.max))
        own.link(v, v.tensor_tensor(tmp, values, bc(biggest[:, :, None], shape), ALU.is_ge))
        own.link(v, v.tensor_tensor(tmp, tmp, place, ALU.mult))
        own.link(v, v.tensor_reduce(index, tmp, AX.X, ALU.min))
        own.link(v, v.tensor_tensor(onehot, place, bc(index[:, :, None], shape), ALU.is_equal))

    def hide(self, v, own, values, onehot, left):
        own.link(v, v.scalar_tensor_tensor(left, onehot, -3.0e38, values, ALU.mult, ALU.add))


class Router:

    def __init__(self, c):
        c.routers += 1
        self.c, self.n = c, c.routers

    def pe(self, t, weights):
        c = self.c
        for j in range(NT):
            last = t.matmul(c.bank[0][:, j * E:(j + 1) * E], c.XT[:, j * P:(j + 1) * P], weights,
                            start=True, stop=True)
        last.then_inc(c.logits_done, 1)

    def logits(self, v):
        v.wait_ge(self.c.logits_done, self.n)
        return self.c.bank[0][:, 0:NT * E].rearrange("p (j e) -> p j e", e=E)

    def softmax(self, v, logits, prob, top):
        c, own, shape = self.c, self.c.dve_chain, (P, NT, E)
        own.link(v, v.tensor_reduce(top, logits, AX.X, ALU.max))
        v.tensor_tensor(prob, logits, bc(top[:, :, None], shape), ALU.subtract).then_inc(c.shift_done, 1)
        v.wait_ge(c.exp_done, self.n)
        own.link(v, v.tensor_reduce(top, prob, AX.X, ALU.add))
        own.link(v, v.reciprocal(top, top))
        own.link(v, v.tensor_tensor(prob, prob, bc(top[:, :, None], shape), ALU.mult))

    def act(self, a, values):
        a.wait_ge(self.c.shift_done, self.n)
        a.activation(values, values, ACT.Exp).then_inc(self.c.exp_done, 1)


class ExpertBias:

    def __init__(self, c, table, turned, bias):
        self.c, self.table, self.turned, self.bias = c, table, turned, bias
        self.before = NG * c.spreads
        c.spreads += 1

    def pe(self, t):
        c = self.c
        for q in range(NG):
            if q >= 2:
                t.wait_ge(c.rows_copied, self.before + q - 1)
            for i in range(GROUP):
                last = t.transpose(c.bank[4 + q % 2][0:E, i * P:(i + 1) * P], self.table[:, GROUP * q + i, :],
                                   c.ident[:])
            last.then_inc(c.rows_turned, 1)
        for q in range(NG):
            t.wait_ge(c.rows_copied, self.before + q + 1)
            for i in range(GROUP):
                j = GROUP * q + i
                last = t.matmul(c.bank[q][:, i * D:(i + 1) * D], self.turned[:, j * P:(j + 1) * P],
                                self.bias, start=True, stop=True)
            last.then_inc(c.bias_products, 1)

    def act(self, a):
        c = self.c
        for q in range(NG):
            a.wait_ge(c.rows_turned, self.before + q + 1)
            a.activation(self.turned[:, q * CHUNK:(q + 1) * CHUNK], c.bank[4 + q % 2][0:E, :], ACT.Copy) \
                .then_inc(c.rows_copied, 1)

    def dve(self, v, rows, done):
        c = self.c
        for q in range(NG):
            v.wait_ge(c.bias_products, self.before + q + 1)
            j = GROUP * q
            v.tensor_tensor(rows[:, j:j + GROUP, :], rows[:, j:j + GROUP, :],
                            c.bank[q][:, :].rearrange("p (j d) -> p j d", d=D), ALU.add).then_inc(done, 1)


class ExpertPairStage:

    def __init__(self, c, after):
        self.c, self.after = c, after
        sc, d = c.scratch(), c.d
        self.norm = Norm(c, c.X, c.XN, 1.0, EPS, c.XT)
        ar = Arena(c.arena_tensor, 10240)
        self.w1 = ar.take(E * 256).rearrange("p (e f) -> p e f", e=E)
        self.w2 = ar.take(E * 256).rearrange("p (e f) -> p e f", e=E)
        self.wg = ar.take(E * 512).rearrange("p (e k f) -> p e k f", e=E, k=2)
        self.w3 = ar.take(E * 256).rearrange("p (e k f) -> p e k f", e=E, k=2)
        self.gate_w = c.sb("b_gate_w", [P, E])
        self.gate_b = c.sb("b_gate_b", [P, E])
        self.bias = c.sb("b_bias", [P, 3, 2 * E])
        self.b3 = c.sb("b_b3", [E, D])
        self.all_added = NG + E * NT
        self.load = (Load(c, "b").add(self.gate_w[:], d["L0_ffn_gate_w"])
                     .add(self.gate_b[:], d["L0_ffn_gate_b"].partition_broadcast(P))
                     .add(self.bias[:, 0, :], d["L0_ffn_b1"]).add(self.bias[:, 1, :], d["L0_ffn_b2"])
                     .add(self.bias[:, 2, :], d["L0_ffn_bg"]).add(self.b3[:], d["L0_ffn_b3"]))
        self.expert_load = [Load(c, f"b_experts{q}")
                            .add(self.w1[:, 2 * q:2 * q + 2], d["L0_ffn_w1"][2 * q:2 * q + 2].rearrange("e h f -> h e f"))
                            .add(self.w2[:, 2 * q:2 * q + 2], d["L0_ffn_w2"][2 * q:2 * q + 2].rearrange("e h f -> h e f"))
                            .add(self.wg[:, 2 * q], d["L0_ffn_wg"][2 * q].rearrange("(k h) f -> h k f", k=2))
                            .add(self.wg[:, 2 * q + 1], d["L0_ffn_wg"][2 * q + 1].rearrange("(k h) f -> h k f", k=2))
                            .add(self.w3[:, 2 * q], d["L0_ffn_w3"][2 * q].rearrange("(k h) f -> h k f", k=2))
                            .add(self.w3[:, 2 * q + 1], d["L0_ffn_w3"][2 * q + 1].rearrange("(k h) f -> h k f", k=2))
                            for q in range(4)]
        self.x2 = sc.take(2 * 1024).rearrange("p (u k n) -> p u k n", u=2, k=2)
        self.z = sc.take(2 * 1024).rearrange("p (u k n) -> p u k n", u=2, k=2)
        self.act_out = sc.take(2 * 1024).rearrange("p (u k n) -> p u k n", u=2, k=2)
        self.weightT = sc.take(NT * P)[0:E, :]
        self.own = c.dve_chain
        self.s = c.signals("b", "weights added second second_copied z third silu result")
        self.router = Router(c)
        self.bias_sum = ExpertBias(c, c.routing.table(2), self.weightT, self.b3[:])

    def dve(self, v):
        c, s, own, r = self.c, self.s, self.own, self.c.routing
        self.norm.dve(v, self.after)
        products = self.router.logits(v)
        self.load.wait(v)
        logits, left, one, two = r.table(0), r.table(1), r.table(2), r.table(3)
        m1, m2, idx, gap, w1, w2 = (r.rows(k) for k in range(6))
        own.link(v, v.tensor_tensor(logits, products, bc(self.gate_b[:, None, :], (P, NT, E)), ALU.add))
        r.first(v, own, logits, m1, one, idx)
        r.hide(v, own, logits, one, left)
        r.first(v, own, left, m2, two, idx)
        v.tensor_tensor(gap, m2, m1, ALU.subtract).then_inc(c.shift_done, 1)
        v.wait_ge(c.exp_done, self.router.n)
        own.link(v, v.tensor_scalar(w1, gap, 1.0, None, ALU.add))
        own.link(v, v.reciprocal(w1, w1))
        own.link(v, v.tensor_tensor(w2, gap, w1, ALU.mult))
        own.link(v, v.tensor_tensor(one, one, bc(w1[:, :, None], (P, NT, E)), ALU.mult))
        own.link(v, v.tensor_tensor(two, two, bc(w2[:, :, None], (P, NT, E)), ALU.mult))
        own.link(v, v.tensor_tensor(one, one, two, ALU.add))
        v.tensor_scalar(one, one, c.gates[:, 4:5], None, ALU.mult).then_inc(s["weights"], 1)
        v.wait_ge(s["weights"], 1)
        self.bias_sum.dve(v, c.X, s["added"])

        def multiply(n):
            e = n // NG
            for k in range(2):
                v.wait_ge(s["second_copied"], 2 * n + k + 1)
                if n >= 2:
                    v.wait_ge(s["third"], n - 1)
                v.scalar_tensor_tensor(self.z[:, n % 2, k, :], c.bank[k][:, :],
                                       self.bias[:, 0, 2 * e + k:2 * e + k + 1], self.x2[:, n % 2, k, :],
                                       ALU.add, ALU.mult).then_inc(s["z"], 1)

        def add(n):
            e, q = n // NG, n % NG
            v.wait_ge(s["result"], n + 1)
            v.wait_ge(s["added"], NG + max(GROUP * (n - NG + 1), 0))
            for i in range(GROUP):
                j = GROUP * q + i
                v.scalar_tensor_tensor(c.X[:, j, :], c.bank[6 + n % 2][:, i * D:(i + 1) * D],
                                       one[:, j, e:e + 1], c.X[:, j, :], ALU.mult, ALU.add) \
                    .then_inc(s["added"], 1)

        for n in range(E * NG):
            multiply(n)
            if n:
                add(n - 1)
        add(E * NG - 1)

    def pool(self, g):
        self.norm.pool(g)

    def act(self, a):
        c, s = self.c, self.s
        self.norm.act(a)
        self.router.act(a, c.routing.rows(3))
        self.bias_sum.act(a)
        self.load.wait(a)

        def copy_second(n):
            e = n // NG
            if n >= 2:
                a.wait_ge(s["z"], 2 * (n - 1))
            for k in range(2):
                a.wait_ge(s["second"], 2 * n + k + 1)
                a.activation(self.x2[:, n % 2, k, :], c.bank[2 + k][:, :], ACT.Identity,
                             bias=self.bias[:, 1, 2 * e + k:2 * e + k + 1]).then_inc(s["second_copied"], 1)

        def silu(n):
            e = n // NG
            if n >= 2:
                a.wait_ge(s["result"], n - 1)
            a.wait_ge(s["third"], n + 1)
            for k in range(2):
                a.activation(self.act_out[:, n % 2, k, :], c.bank[4 + k][:, :], ACT.Silu,
                             bias=self.bias[:, 2, 2 * e + k:2 * e + k + 1]).then_inc(s["silu"], 1)

        for n in range(E * NG):
            copy_second(n)
            silu(n)

    def pe(self, t):
        c, s = self.c, self.s
        self.norm.pe(t)
        self.load.wait(t)
        self.norm.turn.wait(t, NG)
        self.router.pe(t, self.gate_w[:])
        t.wait_ge(s["weights"], 1)
        self.bias_sum.pe(t)

        def project(n):
            e, x = n // NG, c.XT[:, (n % NG) * CHUNK:(n % NG + 1) * CHUNK]
            if n % (2 * NG) == 0:
                self.expert_load[e // 2].wait(t)
            if n == 0:
                t.wait_ge(s["added"], NG)
            else:
                t.wait_ge(s["z"], 2 * n)
            for k in range(2):
                t.matmul(c.bank[k][:, :], self.w1[:, e, k * P:(k + 1) * P], x, start=True, stop=True)
                t.matmul(c.bank[2 + k][:, :], self.w2[:, e, k * P:(k + 1) * P], x, start=True, stop=True) \
                    .then_inc(s["second"], 1)

        def third(n):
            e = n // NG
            t.wait_ge(s["z"], 2 * n + 2)
            if n:
                t.wait_ge(s["silu"], 2 * n)
            for k in range(2):
                for q in range(2):
                    last = t.matmul(c.bank[4 + k][:, :], self.wg[:, e, q, k * P:(k + 1) * P],
                                    self.z[:, n % 2, q, :], start=(q == 0), stop=(q == 1))
            last.then_inc(s["third"], 1)

        def last_product(n):
            e = n // NG
            t.wait_ge(s["silu"], 2 * n + 2)
            if n >= 2:
                t.wait_ge(s["added"], NG + GROUP * (n - 1))
            for i in range(GROUP):
                for k in range(2):
                    last = t.matmul(c.bank[6 + n % 2][:, i * D:(i + 1) * D],
                                    self.act_out[:, n % 2, k, i * P:(i + 1) * P], self.w3[:, e, k, :],
                                    start=(k == 0), stop=(k == 1))
            last.then_inc(s["result"], 1)

        project(0)
        for n in range(E * NG):
            third(n)
            if n + 1 < E * NG:
                project(n + 1)
            last_product(n)


class HeadsStage:

    H, DH = 16, 8
    SCALE = 8 ** -0.5
    KEYS = S + SC
    VW = 168

    def __init__(self, c, after):
        self.c, self.after, self.all_added = c, after, NT
        sc, d = c.scratch(), c.d
        self.norm = Norm(c, c.X, c.XN, 1.0, EPS, c.XT)
        self.Wqkv = c.sb("c_Wqkv", [P, 3 * D])
        self.Wproj = c.sb("c_Wproj", [P, D])
        self.b_proj = c.sb("c_b_proj", [1, D])
        self.load = (Load(c, "c").add(self.Wqkv[:], d["L1_xattn_w_qkv"]).add(self.Wproj[:], d["L1_xattn_w_proj"])
                     .add(self.b_proj[:], d["L1_xattn_b_proj"][None, :]))
        self.Q = sc.take(512).rearrange("p (i h c) -> p i h c", i=2, h=16)
        self.K = sc.take(512).rearrange("p (i h c) -> p i h c", i=2, h=16)
        self.KC = sc.take(256)[0:64, :].rearrange("p (h c) -> p h c", h=16)
        self.V = sc.take(4 * self.VW).rearrange("p (u i n) -> p u i n", u=2, i=2)
        self.VC = sc.take(2 * self.VW).rearrange("p (u n) -> p u n", u=2)
        self.QT = sc.take(512).rearrange("p (g t) -> p g t", g=2)
        self.KM = sc.take(16 * self.KEYS).rearrange("p (h t) -> p h t", h=16)
        more = sc.take(4 * 512)
        spare = c.XN[:, :, :].rearrange("p j n -> p (j n)")
        self.prob = [(spare if u < 4 else more)[:, (u % 4) * 512:(u % 4 + 1) * 512] for u in range(8)]
        self.prob_c = sc.take(2 * 512).rearrange("p (u n) -> p u n", u=2)
        self.rz = sc.take(16)
        self.AT = sc.take(512)
        self.O = sc.take(256).rearrange("p (i n) -> p i n", i=2)
        self.OT = sc.take(256)
        self.s = c.signals("c", "ones_set values keys_c zeroed qkv split q_t k_t q_turned masked scores maxed "
                                "st exp st_c exp_c av evac parts heads o_t o_turned product added")

    def v_rows(self, u, i):
        return self.V[:, u, i, 0:144].rearrange("p (h c) -> p h c", c=9)

    def vc_rows(self, half, u):
        return self.VC[64 * half:64 * half + 64, u, 0:144].rearrange("p (k a c) -> p k a c", a=2, c=9)[:, :, half, :]

    def pool(self, g):
        c, s = self.c, self.s
        self.norm.pool(g)
        c.c2_load.wait(g)
        own = c.pool_chain
        for t in (self.Q, self.K, self.KC, self.VC):
            own.link(g, g.memset(t, 0.0))
        own.link(g, g.memset(self.K[:, :, :, 8], 1.0))
        own.link(g, g.memset(self.KC[:, :, 8], 1.0))
        for u in range(2):
            for half in range(2):
                own.link(g, g.memset(self.vc_rows(half, u)[:, :, 8], 1.0))
        g.memset(self.V, 1.0).then_inc(s["ones_set"], 1)
        g.wait_ge(s["ones_set"], 1)
        for b in range(B):
            if b:
                g.wait_ge(s["q_t"], 3 * b)
                g.memset(self.Q[:, :, :, 8], 0.0).then_inc(s["zeroed"], 1)
                g.wait_ge(s["zeroed"], b)
                g.wait_ge(s["k_t"], 2 * b)
            g.tensor_copy(self.KC[:, :, 0:8], c.C2[0:64, b, 0:D].rearrange("p (h c) -> p h c", c=8)) \
                .then_inc(s["keys_c"], 1)
            g.wait_ge(s["keys_c"], b + 1)
            if b >= 2:
                g.wait_ge(s["av"], 4 * (b - 1))
            for half in range(2):
                rows = c.C2[64 * half:64 * half + 64, b, D:2 * D].rearrange("p (k a c) -> p k a c", a=2, c=8)
                g.tensor_copy(self.vc_rows(half, b % 2)[:, :, 0:8], rows[:, :, half, :]).then_inc(s["values"], 1)
                g.wait_ge(s["values"], 2 * b + half + 1)

    def pe(self, t):
        c, s = self.c, self.s
        self.norm.pe(t)
        self.load.wait(t)
        bank = c.bank

        def project(b):
            self.norm.turn.wait(t, b // 2 + 1)
            if b:
                t.wait_ge(s["exp_c"], 4 * b)
            for i in range(2):
                j = 2 * b + i
                t.matmul(bank[i][:, 0:3 * D], c.XT[:, j * P:(j + 1) * P], self.Wqkv[:], start=True,
                         stop=True).then_inc(s["qkv"], 1)

        def turn_queries(b, g, out):
            for i in range(2):
                last = t.transpose(out[:, i * P:(i + 1) * P],
                                   self.Q[:, i, 8 * g:8 * g + 8, :].rearrange("p h c -> p (h c)"), c.ident[:])
            return last

        def turn_rows(b):
            t.wait_ge(s["split"], 6 * b + 6)
            if b:
                t.wait_ge(s["zeroed"], b)
                t.wait_ge(s["exp"], 16 * b)
            t.wait_ge(s["keys_c"], b + 1)
            turn_queries(b, 0, bank[2][:, 0:S])
            turn_queries(b, 1, bank[2][:, S:2 * S]).then_inc(s["q_t"], 1)
            for g in range(2):
                for i in range(2):
                    t.transpose(bank[g][:, i * P:(i + 1) * P],
                                self.K[:, i, 8 * g:8 * g + 8, :].rearrange("p h c -> p (h c)"), c.ident[:])
                t.transpose(bank[g][:, S:S + SC], self.KC[:, 8 * g:8 * g + 8, :].rearrange("p h c -> p (h c)"),
                            c.ident[0:64, 0:64]).then_inc(s["k_t"], 1)

        def scores(b, n):
            g, pair, i = n // 8, (n % 8) // 2, n % 2
            h = 8 * g + 2 * pair
            if n == 0:
                t.wait_ge(s["q_turned"], 3 * b + 1)
            if i == 0:
                t.wait_ge(s["masked"], 16 * b + h + 2)
            if n >= 2:
                t.wait_ge(s["maxed"], 16 * b + n - 1)
            for q in range(2):
                last = t.matmul(bank[2 + 2 * (n % 2) + q][:, 0:self.KEYS], self.QT[:, g, i * P:(i + 1) * P],
                                self.KM[:, h + q, :], start=True, stop=True)
            last.then_inc(s["scores"], 1)

        def turn_again(b, g):
            t.wait_ge(s["maxed"], 16 * b + 8 * g + 8)
            if g == 0:
                t.wait_ge(s["masked"], 16 * b + 16)
            turn_queries(b, g, bank[g][:, 0:S]).then_inc(s["q_t"], 1)

        def key_major_context(b, j):
            n = 4 * b + j
            if j >= 2:
                t.wait_ge(s["exp_c"], n - 1)
            else:
                t.wait_ge(s["q_turned"], 3 * b + 3)
            for r in range(4):
                half = slice(64 * (r % 2), 64 * (r % 2) + 64)
                last = t.matmul(bank[j % 2][half, (r // 2) * S:(r // 2 + 1) * S],
                                self.KM[:, 4 * j + r, S:S + SC], self.QT[:, j // 2, :], start=True, stop=True)
            last.then_inc(s["st_c"], 1)

        def key_major(b, h):
            n, g = 16 * b + h, h // 8
            t.wait_ge(s["q_turned"], 3 * b + 2 + g)
            if h >= 4:
                t.wait_ge(s["exp"], n - 3)
            else:
                t.wait_ge(s["maxed"], 16 * b + 16)
            for k in range(2):
                last = t.matmul(bank[2 + h % 4][:, k * S:(k + 1) * S], self.KM[:, h, k * P:(k + 1) * P],
                                self.QT[:, g, :], start=True, stop=True)
            last.then_inc(s["st"], 1)

        def values(b, j):
            if j == 0:
                if b:
                    t.wait_ge(s["added"], 2 * b)
                t.wait_ge(s["values"], 2 * b + 2)
            t.wait_ge(s["exp_c"], 4 * b + j + 1)
            t.wait_ge(s["exp"], 16 * b + 4 * j + 4)
            for k in range(3):
                for r in range(4):
                    h = 4 * j + r
                    wide = slice(9 * h, 9 * h + 32)
                    out = bank[6 + j // 2][32 * r:32 * r + 32, (j % 2) * S:(j % 2 + 1) * S]
                    if k < 2:
                        t.matmul(out, self.V[:, b % 2, k, wide], self.prob[h % 8][:, k * S:(k + 1) * S],
                                 start=(k == 0), stop=False, tile_position=(0, 32 * r))
                    else:
                        last = t.matmul(out, self.VC[:, b % 2, wide],
                                        self.prob_c[:, j % 2, (r // 2) * S:(r // 2 + 1) * S],
                                        start=False, stop=True, tile_position=(0, 32 * r))
            last.then_inc(s["av"], 1)

        def turn_parts(b, half):
            t.wait_ge(s["evac"], 2 * b + half + 1)
            for n in range(4):
                last = t.transpose(bank[6 + half][:, n * P:(n + 1) * P], self.AT[:, n * P:(n + 1) * P], c.ident[:])
            last.then_inc(s["parts"], 1)

        def turn_out(b):
            t.wait_ge(s["heads"], 4 * b + 4)
            for i in range(2):
                last = t.transpose(bank[6][:, i * P:(i + 1) * P], self.O[:, i, :], c.ident[:])
            last.then_inc(s["o_t"], 1)

        def project_out(b):
            t.wait_ge(s["o_turned"], b + 1)
            for i in range(2):
                out = bank[6][:, S + i * P:S + (i + 1) * P]
                t.matmul(out, self.OT[:, i * P:(i + 1) * P], self.Wproj[:], start=True, stop=False)
                last = t.matmul(out, c.ones[0:1, :], self.b_proj[0:1, :], start=False, stop=True)
            last.then_inc(s["product"], 1)

        t.wait_ge(s["ones_set"], 1)
        project(0)
        for b in range(B):
            turn_rows(b)
            for n in range(16):
                scores(b, n)
                if b and n == 0:
                    turn_parts(b - 1, 1)
                if b and n == 4:
                    turn_out(b - 1)
                if b and n == 6:
                    project_out(b - 1)
                if n == 11:
                    turn_again(b, 0)
            for h in range(4):
                key_major(b, h)
                if h == 1:
                    turn_again(b, 1)
            key_major_context(b, 0)
            for j in range(1, 4):
                for h in range(4 * j, 4 * j + 4):
                    key_major(b, h)
                key_major_context(b, j)
                values(b, j - 1)
            if b + 1 < B:
                project(b + 1)
            turn_parts(b, 0)
            values(b, 3)
        turn_parts(B - 1, 1)
        turn_out(B - 1)
        project_out(B - 1)

    def act(self, a):
        c, s = self.c, self.s
        self.norm.act(a)
        bank = c.bank
        a.wait_ge(s["ones_set"], 1)

        def split(b):
            for i in range(2):
                a.wait_ge(s["qkv"], 2 * b + i + 1)
                rows = [bank[i][:, k * D:(k + 1) * D].rearrange("p (h c) -> p h c", c=8) for k in range(3)]
                a.activation(self.Q[:, i, :, 0:8], rows[0], ACT.Copy, scale=self.SCALE).then_inc(s["split"], 1)
                a.activation(self.K[:, i, :, 0:8], rows[1], ACT.Copy).then_inc(s["split"], 1)
                a.activation(self.v_rows(b % 2, i)[:, :, 0:8], rows[2], ACT.Copy).then_inc(s["split"], 1)

        def mask(b, h):
            g = h // 8
            if h % 8 == 0:
                a.wait_ge(s["k_t"], 2 * b + g + 1)
            a.activation(self.KM[:, h, :], bank[g][:, 0:self.KEYS], ACT.Copy, scale=c.head16[:, h % 8:h % 8 + 1]) \
                .then_inc(s["masked"], 1)

        def copy_out(b):
            a.wait_ge(s["o_t"], b + 1)
            a.activation(self.OT, bank[6][:, 0:S], ACT.Copy).then_inc(s["o_turned"], 1)

        def exp_context(b, j):
            n = 4 * b + j
            a.wait_ge(s["st_c"], n + 1)
            if n >= 2:
                a.wait_ge(s["av"], n - 1)
            a.activation(self.prob_c[:, n % 2, :], bank[j % 2][:, :], ACT.Exp).then_inc(s["exp_c"], 1)

        def exp_own(b, h):
            n = 16 * b + h
            a.wait_ge(s["st"], n + 1)
            if n >= 8:
                a.wait_ge(s["av"], n // 4 - 1)
            a.activation(self.prob[h % 8], bank[2 + h % 4][:, :], ACT.Exp).then_inc(s["exp"], 1)

        for b in range(B):
            split(b)
            for h in range(16):
                mask(b, h)
                if b and h == 13:
                    copy_out(b - 1)
            for h in range(16):
                exp_own(b, h)
                if h % 4 == 3:
                    exp_context(b, h // 4)
        copy_out(B - 1)

    def dve(self, v):
        c, s = self.c, self.s
        self.norm.dve(v, self.after)
        bank = c.bank

        def copy_queries(b):
            v.wait_ge(s["q_t"], 3 * b + 1)
            v.tensor_copy(self.QT[:, :, :].rearrange("p g t -> p (g t)"), bank[2][:, :]).then_inc(s["q_turned"], 1)

        def copy_again(b, g):
            v.wait_ge(s["q_t"], 3 * b + 2 + g)
            v.tensor_copy(self.QT[:, g, :], bank[g][:, 0:S]).then_inc(s["q_turned"], 1)

        def maxima(b, n):
            g, pair, i = n // 8, (n % 8) // 2, n % 2
            k, h = 2 + 2 * (n % 2), 8 * g + 2 * pair
            v.wait_ge(s["scores"], 16 * b + n + 1)
            v.tensor_reduce(self.Q[:, i, h:h + 2, 8], c.psum[:, k:k + 2, 0:self.KEYS], AX.X, ALU.max,
                            negate=True).then_inc(s["maxed"], 1)

        def take_parts(b, half):
            v.wait_ge(s["parts"], 2 * b + half + 1)
            turned = bank[6 + half]
            c.dve_chain.link(v, v.reciprocal(self.rz, turned.rearrange("p (n k) -> p n k", k=32)[:, :, 8]))
            if b and half == 0:
                v.wait_ge(s["o_t"], b)
            for j in range(2):
                parts = turned[:, j * S:(j + 1) * S].rearrange("p (i r k) -> p i r k", i=2, r=4)
                at = 64 * half + 32 * j
                rz = self.rz[:, 8 * j:8 * j + 8].rearrange("p (i r) -> p i r", i=2)
                v.tensor_tensor(self.O[:, :, at:at + 32].rearrange("p i (r k) -> p i r k", r=4), parts[:, :, :, 0:8],
                                bc(rz[:, :, :, None], (P, 2, 4, 8)), ALU.mult).then_inc(s["heads"], 1)

        def evacuate(b, half):
            v.wait_ge(s["av"], 4 * b + 2 * half + 2)
            if b or half:
                v.wait_ge(s["parts"], 2 * b + half)
            v.tensor_copy(self.AT, bank[6 + half][:, :]).then_inc(s["evac"], 1)

        def add(b):
            v.wait_ge(s["product"], b + 1)
            for i in range(2):
                j = 2 * b + i
                v.scalar_tensor_tensor(c.X[:, j, :], bank[6][:, S + i * P:S + (i + 1) * P],
                                       c.gates[:, 1:2], c.X[:, j, :], ALU.mult, ALU.add).then_inc(s["added"], 1)

        for b in range(B):
            copy_queries(b)
            if b:
                evacuate(b - 1, 1)
            for n in range(16):
                maxima(b, n)
                if b and n == 1:
                    take_parts(b - 1, 1)
                if n == 12:
                    copy_again(b, 0)
                if b and n == 7:
                    add(b - 1)
            copy_again(b, 1)
            evacuate(b, 0)
            take_parts(b, 0)
        evacuate(B - 1, 1)
        take_parts(B - 1, 1)
        add(B - 1)


class AcrossStage:

    HEADS, DH, T = 16, 8, 8
    SCALE = 8 ** -0.5

    def __init__(self, c, after):
        self.c, self.after, self.all_added = c, after, NG
        sc, d = c.scratch(), c.d
        self.norm = Norm(c, c.X, c.XN, 1.0, EPS, c.XT)
        self.Win = c.sb("d_Win", [P, 3 * D])
        self.Wout = c.sb("d_Wout", [P, D])
        self.b_in = c.sb("d_b_in", [1, 3 * D])
        self.b_out = c.sb("d_b_out", [1, D])
        self.affine = c.sb("d_affine", [P, 4, D])
        self.router_w = c.sb("d_router_w", [P, E])
        self.router_b = c.sb("d_router_b", [P, E])
        self.b1 = c.sb("d_b1", [P, E])
        self.b2 = c.sb("d_b2", [E, D])
        self.w1 = c.late[:, 0:1024].rearrange("p (e n) -> p e n", e=E)
        self.w2 = c.late[:, 1024:2048].rearrange("p (e n) -> p e n", e=E)
        self.load = (Load(c, "d").add(self.Win[:], d["L1_ffn_in_proj_w"]).add(self.Wout[:], d["L1_ffn_out_w"])
                     .add(self.b_in[:], d["L1_ffn_in_proj_b"][None, :]).add(self.b_out[:], d["L1_ffn_out_b"][None, :])
                     .add(self.affine[:, 0, :], d["L1_ffn_ln1_g"].partition_broadcast(P))
                     .add(self.affine[:, 1, :], d["L1_ffn_ln1_b"].partition_broadcast(P))
                     .add(self.affine[:, 2, :], d["L1_ffn_ln2_g"].partition_broadcast(P))
                     .add(self.affine[:, 3, :], d["L1_ffn_ln2_b"].partition_broadcast(P))
                     .add(self.router_w[:], d["L1_ffn_router_w"])
                     .add(self.router_b[:], d["L1_ffn_router_b"].partition_broadcast(P))
                     .add(self.b1[:], d["L1_ffn_b1"]).add(self.b2[:], d["L1_ffn_b2"])
                     .add(self.w1, d["L1_ffn_w1"]).add(self.w2, d["L1_ffn_w2"]))
        self.qkv = sc.take(8 * 384).rearrange("p (t n) -> p t n", t=8)
        self.prod = sc.take(4 * 1024).rearrange("p (u n) -> p u n", u=4)
        self.score = sc.take(1024).rearrange("p (t s h) -> p t s h", t=8, s=8)
        self.top = sc.take(128).rearrange("p (t h) -> p t h", t=8)
        self.mixed = sc.take(NT * D).rearrange("p (j d) -> p j d", j=NT)
        sc2 = c.scratch()
        self.hidden = sc2.take(2 * 512).rearrange("p (u n) -> p u n", u=2)
        self.pickT = sc2.take(NT * P)[0:E, :]
        self.own = c.dve_chain
        self.s = c.signals("d", "qkv qkv_copied prod scored shifted exp attn prod_v summed out residual "
                                "h_norm h_affine pick "
                                "hidden gelu result moe moe_affine added")
        self.out_turn = Turn(c, self.mixed, c.XT, self.s["summed"], 2, 8)
        self.ln1 = Norm(c, c.XN, c.XN)
        self.h_turn = Turn(c, c.XN, c.XT, self.s["h_affine"], 1)
        self.router = Router(c)
        self.bias_sum = ExpertBias(c, c.routing.table(2), self.pickT, self.b2[:])
        self.ln2 = Norm(c, c.XN, c.XN)

    def products(self, eng, m, t, kind):
        s = self.s
        n = 8 * m + t
        if kind == "scores":
            done, used = s["prod"], s["scored"]
            if n >= 2:
                eng.wait_ge(used, n - 1)
            q = bc(self.qkv[:, t, 0:D][:, None, :], (P, 8, D))
            eng.tensor_tensor(self.prod[:, n % 2, :].rearrange("p (s n) -> p s n", s=8), q,
                              self.qkv[:, :, D:2 * D], ALU.mult).then_inc(done, 1)
        else:
            if n >= 2:
                eng.wait_ge(s["summed"], n - 1)
            w = bc(self.score[:, t, :, :][:, :, :, None], (P, 8, 16, 8))
            eng.tensor_tensor(self.prod[:, 2 + n % 2, :].rearrange("p (s h c) -> p s h c", s=8, c=8), w,
                              self.qkv[:, :, 2 * D:3 * D].rearrange("p s (h c) -> p s h c", c=8),
                              ALU.mult).then_inc(s["prod_v"], 1)

    def pool(self, g):
        c, s = self.c, self.s
        self.norm.pool(g)
        for m in range(2):
            g.wait_ge(s["qkv_copied"], 16 * m + 16)
            for t in range(8):
                self.products(g, m, t, "scores")
            g.wait_ge(s["attn"], m + 1)
            for t in range(8):
                self.products(g, m, t, "values")
        self.ln1.pool(g)
        self.ln2.pool(g)

    def dve(self, v):
        c, s, own, r = self.c, self.s, self.own, self.c.routing
        self.norm.dve(v, self.after)
        for m in range(2):
            for t in range(8):
                n = 8 * m + t
                v.wait_ge(s["prod"], n + 1)
                if m and t == 0:
                    v.wait_ge(s["prod_v"], 8)
                v.tensor_reduce(self.score[:, t, :, :].rearrange("p s h -> p (s h)"),
                                self.prod[:, n % 2, :].rearrange("p (n c) -> p n c", c=8), AX.X, ALU.add) \
                    .then_inc(s["scored"], 1)
            v.wait_ge(s["scored"], 8 * m + 8)
            over_s = self.score[:, :, :, :].rearrange("p t s h -> p t h s")
            spread = bc(self.top[:, :, None, :], (P, 8, 8, 16))
            own.link(v, v.tensor_reduce(self.top, over_s, AX.X, ALU.max))
            v.tensor_tensor(self.score, self.score, spread, ALU.subtract).then_inc(s["shifted"], 1)
            v.wait_ge(s["exp"], m + 1)
            own.link(v, v.tensor_reduce(self.top, over_s, AX.X, ALU.add))
            own.link(v, v.reciprocal(self.top, self.top))
            v.tensor_tensor(self.score, self.score, spread, ALU.mult).then_inc(s["attn"], 1)
            for t in range(8):
                n = 8 * m + t
                v.wait_ge(s["prod_v"], n + 1)
                v.tensor_reduce(self.mixed[:, 2 * t + m, :],
                                self.prod[:, 2 + n % 2, :].rearrange("p (s n) -> p n s", s=8), AX.X, ALU.add) \
                    .then_inc(s["summed"], 1)
        for j in range(NT):
            v.wait_ge(s["out"], j + 1)
            v.tensor_tensor(c.XN[:, j, :], c.XN[:, j, :], c.bank[j % 4][:, 0:D], ALU.add) \
                .then_inc(s["residual"], 1)
        self.ln1.dve(v, s["residual"])
        self.scale_shift(v, self.ln1, 0, s["h_affine"])

        products = self.router.logits(v)
        logits, left, one, two = (r.table(k) for k in range(4))
        m1, m2, i1, i2 = (r.rows(k) for k in range(4))
        shape = (P, NT, E)
        own.link(v, v.tensor_tensor(logits, products, bc(self.router_b[:, None, :], shape), ALU.add))
        self.router.softmax(v, logits, logits, m1)
        r.first(v, own, logits, m1, one, i1)
        r.hide(v, own, logits, one, left)
        r.first(v, own, left, m2, two, i2)
        own.link(v, v.tensor_tensor(i1, i1, i2, ALU.max))
        v.tensor_tensor(one, bc(c.expert_m8[:, None, :], shape), bc(i1[:, :, None], shape), ALU.is_equal) \
            .then_inc(s["pick"], 1)
        v.wait_ge(s["pick"], 1)
        self.bias_sum.dve(v, c.XN, s["moe"])
        for n in range(E * NG):
            e, q = n // NG, n % NG
            v.wait_ge(s["result"], n + 1)
            v.wait_ge(s["moe"], NG + max(GROUP * (n - NG + 1), 0))
            for i in range(GROUP):
                j = GROUP * q + i
                v.scalar_tensor_tensor(c.XN[:, j, :], c.bank[2 + n % 2][:, i * D:(i + 1) * D],
                                       one[:, j, e:e + 1], c.XN[:, j, :], ALU.mult, ALU.add) \
                    .then_inc(s["moe"], 1)
        v.wait_ge(s["moe"], NG + E * NT)
        self.ln2.dve(v)
        self.scale_shift(v, self.ln2, 2, s["moe_affine"])
        for q in range(NG):
            v.wait_ge(s["moe_affine"], q + 1)
            tiles = slice(GROUP * q, GROUP * q + GROUP)
            v.scalar_tensor_tensor(c.X[:, tiles, :], c.XN[:, tiles, :], c.gates[:, 5:6], c.X[:, tiles, :],
                                   ALU.mult, ALU.add).then_inc(s["added"], 1)

    def scale_shift(self, v, norm, k, done):
        c = self.c
        for q in range(NG):
            tiles = c.XN[:, GROUP * q:GROUP * q + GROUP, :]
            norm.wait_normed(v, GROUP * q + GROUP)
            self.own.link(v, v.tensor_tensor(tiles, tiles, bc(self.affine[:, k, :][:, None, :], (P, GROUP, D)),
                                             ALU.mult))
            v.tensor_tensor(tiles, tiles, bc(self.affine[:, k + 1, :][:, None, :], (P, GROUP, D)),
                            ALU.add).then_inc(done, 1)

    def act(self, a):
        c, s = self.c, self.s
        self.norm.act(a)
        for m in range(2):
            if m:
                a.wait_ge(s["scored"], 8)
                a.wait_ge(s["prod_v"], 8)
            for t in range(8):
                n = 8 * m + t
                a.wait_ge(s["qkv"], n + 1)
                a.activation(self.qkv[:, t, 0:D], c.bank[n % 4][:, 0:D], ACT.Copy, scale=self.SCALE) \
                    .then_inc(s["qkv_copied"], 1)
                a.activation(self.qkv[:, t, D:3 * D], c.bank[n % 4][:, D:3 * D], ACT.Copy) \
                    .then_inc(s["qkv_copied"], 1)
            a.wait_ge(s["shifted"], m + 1)
            a.activation(self.score, self.score, ACT.Exp).then_inc(s["exp"], 1)
        self.out_turn.act(a)
        self.h_turn.act(a)
        self.router.act(a, c.routing.table(0))
        self.bias_sum.act(a)
        for n in range(E * NG):
            if n >= 2:
                a.wait_ge(s["result"], n - 1)
            a.wait_ge(s["hidden"], n + 1)
            a.activation(self.hidden[:, n % 2, :], c.bank[4 + n % 2][:, :], ACT.Gelu,
                         bias=self.b1[:, n // NG:n // NG + 1]).then_inc(s["gelu"], 1)

    def pe(self, t):
        c, s = self.c, self.s
        self.norm.pe(t)
        self.load.wait(t)
        self.norm.turn.wait(t, NG)
        for n in range(NT):
            j = 2 * (n % 8) + n // 8
            if n >= 4:
                t.wait_ge(s["qkv_copied"], 2 * (n - 3))
            out = c.bank[n % 4][:, 0:3 * D]
            t.matmul(out, c.XT[:, j * P:(j + 1) * P], self.Win[:], start=True, stop=False)
            t.matmul(out, c.ones[0:1, :], self.b_in[0:1, :], start=False, stop=True).then_inc(s["qkv"], 1)
        self.out_turn.pe(t)
        for j in range(NT):
            self.out_turn.wait(t, j // GROUP + 1)
            if j >= 4:
                t.wait_ge(s["residual"], j - 3)
            out = c.bank[j % 4][:, 0:D]
            t.matmul(out, c.XT[:, j * P:(j + 1) * P], self.Wout[:], start=True, stop=False)
            t.matmul(out, c.ones[0:1, :], self.b_out[0:1, :], start=False, stop=True).then_inc(s["out"], 1)
        self.h_turn.pe(t)
        self.h_turn.wait(t, NG)
        self.router.pe(t, self.router_w[:])
        t.wait_ge(s["pick"], 1)
        self.bias_sum.pe(t)

        def first(n):
            e, x = n // NG, c.XT[:, (n % NG) * CHUNK:(n % NG + 1) * CHUNK]
            if n >= 2:
                t.wait_ge(s["gelu"], n - 1)
            t.matmul(c.bank[4 + n % 2][:, :], self.w1[:, e, :], x, start=True, stop=True) \
                .then_inc(s["hidden"], 1)

        def second(n):
            e = n // NG
            t.wait_ge(s["gelu"], n + 1)
            t.wait_ge(s["moe"], NG + GROUP * max(n - 1, 0))
            for i in range(GROUP):
                last = t.matmul(c.bank[2 + n % 2][:, i * D:(i + 1) * D],
                                self.hidden[:, n % 2, i * P:(i + 1) * P], self.w2[:, e, :],
                                start=True, stop=True)
            last.then_inc(s["result"], 1)

        first(0)
        for n in range(E * NG):
            if n + 1 < E * NG:
                first(n + 1)
            second(n)


class MaskedStage:

    H, DH = 8, 16
    SCALE = 16 ** -0.5

    def __init__(self, c, after):
        self.c, self.after, self.all_added = c, after, NT
        sc, d = c.scratch(), c.d
        self.norm = Norm(c, c.X, c.XN, 1.0, EPS, c.XT)
        self.shift = c.sb("e_shift", [P, 1])
        self.mask_in = c.sb("e_mask_in", [P, B * SC], I32)
        self.load = (Load(c, "e").add(self.shift[:], d["L2_xattn_b"].partition_broadcast(P))
                     .add(self.mask_in[:], d["seq_mask"].partition_broadcast(P))
                     .add(c.CT[:], d["ctx_T"]))
        self.keys = sc.take(B * 512).rearrange("p (b h k) -> p b h k", b=B, h=8)
        self.vals = sc.take(B * 136).rearrange("p (b h n) -> p b h n", b=B, h=8)
        self.mask = sc.take(B * SC)
        self.prob = sc.take(2 * 512).rearrange("p (u n) -> p u n", u=2)
        self.probT = sc.take(2 * 512).rearrange("p (u n) -> p u n", u=2)
        self.top = sc.take(2 * 8).rearrange("p (u h) -> p u h", u=2)
        self.rz = sc.take(8)
        self.part = sc.take(D)
        self.head = sc.take(8)
        self.own, self.own_pool = c.dve_chain, c.pool_chain
        self.s = c.signals("e", "operands scores biased topped shifted exp p_t p_turned av rz added")

    def pool(self, g):
        c, s, own = self.c, self.s, self.own_pool
        self.norm.pool(g)
        self.load.wait(g)
        c.c2_load.wait(g)
        own.link(g, g.tensor_scalar(self.head, c.head16[:], self.SCALE, None, ALU.mult))
        own.link(g, g.tensor_copy(self.mask, self.mask_in[:]))
        own.link(g, g.tensor_scalar(self.mask, self.mask, -1.0, 1.0e30, ALU.add, ALU.mult))
        for b in range(B):
            own.link(g, g.tensor_tensor(self.keys[:, b, :, :], bc(c.CT[:, 0, b * SC:(b + 1) * SC][:, None, :], (P, 8, SC)),
                                        bc(self.head[:, :, None], (P, 8, SC)), ALU.mult))
            own.link(g, g.tensor_tensor(self.vals[:, b, :, 0:16],
                                        c.C2[:, b, D:2 * D].rearrange("p (h n) -> p h n", h=8),
                                        bc(c.parity[:, :, None], (P, 8, 16)), ALU.mult))
            g.tensor_copy(self.vals[:, b, :, 16], c.parity[:]).then_inc(s["operands"], 1)

    def dve(self, v):
        c, s, own = self.c, self.s, self.own
        self.norm.dve(v, self.after)
        v.wait_ge(s["operands"], B)
        self.load.wait(v)

        def softmax(j):
            u, b = j % 2, j // 2
            tile = self.prob[:, u, :].rearrange("p (h k) -> p h k", h=8)
            v.wait_ge(s["scores"], j + 1)
            if j >= 2:
                v.wait_ge(s["p_t"], j - 1)
            v.scalar_tensor_tensor(tile, c.bank[u][:, :].rearrange("p (h k) -> p h k", h=8), self.shift[:, 0:1],
                                   bc(self.mask[:, b * SC:(b + 1) * SC][:, None, :], (P, 8, SC)),
                                   ALU.add, ALU.add).then_inc(s["biased"], 1)
            v.wait_ge(s["biased"], j + 1)
            v.tensor_reduce(self.top[:, u, :], tile, AX.X, ALU.max).then_inc(s["topped"], 1)
            v.wait_ge(s["topped"], j + 1)
            v.tensor_tensor(tile, tile, bc(self.top[:, u, :][:, :, None], (P, 8, SC)), ALU.subtract) \
                .then_inc(s["shifted"], 1)

        def finish(j):
            v.wait_ge(s["av"], j + 1)
            av = c.bank[4 + j % 2][:, 0:136].rearrange("p (h n) -> p h n", h=8)
            own.link(v, v.reciprocal(self.rz, av[:, :, 16]))
            own.link(v, v.tensor_scalar(self.rz, self.rz, c.gates[:, 2:3], None, ALU.mult))
            own.link(v, v.tensor_tensor(self.part.rearrange("p (h n) -> p h n", h=8), av[:, :, 0:16],
                                        bc(self.rz[:, :, None], (P, 8, 16)), ALU.mult))
            v.tensor_tensor(c.X[:, j, :], c.X[:, j, :], self.part, ALU.add).then_inc(s["added"], 1)

        for j in range(NT):
            softmax(j)
            if j:
                finish(j - 1)
        finish(NT - 1)

    def act(self, a):
        c, s = self.c, self.s
        self.norm.act(a)
        for j in range(NT):
            u = j % 2
            a.wait_ge(s["shifted"], j + 1)
            a.activation(self.prob[:, u, :], self.prob[:, u, :], ACT.Exp).then_inc(s["exp"], 1)
            a.wait_ge(s["p_t"], j + 1)
            if j >= 2:
                a.wait_ge(s["av"], j - 1)
            a.activation(self.probT[:, u, :], c.bank[2 + u][:, :], ACT.Copy).then_inc(s["p_turned"], 1)

    def pe(self, t):
        c, s = self.c, self.s
        self.norm.pe(t)
        self.norm.turn.wait(t, NG)

        def scores(j):
            t.wait_ge(s["operands"], j // 2 + 1)
            if j >= 2:
                t.wait_ge(s["biased"], j - 1)
            t.matmul(c.bank[j % 2][:, :], c.XT[:, j * P:(j + 1) * P],
                     self.keys[:, j // 2, :, :].rearrange("p h k -> p (h k)"), start=True, stop=True) \
                .then_inc(s["scores"], 1)

        def turn(j):
            u = j % 2
            t.wait_ge(s["exp"], j + 1)
            if j >= 2:
                t.wait_ge(s["p_turned"], j - 1)
            for k in range(4):
                last = t.transpose(c.bank[2 + u][:, k * P:(k + 1) * P], self.prob[:, u, k * P:(k + 1) * P],
                                   c.ident[:])
            last.then_inc(s["p_t"], 1)

        def values(j):
            u = j % 2
            t.wait_ge(s["p_turned"], j + 1)
            if j >= 2:
                t.wait_ge(s["added"], j - 1)
            for k in range(4):
                last = t.matmul(c.bank[4 + u][:, k * 34:(k + 1) * 34], self.probT[:, u, k * P:(k + 1) * P],
                                self.vals[:, j // 2, 2 * k:2 * k + 2, :].rearrange("p h n -> p (h n)"),
                                start=True, stop=True)
            last.then_inc(s["av"], 1)

        scores(0)
        for j in range(NT):
            if j + 1 < NT:
                scores(j + 1)
            turn(j)
            values(j)


class Ranks:

    def __init__(self, c, name):
        self.c = c
        self.counted = c.sem(name + "_rank_products")
        self.own = c.dve_chain

    def pe(self, t, chosen):
        c = self.c
        t.matmul(c.bank[1][:, 0:NT * E], c.before[:], chosen, start=True, stop=True)
        t.matmul(c.bank[2][:, 0:NT * E], c.ones[:], chosen, start=True, stop=True).then_inc(self.counted, 1)

    def dve(self, v, ranks, totals, running, zeros):
        c, own = self.c, self.own
        own.link(v, v.memset(zeros, 0.0))
        v.wait_ge(self.counted, 1)
        own.link(v, v.tensor_copy(totals, c.bank[2][:, 0:NT * E].rearrange("p (j e) -> p j e", e=E)))
        for e in range(E):
            last = v.tensor_tensor_scan(running[:, :, e], totals[:, :, e], zeros, 0.0, ALU.add, ALU.add)
        own.link(v, last)
        own.link(v, v.tensor_tensor(running, running, totals, ALU.subtract))
        own.link(v, v.tensor_tensor(ranks, c.bank[1][:, 0:NT * E].rearrange("p (j e) -> p j e", e=E), running,
                                    ALU.add))


class CapacityStage:

    CAPACITY = math.ceil(B * S / E * 1.25)

    def __init__(self, c, after):
        self.c, self.after, self.all_added = c, after, NT * E
        sc, d = c.scratch(), c.d
        self.norm = Norm(c, c.X, c.XN, 1.0, EPS, c.XT)
        self.router_w = c.sb("f_router_w", [P, E])
        self.w_gate = c.sb("f_w_gate", [P, 256])
        self.w_down = c.late[:, 2048:4096].rearrange("p (k n) -> p k n", k=2)
        self.load = (Load(c, "f").add(self.router_w[:], d["L2_ffn_w_router"]).add(self.w_gate[:], d["L2_ffn_w_gate"])
                     .add(self.w_down, d["L2_ffn_w_down"]))
        self.hidden = sc.take(2 * NT * P).rearrange("p (k n) -> p k n", k=2)
        self.own = c.dve_chain
        self.router = Router(c)
        self.ranks = Ranks(c, "f")
        self.s = c.signals("f", "chosen hidden_in hidden result combine added")

    def dve(self, v):
        c, s, own, r = self.c, self.s, self.own, self.c.routing
        self.norm.dve(v, self.after)
        shape = (P, NT, E)
        prob, left, one, two, chosen, ranks, totals, running = (r.table(k) for k in range(8))
        m1, m2, i1, i2, zeros, total = (r.rows(k) for k in range(6))
        self.router.softmax(v, self.router.logits(v), prob, m1)
        r.first(v, own, prob, m1, one, i1)
        r.hide(v, own, prob, one, left)
        r.first(v, own, left, m2, two, i2)
        v.tensor_tensor(chosen, one, two, ALU.add).then_inc(s["chosen"], 1)
        v.wait_ge(s["chosen"], 1)
        self.ranks.dve(v, ranks, totals, running, zeros)
        own.link(v, v.tensor_scalar(ranks, ranks, float(self.CAPACITY), None, ALU.is_lt))
        own.link(v, v.tensor_tensor(one, one, bc(m1[:, :, None], shape), ALU.mult))
        own.link(v, v.tensor_tensor(two, two, bc(m2[:, :, None], shape), ALU.mult))
        own.link(v, v.tensor_tensor(one, one, two, ALU.add))
        own.link(v, v.tensor_tensor(one, one, ranks, ALU.mult))
        own.link(v, v.tensor_reduce(total, one, AX.X, ALU.add))
        own.link(v, v.tensor_scalar(total, total, 1.0e-6, None, ALU.add))
        own.link(v, v.reciprocal(total, total))
        own.link(v, v.tensor_tensor(one, one, bc(total[:, :, None], shape), ALU.mult))
        v.tensor_scalar(one, one, c.gates[:, 6:7], None, ALU.mult).then_inc(s["combine"], 1)
        v.wait_ge(s["combine"], 1)
        n = 0
        for q in range(NT // 2):
            v.wait_ge(s["result"], q + 1)
            for e in range(E):
                for i in range(2):
                    j = 2 * q + i
                    if e:
                        v.wait_ge(s["added"], n - 1)
                    bank = c.bank[4 * (q % 2) + 2 * i + e // 4]
                    v.scalar_tensor_tensor(c.X[:, j, :], bank[:, (e % 4) * D:(e % 4 + 1) * D],
                                           one[:, j, e:e + 1], c.X[:, j, :], ALU.mult, ALU.add) \
                        .then_inc(s["added"], 1)
                    n += 1

    def pool(self, g):
        self.norm.pool(g)

    def act(self, a):
        c, s = self.c, self.s
        self.norm.act(a)
        self.router.act(a, c.routing.table(0))
        for n in range(2 * NG):
            k, q = n % 2, n // 2
            a.wait_ge(s["hidden_in"], n + 1)
            a.activation(self.hidden[:, k, q * CHUNK:(q + 1) * CHUNK], c.bank[4 + n % 4][:, :], ACT.Silu) \
                .then_inc(s["hidden"], 1)

    def pe(self, t):
        c, s = self.c, self.s
        self.norm.pe(t)
        self.load.wait(t)
        self.norm.turn.wait(t, NG)
        self.router.pe(t, self.router_w[:])
        for n in range(2 * NG):
            k, q = n % 2, n // 2
            if n >= 4:
                t.wait_ge(s["hidden"], n - 3)
            t.matmul(c.bank[4 + n % 4][:, :], self.w_gate[:, k * P:(k + 1) * P],
                     c.XT[:, q * CHUNK:(q + 1) * CHUNK], start=True, stop=True).then_inc(s["hidden_in"], 1)
        t.wait_ge(s["chosen"], 1)
        self.ranks.pe(t, c.routing.table(4).rearrange("p j e -> p (j e)"))
        t.wait_ge(s["combine"], 1)
        t.wait_ge(s["hidden"], 2 * NG)
        for q in range(NT // 2):
            if q >= 2:
                t.wait_ge(s["added"], 2 * E * (q - 1))
            for i in range(2):
                j = 2 * q + i
                for half in range(2):
                    for k in range(2):
                        last = t.matmul(c.bank[4 * (q % 2) + 2 * i + half][:, :],
                                        self.hidden[:, k, j * P:(j + 1) * P],
                                        self.w_down[:, k, half * 512:(half + 1) * 512],
                                        start=(k == 0), stop=(k == 1))
            last.then_inc(s["result"], 1)


class NullStage:

    H, DH = 16, 64
    SCALE = 64 ** -0.5

    def __init__(self, c, after):
        self.c, self.after, self.all_added = c, after, NG
        sc, d = c.scratch(), c.d
        ar = Arena(c.arena_tensor, 10240)
        self.norm = Norm(c, c.X, c.XN, 1.0, EPS, c.XT)
        self.Wq = c.sb("g_Wq", [P, 8, D])
        self.Wkv = c.wide[:, :].rearrange("p (k n) -> p k n", k=2)
        self.Wout = c.sb("g_Wout", [P, 8, D])
        self.affine = c.sb("g_affine", [P, 2, D])
        self.null = c.sb("g_null", [P, 2])
        self.load = (Load(c, "g").add(self.Wq[:], d["L3_xattn_Wq"]).add(self.Wkv, d["L3_xattn_Wkv"])
                     .add(self.Wout[:], d["L3_xattn_Wout"])
                     .add(self.affine[:, 0, :], d["L3_xattn_ln_scale"].partition_broadcast(P))
                     .add(self.affine[:, 1, :], d["L3_xattn_ln_bias"].partition_broadcast(P))
                     .add(self.null[0:64, :], d["L3_xattn_null_kv"]).add(self.null[64:128, :], d["L3_xattn_null_kv"]))
        self.keys = ar.take(B * 1024).rearrange("p (b n) -> p b n", b=B)
        self.null_rows = ar.take(2 * 128).rearrange("p (k n) -> p k n", k=2)
        self.null_keys = ar.take(16)
        self.null_scores = ar.take(16 * NT)
        self.null_vals = ar.take(D)[0:16, :]
        self.null_probT = ar.take(2 * P)[0:16, :].rearrange("p (u n) -> p u n", u=2)
        self.top = ar.take(3 * 16).rearrange("p (u h) -> p u h", u=3)
        self.sums = ar.take(3 * 16).rearrange("p (u h) -> p u h", u=3)
        self.vals = sc.take(B * 1024).rearrange("p (b k d) -> p b k d", b=B, k=8)
        room = sc.take(3 * 1040 + 1024)
        self.kv = room[:, 0:4096].rearrange("p (u b a n) -> p u b a n", u=4, b=B, a=2)
        self.prob = room[:, 0:3120].rearrange("p (u n) -> p u n", u=3)
        self.probT = room[:, 3120:4144]
        self.own = c.dve_chain
        self.post = Norm(c, c.XN, c.XN, 1.0, 1.0e-6)
        self.s = c.signals("g", "zeroed null_set nulls nulls_copied kv kv_even kv_odd folded copied_a copied_b "
                                "scores null_scores raised shifted exp summed divided p_t p_turned out "
                                "out_copied affine added")

    def pool(self, g):
        c, s = self.c, self.s
        self.load.wait(g)
        g.memset(self.null_rows, 0.0).then_inc(s["zeroed"], 1)
        g.wait_ge(s["zeroed"], 1)
        g.wait_ge(self.before.s["added"], self.before.all_added)
        for half in range(2):
            rows = slice(64 * (1 - half), 64 * (1 - half) + 64)
            g.memset(self.kv[rows, :, :, half, :], 0.0).then_inc(s["zeroed"], 1)
            g.wait_ge(s["zeroed"], 2 + half)
        for k in range(2):
            g.tensor_copy(self.null_rows[0:64, k, 0:P:18], bc(self.null[0:64, k:k + 1], (64, 8))) \
                .then_inc(s["null_set"], 1)
            g.tensor_copy(self.null_rows[64:128, k, 1:P:18], bc(self.null[64:128, k:k + 1], (64, 8))) \
                .then_inc(s["null_set"], 1)
        self.norm.pool(g)
        for j in range(NT):
            g.wait_ge(s["summed"], 2 * (j + 1))
            main = self.prob[:, j % 3, 0:1024].rearrange("p (h k) -> p h k", h=16)
            g.tensor_tensor(main, main, bc(self.sums[:, j % 3, :][:, :, None], (P, 16, 64)), ALU.mult) \
                .then_inc(s["divided"], 1)
            g.tensor_tensor(self.prob[:, j % 3, 1024:1040], self.prob[:, j % 3, 1024:1040],
                            self.sums[:, j % 3, :], ALU.mult).then_inc(s["divided"], 1)
        self.post.pool(g)

    def pe(self, t):
        c, s, bank = self.c, self.s, self.c.bank
        self.load.wait(t)
        t.wait_ge(self.before.s["added"], self.before.all_added)
        t.wait_ge(s["null_set"], 4)
        for k in range(8):
            t.matmul(bank[0][:, 0:16], self.Wq[:, k, :], self.null_rows[:, 0, 16 * k:16 * k + 16],
                     start=(k == 0), stop=(k == 7))
        for k in range(8):
            last = t.matmul(bank[1][0:16, 0:D], self.null_rows[:, 1, 16 * k:16 * k + 16], self.Wout[:, k, :],
                            start=(k == 0), stop=(k == 7))
        last.then_inc(s["nulls"], 1)

        def project(n):
            if n >= 2:
                t.wait_ge(s["kv_even"], n - 1)
                t.wait_ge(s["kv_odd"], n - 1)
            for k in range(2):
                last = t.matmul(bank[2 + n % 2][:, :], self.Wkv[:, k, n * P:(n + 1) * P], c.CT[:, k, :],
                                start=(k == 0), stop=(k == 1))
            last.then_inc(s["kv"], 1)

        def fold(n):
            k = n % 8
            t.wait_ge(s["kv_even"], n + 1)
            t.wait_ge(s["kv_odd"], n + 1)
            for q in range(2):
                m = 2 * n + q
                if m >= 4:
                    t.wait_ge(s["copied_b" if q else "copied_a"], n - 1)
                out = bank[4 + m % 4]
                if n < 8:
                    last = t.matmul(out[:, :], self.Wq[:, k, :],
                                    self.kv[:, n % 4, 4 * q:4 * q + 4, :, :].rearrange("p b a n -> p (b a n)"),
                                    start=True, stop=True)
                else:
                    for b in range(4):
                        last = t.matmul(out[:, b * D:(b + 1) * D],
                                        self.kv[:, n % 4, 4 * q + b, :, :].rearrange("p a n -> p (a n)"),
                                        self.Wout[:, k, :], start=True, stop=True)
                last.then_inc(s["folded"], 1)

        t.wait_ge(s["zeroed"], 3)
        project(0)
        project(1)
        for n in range(16):
            if n + 2 < 16:
                project(n + 2)
            fold(n)
        t.wait_ge(s["copied_a"], 16)
        t.wait_ge(s["copied_b"], 16)
        self.norm.pe(t)
        self.norm.turn.wait(t, NG)
        t.wait_ge(s["nulls_copied"], 2)

        def scores(j):
            if j >= 2:
                t.wait_ge(s["shifted"], 2 * (j - 1))
            for half in range(2):
                last = t.matmul(bank[2 * (j % 2) + half][:, :], c.XT[:, j * P:(j + 1) * P],
                                self.keys[:, j // 2, half * 512:(half + 1) * 512], start=True, stop=True)
            last.then_inc(s["scores"], 1)

        for j in range(NT):
            last = t.matmul(bank[5][:, 16 * j:16 * j + 16], c.XT[:, j * P:(j + 1) * P], self.null_keys,
                            start=True, stop=True)
        last.then_inc(s["null_scores"], 1)

        def turn(j):
            t.wait_ge(s["divided"], 2 * j + 2)
            if j:
                t.wait_ge(s["p_turned"], 3 * j)
            if j >= 2:
                t.wait_ge(s["out_copied"], j - 1)
            if j == 0:
                t.wait_ge(s["shifted"], 2)
            for k in range(8):
                last = t.transpose(bank[6 + k // 4][:, (k % 4) * P:(k % 4 + 1) * P],
                                   self.prob[:, j % 3, k * P:(k + 1) * P], c.ident[:])
                if k == 3:
                    last.then_inc(s["p_t"], 1)
            last.then_inc(s["p_t"], 1)
            t.transpose(bank[4 + j % 2][0:16, P:2 * P], self.prob[:, j % 3, 1024:1040], c.ident[:]) \
                .then_inc(s["p_t"], 1)

        def values(j):
            t.wait_ge(s["p_turned"], 3 * j + 3)
            out = bank[4 + j % 2][:, 256:256 + D]
            for k in range(8):
                t.matmul(out, self.probT[:, k * P:(k + 1) * P], self.vals[:, j // 2, k, :], start=(k == 0),
                         stop=False)
            t.matmul(out, self.null_probT[:, j % 2, :], self.null_vals, start=False, stop=True) \
                .then_inc(s["out"], 1)

        scores(0)
        scores(1)
        scores(2)
        for j in range(NT):
            turn(j)
            if j + 3 < NT:
                scores(j + 3)
            values(j)

    def act(self, a):
        c, s, bank = self.c, self.s, self.c.bank
        a.wait_ge(s["nulls"], 1)
        a.activation(self.null_keys, bank[0][:, 0:16], ACT.Copy, scale=self.SCALE).then_inc(s["nulls_copied"], 1)
        a.activation(self.null_vals, bank[1][0:16, 0:D], ACT.Copy).then_inc(s["nulls_copied"], 1)

        def take_half(n):
            a.wait_ge(s["kv"], n + 1)
            if n >= 4:
                a.wait_ge(s["folded"], 2 * (n - 3))
            a.activation(self.kv[0:64, n % 4, :, 0, :], bank[2 + n % 2][0:64, :].rearrange("p (b n) -> p b n", b=B),
                         ACT.Copy).then_inc(s["kv_even"], 1)

        def take_fold(n):
            k = n % 8
            a.wait_ge(s["folded"], 2 * n + 1)
            out = (self.keys[:, 0:4, 128 * k:128 * k + 128] if n < 8 else self.vals[:, 0:4, k, :])
            a.activation(out, bank[4 + 2 * (n % 2)][:, :].rearrange("p (b n) -> p b n", b=4), ACT.Copy,
                         scale=self.SCALE if n < 8 else 1.0).then_inc(s["copied_a"], 1)

        a.wait_ge(s["zeroed"], 3)
        take_half(0)
        take_half(1)
        for n in range(16):
            if n + 2 < 16:
                take_half(n + 2)
            take_fold(n)
        self.norm.act(a)

        def exponentials(j):
            a.wait_ge(s["shifted"], 2 * j + 2)
            a.activation(self.prob[:, j % 3, :], self.prob[:, j % 3, :], ACT.Exp).then_inc(s["exp"], 1)

        def copy_turned(j):
            for k in range(2):
                a.wait_ge(s["p_t"], 3 * j + k + 1)
                if j:
                    a.wait_ge(s["out"], j)
                a.activation(self.probT[:, k * 512:(k + 1) * 512], bank[6 + k][:, :], ACT.Copy) \
                    .then_inc(s["p_turned"], 1)
            a.wait_ge(s["p_t"], 3 * j + 3)
            a.activation(self.null_probT[:, j % 2, :], bank[4 + j % 2][0:16, P:2 * P], ACT.Copy) \
                .then_inc(s["p_turned"], 1)

        def copy_result(j):
            a.wait_ge(s["out"], j + 1)
            a.activation(c.XN[:, j, :], bank[4 + j % 2][:, 256:256 + D], ACT.Copy).then_inc(s["out_copied"], 1)

        exponentials(0)
        exponentials(1)
        for j in range(NT):
            copy_turned(j)
            if j + 2 < NT:
                exponentials(j + 2)
            copy_result(j)

    def dve(self, v):
        c, s, own, bank = self.c, self.s, self.own, self.c.bank

        def take_half(n):
            v.wait_ge(s["kv"], n + 1)
            if n >= 4:
                v.wait_ge(s["folded"], 2 * (n - 3))
            v.tensor_copy(self.kv[64:128, n % 4, :, 1, :],
                          bank[2 + n % 2][64:128, :].rearrange("p (b n) -> p b n", b=B)).then_inc(s["kv_odd"], 1)

        def take_fold(n):
            k = n % 8
            v.wait_ge(s["folded"], 2 * n + 2)
            out = (self.keys[:, 4:8, 128 * k:128 * k + 128] if n < 8 else self.vals[:, 4:8, k, :])
            v.tensor_scalar(out, bank[5 + 2 * (n % 2)][:, :].rearrange("p (b n) -> p b n", b=4),
                            self.SCALE if n < 8 else 1.0, None, ALU.mult).then_inc(s["copied_b"], 1)

        v.wait_ge(s["zeroed"], 3)
        take_half(0)
        take_half(1)
        for n in range(16):
            if n + 2 < 16:
                take_half(n + 2)
            take_fold(n)
        self.norm.dve(v, self.after)

        def softmax(j):
            u = j % 3
            main_in = c.psum[:, 2 * (j % 2):2 * (j % 2) + 2, :].rearrange("p k (h n) -> p (k h) n", n=64)
            null_in = self.null_scores[:, 16 * j:16 * j + 16]
            main = self.prob[:, u, 0:1024].rearrange("p (h n) -> p h n", n=64)
            null = self.prob[:, u, 1024:1040]
            top, sums = self.top[:, u, :], self.sums[:, u, :]
            v.wait_ge(s["scores"], j + 1)
            own.link(v, v.tensor_reduce(top, main_in, AX.X, ALU.max))
            own.link(v, v.tensor_tensor(top, null_in, top, ALU.max))
            if j >= 3:
                v.wait_ge(s["p_t"], 3 * (j - 2))
            v.tensor_tensor(main, main_in, bc(top[:, :, None], (P, 16, 64)), ALU.subtract) \
                .then_inc(s["shifted"], 1)
            v.tensor_tensor(null, null_in, top, ALU.subtract).then_inc(s["shifted"], 1)

        def sums(j):
            u = j % 3
            total = self.sums[:, u, :]
            main = self.prob[:, u, 0:1024].rearrange("p (h n) -> p h n", n=64)
            v.wait_ge(s["exp"], j + 1)
            if j >= 3:
                v.wait_ge(s["divided"], 2 * (j - 2))
            own.link(v, v.tensor_reduce(total, main, AX.X, ALU.add))
            v.tensor_tensor(total, total, self.prob[:, u, 1024:1040], ALU.add).then_inc(s["summed"], 1)
            v.wait_ge(s["summed"], 2 * j + 1)
            v.reciprocal(total, total).then_inc(s["summed"], 1)

        v.wait_ge(s["null_scores"], 1)
        own.link(v, v.tensor_copy(self.null_scores, bank[5][:, 0:256]))
        softmax(0)
        softmax(1)
        sums(0)
        for j in range(NT):
            if j + 2 < NT:
                softmax(j + 2)
            if j + 1 < NT:
                sums(j + 1)
        self.post.dve(v, s["out_copied"])
        for q in range(NG):
            tiles = slice(GROUP * q, GROUP * q + GROUP)
            self.post.wait_normed(v, GROUP * q + GROUP)
            own.link(v, v.tensor_tensor(c.XN[:, tiles, :], c.XN[:, tiles, :],
                                        bc(self.affine[:, 0, :][:, None, :], (P, GROUP, D)), ALU.mult))
            own.link(v, v.tensor_tensor(c.XN[:, tiles, :], c.XN[:, tiles, :],
                                        bc(self.affine[:, 1, :][:, None, :], (P, GROUP, D)), ALU.add))
            v.scalar_tensor_tensor(c.X[:, tiles, :], c.XN[:, tiles, :], c.gates[:, 3:4], c.X[:, tiles, :],
                                   ALU.mult, ALU.add).then_inc(s["added"], 1)


class DispatchStage:

    CAPACITY = math.ceil(B * S * 1.0 / E)
    SLOTS = E * CAPACITY
    TILES = CAPACITY // P

    def __init__(self, c, after):
        self.c, self.after, self.all_added = c, after, NT
        sc, d = c.scratch(), c.d
        assert self.CAPACITY == self.TILES * P
        self.norm = Norm(c, c.X, c.XN, 1.0, EPS, c.XT)
        self.router_w = c.sb("h_router_w", [P, E])
        self.w1 = c.wide[:, :].rearrange("p (e n) -> p e n", e=E)
        self.w2 = c.late[:, :].rearrange("p (e k d) -> p e k d", e=E, k=4)
        self.load = Load(c, "h").add(self.router_w[:], d["L3_ffn_Wr"])
        self.expert_load = Load(c, "h_experts").add(self.w1, d["L3_ffn_W1"].rearrange("e d f -> d e f"))
        for e in range(E):
            self.expert_load.add(self.w2[:, e], d["L3_ffn_W2"][e].rearrange("(k f) d -> f k d", k=4))
        self.taken = c.nc.dram_tensor("slots_in", (self.SLOTS, D), F32).ap()
        self.given = c.nc.dram_tensor("slots_out", (self.SLOTS, D), F32).ap()
        self.rows = sc.take(NT * D).rearrange("p (j d) -> p j d", j=NT)
        self.hidden = sc.take(2 * 1024).rearrange("p (u k n) -> p u k n", u=2, k=4)
        self.results = sc.take(NT * D).rearrange("p (j d) -> p j d", j=NT)
        self.scatter_at = c.sb("h_scatter_at", [P, NT], I32)
        self.gather_at = c.sb("h_gather_at", [P, NT], I32)
        self.own = c.dve_chain
        self.router = Router(c)
        self.ranks = Ranks(c, "h")
        self.s = c.signals("h", "cleared chosen slots scattered fetched hidden_in hidden_a "
                                "hidden_v result copied stored gathered added")
        self.slot_turn = Turn(c, self.rows, c.XT, self.s["fetched"], 0, 16 * NG)

    def clear(self, sp):
        c = self.c
        sp.wait_ge(c.zeroed, 1)
        for j in range(NT):
            sp.dma_start(self.taken[j * P:(j + 1) * P, :], c.zero_tile[:]).then_inc(self.s["cleared"], 16)

    def pool(self, g):
        c, s = self.c, self.s
        self.norm.pool(g)
        g.wait_ge(s["slots"], 1)
        g.wait_ge(s["cleared"], 16 * NT)
        for j in range(NT):
            g.indirect_dma_start(self.taken, bass.IndirectOffsetOnAxis(ap=self.scatter_at[:, j:j + 1], axis=0),
                                 c.XN[:, j, :], None, bounds_check=self.SLOTS - 1, oob_is_err=False) \
                .then_inc(s["scattered"], 16)
        g.wait_ge(s["stored"], 16 * E)
        for j in range(NT):
            g.indirect_dma_start(self.rows[:, j, :], None, self.given,
                                 bass.IndirectOffsetOnAxis(ap=self.gather_at[:, j:j + 1], axis=0),
                                 bounds_check=self.SLOTS - 1, oob_is_err=False) \
                .then_inc(s["gathered"], 16)

    def sync(self, sp):
        s = self.s
        sp.wait_ge(s["scattered"], 16 * NT)
        for q in range(NG):
            sp.dma_start(self.rows[:, GROUP * q:GROUP * q + GROUP, :],
                         self.taken.rearrange("(j p) d -> p j d", p=P)[:, GROUP * q:GROUP * q + GROUP, :]) \
                .then_inc(s["fetched"], 16)
        for e in range(E):
            j = self.TILES * e
            sp.wait_ge(s["copied"], e + 1)
            sp.dma_start(self.given.rearrange("(j p) d -> p j d", p=P)[:, j:j + self.TILES, :],
                         self.results[:, j:j + self.TILES, :]).then_inc(s["stored"], 16)

    def dve(self, v):
        c, s, own, r = self.c, self.s, self.own, self.c.routing
        self.norm.dve(v, self.after)
        shape = (P, NT, E)
        prob, tmp, one, chosen_at, ranks, totals, running = (r.table(k) for k in range(7))
        m1, i1, zeros, rank, kept, slot, weight = (r.rows(k) for k in range(7))
        self.router.softmax(v, self.router.logits(v), prob, m1)
        r.first(v, own, prob, m1, one, i1)
        v.tensor_copy(chosen_at, one).then_inc(s["chosen"], 1)
        self.ranks.dve(v, ranks, totals, running, zeros)
        own.link(v, v.tensor_tensor(ranks, ranks, one, ALU.mult))
        own.link(v, v.tensor_reduce(rank, ranks, AX.X, ALU.add))
        own.link(v, v.tensor_scalar(kept, rank, float(self.CAPACITY), None, ALU.is_lt))
        own.link(v, v.tensor_scalar(slot, i1, float(E), float(self.CAPACITY), ALU.add, ALU.mult))
        own.link(v, v.tensor_tensor(slot, slot, rank, ALU.add))
        own.link(v, v.tensor_tensor(slot, slot, kept, ALU.mult))
        own.link(v, v.tensor_copy(self.gather_at[:], slot))
        own.link(v, v.tensor_scalar(rank, kept, -float(2 * self.SLOTS), float(2 * self.SLOTS), ALU.mult, ALU.add))
        own.link(v, v.tensor_tensor(slot, slot, rank, ALU.add))
        own.link(v, v.tensor_tensor(weight, m1, kept, ALU.mult))
        own.link(v, v.tensor_scalar(weight, weight, c.gates[:, 7:8], None, ALU.mult))
        v.tensor_copy(self.scatter_at[:], slot).then_inc(s["slots"], 1)
        for e in range(E):
            v.wait_ge(s["hidden_in"], 2 * e + 2)
            if e >= 2:
                v.wait_ge(s["result"], e - 1)
            v.tensor_scalar(self.hidden[:, e % 2, 2:4, :].rearrange("p k n -> p (k n)"),
                            c.bank[2 * (e % 2) + 1][:, :], 0.0, None, ALU.max).then_inc(s["hidden_v"], 1)
        for j in range(NT):
            v.wait_ge(s["gathered"], 16 * NT)
            v.scalar_tensor_tensor(c.X[:, j, :], self.rows[:, j, :], weight[:, j:j + 1], c.X[:, j, :],
                                   ALU.mult, ALU.add).then_inc(s["added"], 1)

    def act(self, a):
        c, s = self.c, self.s
        self.norm.act(a)
        self.router.act(a, c.routing.table(0))
        self.slot_turn.act(a)

        def copy(e):
            a.wait_ge(s["result"], e + 1)
            a.activation(self.results[:, self.TILES * e:self.TILES * (e + 1), :].rearrange("p j d -> p (j d)"),
                         c.bank[4 + e % 2][:, 0:self.TILES * D], ACT.Copy).then_inc(s["copied"], 1)

        for e in range(E):
            a.wait_ge(s["hidden_in"], 2 * e + 1)
            if e >= 2:
                a.wait_ge(s["result"], e - 1)
            a.activation(self.hidden[:, e % 2, 0:2, :].rearrange("p k n -> p (k n)"),
                         c.bank[2 * (e % 2)][:, :], ACT.Relu).then_inc(s["hidden_a"], 1)
            if e:
                copy(e - 1)
        copy(E - 1)

    def pe(self, t):
        c, s = self.c, self.s
        self.norm.pe(t)
        self.load.wait(t)
        self.norm.turn.wait(t, NG)
        self.router.pe(t, self.router_w[:])
        t.wait_ge(s["chosen"], 1)
        self.ranks.pe(t, c.routing.table(3).rearrange("p j e -> p (j e)"))
        self.slot_turn.pe(t)
        self.expert_load.wait(t)
        t.wait_ge(s["slots"], 1)
        n = self.CAPACITY

        def first(e):
            self.slot_turn.wait(t, e // 2 + 1)
            if e >= 2:
                t.wait_ge(s["hidden_a"], e - 1)
                t.wait_ge(s["hidden_v"], e - 1)
            for k in range(4):
                last = t.matmul(c.bank[2 * (e % 2) + k // 2][:, (k % 2) * n:(k % 2 + 1) * n],
                                self.w1[:, e, k * P:(k + 1) * P], c.XT[:, e * n:(e + 1) * n], start=True, stop=True)
                if k % 2:
                    last.then_inc(s["hidden_in"], 1)

        def second(e):
            t.wait_ge(s["hidden_a"], e + 1)
            t.wait_ge(s["hidden_v"], e + 1)
            if e >= 2:
                t.wait_ge(s["copied"], e - 1)
            for i in range(self.TILES):
                for k in range(4):
                    last = t.matmul(c.bank[4 + e % 2][:, i * D:(i + 1) * D],
                                    self.hidden[:, e % 2, k, i * P:(i + 1) * P], self.w2[:, e, k, :],
                                    start=(k == 0), stop=(k == 3))
            last.then_inc(s["result"], 1)

        first(0)
        for e in range(E):
            if e + 1 < E:
                first(e + 1)
            second(e)


KINDS = (DepoolStage, ExpertPairStage, HeadsStage, AcrossStage, MaskedStage, CapacityStage, NullStage, DispatchStage,)


STAGES = 8


def build(nc, d, out):
    with ExitStack() as ctx:
        c = Core(nc, ctx, d)
        constants = Constants(c)
        c.arena_tensor = c.sb("arena", [P, 10240])
        c.late = c.sb("late", [P, 4096])
        c.wide = c.sb("wide", [P, 4096])
        c.routing = Routing(c)
        c.gates_in = c.sb("gates_in", [P, 8])
        c.gates_done = c.sem("gates_done")
        c.gate_load = (Load(c, "gates").add(c.gates_in[:, 0:4], d["g_xattn"].partition_broadcast(P))
                       .add(c.gates_in[:, 4:8], d["g_ffn"].partition_broadcast(P)))
        x_tiles = d["x"].rearrange("b (i p) d -> p (b i) d", p=P)
        x_load = Load(c, "x")
        for g in range(2):
            x_load.add(c.X[:, 8 * g:8 * g + 8, :], x_tiles[:, 8 * g:8 * g + 8, :])
        c2_load = (Load(c, "context").add(c.C2[0:64], d["ctx_2048"].rearrange("b s d -> s b d"))
                   .add(c.C2[64:128], d["ctx_2048"].rearrange("b s d -> s b d")))
        c.c2_load = c2_load
        stored = c.sem("stored")
        c.zero_tile, c.zeroed = c.sb("zero_tile", [P, D]), c.sem("zero_tile")
        stages = []
        for kind in KINDS[:STAGES]:
            stages.append(kind(c, None))
            stages[-1].before = stages[-2] if len(stages) > 1 else None
        block = ctx.enter_context(nc.Block())

        dispatch = [st for st in stages if isinstance(st, DispatchStage)]

        @block.sync
        def _(sp):
            c.gate_load.issue(sp)
            x_load.issue(sp)
            for n, st in enumerate(stages):
                if n == 2:
                    c2_load.issue(sp)
                st.load.issue(sp)
                if isinstance(st, ExpertPairStage):
                    for q in range(4):
                        st.expert_load[q].issue(sp)
            for st in dispatch:
                st.clear(sp)
                if st.before is not None:
                    sp.wait_ge(st.before.before.s["result"], NT // 2)
                    sp.wait_ge(st.before.s["kv"], 16)
                st.expert_load.issue(sp)
                st.sync(sp)
            for g in range(NG):
                sp.wait_ge(stages[-1].s["added"], stages[-1].all_added)
                sp.dma_start(out.rearrange("b (i p) d -> p (b i) d", p=P)[:, GROUP * g:GROUP * g + GROUP, :],
                             c.X[:, GROUP * g:GROUP * g + GROUP, :]).then_inc(stored, 16)
            sp.wait_ge(stored, 16 * NG)

        @block.gpsimd
        def _(g):
            constants.pool(g)
            g.wait_ge(c.constants_done, 1)
            g.memset(c.zero_tile[:], 0.0).then_inc(c.zeroed, 1)
            for st in stages:
                st.pool(g)

        @block.scalar
        def _(a):
            for st in stages:
                st.act(a)

        @block.vector
        def _(v):
            x_load.wait(v)
            v.wait_ge(c.gates_done, 1)
            for n, st in enumerate(stages):
                if n:
                    v.wait_ge(stages[n - 1].s["added"], stages[n - 1].all_added)
                st.dve(v)

        @block.tensor
        def _(t):
            for st in stages:
                st.pe(t)


def kernel(**inputs):
    import numpy as np
    import concourse.bacc as bacc
    from concourse.bass_utils import run_bass_kernel_spmd

    given = {n: np.asarray(a) for n, a in inputs.items()}
    T = lambda n: given[n].T
    lay = {
        "x": given["x"],
        "ctx_pairs": given["ctx_2048"].reshape(4, 2, SC, DC).transpose(1, 2, 0, 3).reshape(P, 4, DC),
        "ctx_T": given["ctx_2048"].reshape(B * SC, 2, P).transpose(2, 1, 0),
        "ctx_2048": given["ctx_2048"],
        "patch_lens": given["mask_BxS2_if0"].reshape(4, P).T,
        "seq_mask": given["mask_BxS2_ik0"].reshape(B * SC),
        "g_xattn": given["g_xattn"], "g_ffn": given["g_ffn"],
        "L0_xattn_g_res": given["L0_xattn_g_res"].reshape(D, 1),
        "L0_xattn_W_in": T("L0_xattn_W_in"),
        "L0_ffn_b1": given["L0_ffn_b1"].reshape(2 * E, P).T,
        "L0_ffn_b2": given["L0_ffn_b2"].reshape(2 * E, P).T,
        "L0_ffn_bg": given["L0_ffn_bg"].reshape(2 * E, P).T,
        "L1_xattn_w_qkv": T("L1_xattn_w_qkv"), "L1_xattn_w_proj": T("L1_xattn_w_proj"),
        "L1_ffn_in_proj_w": T("L1_ffn_in_proj_w"), "L1_ffn_out_w": T("L1_ffn_out_w"),
        "L1_ffn_router_w": T("L1_ffn_router_w"), "L1_ffn_b1": T("L1_ffn_b1"),
        "L1_ffn_w1": given["L1_ffn_w1"].transpose(2, 0, 1), "L1_ffn_w2": given["L1_ffn_w2"].transpose(2, 0, 1),
        "L2_ffn_w_router": T("L2_ffn_w_router"), "L2_ffn_w_gate": T("L2_ffn_w_gate"),
        "L2_ffn_w_down": given["L2_ffn_w_down"].transpose(2, 0, 1).reshape(2, P, E * D).transpose(1, 0, 2),
        "L3_xattn_null_kv": T("L3_xattn_null_kv"),
        "L3_xattn_Wq": given["L3_xattn_Wq"].T.reshape(8, P, D).transpose(1, 0, 2),
        "L3_xattn_Wkv": given["L3_xattn_Wkv"].reshape(2, P, 2048).transpose(1, 0, 2),
        "L3_xattn_Wout": given["L3_xattn_Wout"].reshape(8, P, D).transpose(1, 0, 2),
    }
    for n in ("L0_xattn_b_in L0_xattn_g_init L0_ffn_gate_w L0_ffn_gate_b L0_ffn_w1 L0_ffn_w2 "
              "L0_ffn_wg L0_ffn_w3 L0_ffn_b3 L1_xattn_b_proj L1_ffn_in_proj_b L1_ffn_out_b L1_ffn_ln1_g "
              "L1_ffn_ln1_b L1_ffn_router_b L1_ffn_b2 L1_ffn_ln2_g L1_ffn_ln2_b L2_xattn_b "
              "L3_xattn_ln_scale L3_xattn_ln_bias L3_ffn_Wr L3_ffn_W1 L3_ffn_W2").split():
        lay[n] = given[n]
    nc = bacc.Bacc("TRN2", target_bir_lowering=False, num_devices=1)
    arrays, d = {}, {}
    for n, a in lay.items():
        a = np.ascontiguousarray(a)
        arrays["in_" + n] = a
        d[n] = nc.dram_tensor("in_" + n, a.shape, mybir.dt.from_np(a.dtype), kind="ExternalInput").ap()
    out = nc.dram_tensor("out_x", (B, S, D), F32, kind="ExternalOutput").ap()
    build(nc, d, out)
    r = run_bass_kernel_spmd(nc, [arrays], core_ids=[0])
    return r.results[0]["out_x"]
```

```python
import math
from contextlib import ExitStack

import concourse.bass as bass
from concourse import mybir

F32 = mybir.dt.float32
I32 = mybir.dt.int32
BF16 = mybir.dt.bfloat16
ALU = mybir.AluOpType
ACT = mybir.ActivationFunctionType
AX = mybir.AxisListType

P = 128
B, S, D = 8, 256, 128
NT = B * S // P
SC, DC = 64, 256
E = 8
GROUP = 4
NG = NT // GROUP
CHUNK = GROUP * P
EPS = 1e-5

SMALL_STEP = 0.001
DECAY = -math.expm1(-SMALL_STEP)
KEEP = math.exp(-SMALL_STEP)


def bc(ap, shape):
    return ap.to_broadcast(list(shape))


class Arena:

    def __init__(self, tensor, size):
        self.tensor, self.size, self.at = tensor, size, 0

    def take(self, n):
        a = self.at
        self.at += n
        assert self.at <= self.size, (self.at, self.size)
        return self.tensor[:, a:a + n]


class Core:

    def __init__(self, nc, ctx, d):
        self.nc, self.ctx, self.d = nc, ctx, d
        self.psum = ctx.enter_context(nc.psum_tensor("psum", [P, 8, 512], F32))
        self.bank = [self.psum[:, i, :] for i in range(8)]
        self.X = self.sb("X", [P, NT, D])
        self.XN = self.sb("XN", [P, NT, D])
        self.XT = self.sb("XT", [P, NT * P])
        self.stats = self.sb("stats", [P, NT, 6])
        self.moments = self.sb("moments", [P, NT, 2])
        self.veps = self.sb("veps", [P, NT])
        self.rstd = self.sb("rstd", [P, NT])
        self.gates = self.sb("gates", [P, 8])
        self.scratch_tensor = self.sb("scratch", [P, 12544])
        self.C = self.sb("C", [P, 4, DC])
        self.CT = self.sb("CT", [P, 2, B * SC])
        self.C2 = self.sb("C2", [P, B, DC])

        self.norms = self.turns = 0
        self.stats_done, self.moments_done = self.sem("stats_done"), self.sem("moments_done")
        self.veps_done, self.rstd_done = self.sem("veps_done"), self.sem("rstd_done")
        self.normed, self.transposed = self.sem("normed"), self.sem("transposed")
        self.turned_done = self.sem("turned_done")
        self.routers, self.spreads = 0, 0
        self.logits_done, self.shift_done = self.sem("logits_done"), self.sem("shift_done")
        self.exp_done = self.sem("exp_done")
        self.rows_turned, self.rows_copied = self.sem("rows_turned"), self.sem("rows_copied")
        self.bias_products = self.sem("bias_products")
        self.dve_chain, self.pool_chain = Chain(self, "dve_chain"), Chain(self, "pool_chain")

    def scratch(self):
        return Arena(self.scratch_tensor, 12544)

    def signals(self, prefix, names):
        return {n: self.sem(prefix + "_" + n) for n in names.split()}

    def sb(self, name, shape, dt=F32):
        return self.ctx.enter_context(self.nc.sbuf_tensor(name, shape, dt))

    def sem(self, name):
        return self.ctx.enter_context(self.nc.semaphore(name))


class Chain:

    def __init__(self, c, name):
        self.sem, self.n = c.sem(name), 0

    def link(self, eng, ins):
        eng.wait_ge(self.sem, self.step(ins))

    def step(self, ins):
        self.n += 1
        ins.then_inc(self.sem, 1)
        return self.n


class Norm:

    def __init__(self, c, src, dst, mul=1.0, add=EPS, turned=None):
        self.c, self.src, self.dst, self.mul, self.add = c, src, dst, mul, add
        self.tiles_before, self.groups_before = NT * c.norms, NG * c.norms
        c.norms += 1
        self.at = 0
        self.turn = Turn(c, dst, turned, c.normed, GROUP, self.tiles_before) if turned is not None else None

    def stats(self, v, g, ready=None):
        c = self.c
        assert g == self.at
        self.at += 1
        for j in range(GROUP * g, GROUP * g + GROUP):
            if ready is not None:
                v.wait_ge(ready, j + 1)
            v.bn_stats(c.stats[:, j, :], self.src[:, j, :]).then_inc(c.stats_done, 1)
        for j in range(GROUP * g, GROUP * g + GROUP):
            v.wait_ge(c.stats_done, self.tiles_before + j + 1)
            v.bn_aggr(c.moments[:, j, :], c.stats[:, j, :]).then_inc(c.moments_done, 1)

    def normalize(self, v, g):
        c = self.c
        v.wait_ge(c.rstd_done, self.groups_before + g + 1)
        for j in range(GROUP * g, GROUP * g + GROUP):
            v.tensor_scalar(self.dst[:, j, :], self.src[:, j, :], c.moments[:, j, 0:1],
                            c.rstd[:, j:j + 1], ALU.subtract, ALU.mult).then_inc(c.normed, 1)

    def add_to(self, v, g, scale, sums, done):
        c = self.c
        v.wait_ge(c.rstd_done, self.groups_before + g + 1)
        tiles = range(GROUP * g, GROUP * g + GROUP)
        for j in tiles:
            v.scalar_tensor_tensor(self.dst[:, j, :], self.src[:, j, :], c.moments[:, j, 0:1], scale,
                                   ALU.subtract, ALU.mult).then_inc(c.normed, 1)
        for j in tiles:
            v.wait_ge(c.normed, self.tiles_before + j + 1)
            last = v.scalar_tensor_tensor(sums[:, j, :], self.dst[:, j, :], c.rstd[:, j:j + 1], sums[:, j, :],
                                          ALU.mult, ALU.add)
        last.then_inc(done, 1)

    def dve(self, v, ready=None):
        done = 0
        for g in range(self.at, NG):
            self.stats(v, g, ready)
            if g:
                self.normalize(v, done)
                done += 1
        for g in range(done, NG):
            self.normalize(v, g)

    def wait_normed(self, eng, tiles):
        eng.wait_ge(self.c.normed, self.tiles_before + tiles)

    def pool(self, g_):
        c = self.c
        for g in range(NG):
            a, b = GROUP * g, GROUP * g + GROUP
            g_.wait_ge(c.moments_done, self.tiles_before + b)
            g_.tensor_scalar(c.veps[:, a:b], c.moments[:, a:b, 1], self.mul, self.add,
                             ALU.mult, ALU.add).then_inc(c.veps_done, 1)
            g_.wait_ge(c.veps_done, self.groups_before + g + 1)
            g_.tensor_tensor(c.rstd[:, a:b], c.veps[:, a:b], c.minus_half[:, a:b],
                             ALU.pow).then_inc(c.rstd_done, 1)

    def pe(self, t):
        self.turn.pe(t)

    def act(self, a):
        self.turn.act(a)


class Turn:

    def __init__(self, c, src, dst, ready, per_group, base=0, banks=(6, 7)):
        self.c, self.src, self.dst, self.ready, self.per_group = c, src, dst, ready, per_group
        self.base, self.banks, self.before = base, banks, NG * c.turns
        c.turns += 1

    def wait(self, eng, groups):
        eng.wait_ge(self.c.turned_done, self.before + groups)

    def pe(self, t):
        c = self.c
        for g in range(NG):
            t.wait_ge(self.ready, self.base + self.per_group * (g + 1))
            if g >= 2:
                self.wait(t, g - 1)
            for i in range(GROUP):
                last = t.transpose(c.bank[self.banks[g % 2]][:, i * P:(i + 1) * P],
                                   self.src[:, GROUP * g + i, :], c.ident[:])
            last.then_inc(c.transposed, 1)

    def act(self, a):
        c = self.c
        for g in range(NG):
            a.wait_ge(c.transposed, self.before + g + 1)
            a.activation(self.dst[:, g * CHUNK:(g + 1) * CHUNK], c.bank[self.banks[g % 2]][:, :],
                         ACT.Copy).then_inc(c.turned_done, 1)


class Load:

    def __init__(self, c, name):
        self.sem, self.parts = c.sem(name + "_loaded"), []

    def add(self, dst, src):
        self.parts.append((dst, src))
        return self

    def issue(self, eng):
        for dst, src in self.parts:
            eng.dma_start(dst, src).then_inc(self.sem, 16)

    def wait(self, eng):
        eng.wait_ge(self.sem, 16 * len(self.parts))


class Constants:

    def __init__(self, c):
        self.c = c
        c.ident = c.sb("ident", [P, P])
        c.ident16 = c.sb("ident16", [P, P], BF16)
        c.ones = c.sb("ones", [P, P])
        c.half_ones = c.sb("half_ones", [P, P])
        c.half_upto = c.sb("half_upto", [P, P])
        c.before = c.sb("before", [P, P])
        c.minus_half = c.sb("minus_half", [P, NT])
        c.expert_m8 = c.sb("expert_m8", [P, E])
        c.column = c.sb("column", [P, S])
        c.row64 = c.sb("row64", [P, 1])
        c.head16 = c.sb("head16", [P, 8])
        c.parity = c.sb("parity", [P, 8])
        c.tile8 = c.sb("tile8", [P, NT])
        c.spread8 = c.sb("spread8", [E, P])
        c.decay = c.sb("decay", [P, P])
        c.decayT = c.sb("decayT", [P, P])
        self.own = c.pool_chain
        c.constants_done = c.sem("constants_done")

    def pool(self, g):
        c, own = self.c, self.own

        def select(t, pattern, base, mult, op=ALU.is_ge, fill=0.0):
            own.link(g, g.affine_select(out=t, in_=t, compare_op=op, fill=fill, base=base,
                                        pattern=pattern, channel_multiplier=mult))

        own.link(g, g.memset(c.ident[:], 0.0))
        select(c.ident[:], [[-1, P]], 0, 1, ALU.not_equal, 1.0)
        g.memset(c.minus_half[:], -0.5)
        g.memset(c.decay[:], DECAY)
        own.link(g, g.memset(c.ones[:], 1.0))
        own.link(g, g.memset(c.before[:], 1.0))
        select(c.before[:], [[1, P]], -1, -1)
        own.link(g, g.memset(c.half_upto[:], 1.0))
        select(c.half_upto[:], [[1, P]], 0, -1)
        own.link(g, g.memset(c.half_upto[0:64, 64:128], 0.0))
        own.link(g, g.memset(c.half_ones[:], 1.0))
        own.link(g, g.memset(c.half_ones[0:64, 64:128], 0.0))
        own.link(g, g.memset(c.half_ones[64:128, 0:64], 0.0))
        own.link(g, g.memset(c.head16[:], 1.0))
        select(c.head16[:], [[-16, 8]], 0, 1)
        select(c.head16[:], [[16, 8]], 15, -1)
        own.link(g, g.memset(c.tile8[:], 1.0))
        select(c.tile8[:], [[-E, NT]], 0, 1)
        select(c.tile8[:], [[E, NT]], E - 1, -1)
        own.link(g, g.memset(c.spread8[:], 0.0))
        select(c.spread8[:, :].rearrange("e (j f) -> e j f", f=E), [[0, NT], [1, E]], 0, -1, ALU.not_equal, 1.0)
        par = c.parity[:, :].rearrange("p (k a) -> p k a", a=2)
        own.link(g, g.memset(c.parity[:], 0.0))
        g.memset(par[0:64, :, 0], 1.0)
        own.link(g, g.memset(par[64:128, :, 1], 1.0))
        own.link(g, g.iota(c.expert_m8[:], pattern=[[1, E]], base=-E, channel_multiplier=0,
               allow_small_or_imprecise_dtypes=True))
        own.link(g, g.iota(c.column[:], pattern=[[1, S]], base=0, channel_multiplier=0,
               allow_small_or_imprecise_dtypes=True))
        own.link(g, g.iota(c.row64[0:64, :], pattern=[[0, 1]], base=0, channel_multiplier=1,
               allow_small_or_imprecise_dtypes=True))
        g.iota(c.row64[64:128, :], pattern=[[0, 1]], base=0, channel_multiplier=1,
               allow_small_or_imprecise_dtypes=True).then_inc(c.constants_done, 1)


class DepoolStage:

    def __init__(self, c):
        self.c = c
        sc, d = c.scratch(), c.d
        self.norm = Norm(c, c.X, c.XN, 1.0 + EPS, EPS * EPS, c.XT)
        self.WinT = c.sb("WinT", [P, D])
        self.Wg = c.sb("Wg", [P, D])
        self.g_res = c.sb("g_res", [P, 1])
        self.b_in = c.sb("b_in", [1, D])
        self.lens = c.sb("lens", [P, 4], I32)
        self.small = c.sb("a_small", [P, 7, 4])
        self.g_init = sc.take(D)
        self.square = sc.take(DC)
        self.hp = sc.take(4 * D).rearrange("p (a d) -> p a d", a=4)
        self.states = sc.take(4 * D).rearrange("p (a d) -> p a d", a=4)
        self.hit = sc.take(4 * S).rearrange("p (a t) -> p a t", a=4)
        self.count = sc.take(4 * S).rearrange("p (a t) -> p a t", a=4)
        self.zeros = sc.take(S)
        self.pick = sc.take(4 * S).rearrange("p (a t) -> p a t", a=4)
        self.all_added = NT
        self.load = (Load(c, "a").add(c.C[:], d["ctx_pairs"])
                     .add(self.lens[:], d["patch_lens"])
                     .add(self.g_init, d["L0_xattn_g_init"][0:D].partition_broadcast(P))
                     .add(self.g_res[:], d["L0_xattn_g_res"])
                     .add(self.WinT[:], d["L0_xattn_W_in"])
                     .add(self.b_in[:], d["L0_xattn_b_in"][None, :]))
        self.own = c.dve_chain
        self.s = c.signals("a", "mean_square patch_eps patch_rstd patches scanned states lengths ends "
                                "hits counted picks product added")

    def dve(self, v):
        c, s, own, sm = self.c, self.s, self.own, self.small
        v.wait_ge(c.constants_done, 1)
        own.link(v, v.tensor_scalar(c.decayT[:], c.ident[:], KEEP, None, ALU.mult))
        own.link(v, v.tensor_tensor_scan(c.decayT[:], c.decay[:], c.decayT[:], 0.0, ALU.mult, ALU.add))
        own.link(v, v.memset(c.decayT[0:64, 64:128], 0.0))
        self.load.wait(v)
        own.link(v, v.tensor_copy(sm[:, 0, :], self.lens[:]))
        v.tensor_scalar(self.Wg[:], self.WinT[:], self.g_res[:, 0:1], None, ALU.mult) \
            .then_inc(s["lengths"], 1)
        v.wait_ge(s["patch_rstd"], 1)
        for a in range(4):
            v.scalar_tensor_tensor(self.hp[:, a, :], c.C[:, a, 0:D], sm[:, 6, a:a + 1], self.g_init,
                                   ALU.mult, ALU.mult).then_inc(s["patches"], 1)
        v.wait_ge(s["ends"], 1)
        own.link(v, v.tensor_scalar(sm[:, 1, :], c.bank[4][:, 0:4], -1.0, None, ALU.add))
        own.link(v, v.tensor_scalar(sm[:, 2, :], sm[:, 1, :], 0.0, float(S), ALU.is_lt, ALU.mult))
        own.link(v, v.tensor_tensor(sm[:, 3, :], sm[:, 1, :], sm[:, 2, :], ALU.add))
        for a in range(4):
            v.tensor_scalar(self.hit[:, a, :], c.column[:], sm[:, 3, a:a + 1], None, ALU.is_equal) \
                .then_inc(s["hits"], 1)
        own.link(v, v.memset(self.zeros, 0.0))
        v.wait_ge(s["counted"], 1)
        for k in range(2):
            own.link(v, v.tensor_scalar(self.count[:, 2 * k:2 * k + 2, :].rearrange("p a t -> p (a t)"),
                                        c.bank[4 + k][:, :], 1.0, None, ALU.min))
        for a in range(4):
            own.link(v, v.tensor_tensor_scan(self.count[:, a, :], self.count[:, a, :], self.zeros, 0.0,
                                             ALU.add, ALU.add))
        own.link(v, v.tensor_scalar(self.count[:, :, :], self.count[:, :, :], -1.0, 0.0, ALU.add, ALU.max))
        v.tensor_scalar(self.pick[:, :, :], self.count[:, :, :], float(SC - 1), c.row64[:, 0:1],
                        ALU.min, ALU.is_equal).then_inc(s["picks"], 1)
        self.norm.dve(v)
        for j in range(NT):
            v.wait_ge(s["product"], j // 2 + 1)
            v.scalar_tensor_tensor(c.X[:, j, :], c.bank[j // 2 % 4][:, (j % 2) * D:(j % 2 + 1) * D],
                                   c.gates[:, 0:1], c.X[:, j, :], ALU.mult, ALU.add) \
                .then_inc(s["added"], 1)
            if j % GROUP == GROUP - 1 and self.next is not None:
                v.wait_ge(s["added"], j + 1)
                self.next.norm.stats(v, j // GROUP)

    def pool(self, g):
        c, s, sm = self.c, self.s, self.small
        g.wait_ge(s["mean_square"], 4)
        g.tensor_scalar(sm[:, 5, :], sm[:, 4, :], 1.0 / DC, EPS, ALU.mult, ALU.add) \
            .then_inc(s["patch_eps"], 1)
        g.wait_ge(s["patch_eps"], 1)
        g.tensor_tensor(sm[:, 6, :], sm[:, 5, :], c.minus_half[:, 0:4], ALU.pow) \
            .then_inc(s["patch_rstd"], 1)
        self.norm.pool(g)

    def act(self, a):
        c, s, sm = self.c, self.s, self.small
        c.gate_load.wait(a)
        a.activation(c.gates[:], c.gates_in[:], ACT.Tanh).then_inc(c.gates_done, 1)
        self.load.wait(a)
        for k in range(4):
            if k:
                a.wait_ge(s["mean_square"], k)
            a.activation(self.square, c.C[:, k, :], ACT.Square, accum_out=sm[:, 4, k:k + 1]) \
                .then_inc(s["mean_square"], 1)
        a.wait_ge(s["scanned"], 1)
        a.activation(self.states[:, :, :].rearrange("p a d -> p (a d)"), c.bank[5][:, :], ACT.Copy) \
            .then_inc(s["states"], 1)
        self.norm.act(a)

    def pe(self, t):
        c, s = self.c, self.s
        t.wait_ge(c.constants_done, 1)
        t.wait_ge(s["lengths"], 1)
        t.matmul(c.bank[4][:, 0:4], c.half_upto[:], self.small[:, 0, :], start=True, stop=True) \
            .then_inc(s["ends"], 1)
        t.wait_ge(s["patches"], 4)
        t.matmul(c.bank[5][:, :], c.decayT[:], self.hp[:, :, :].rearrange("p a d -> p (a d)"),
                 start=True, stop=False)
        for a in range(4):
            last = t.matmul(c.bank[5][:, a * D:(a + 1) * D], c.ones[0:1, :], self.b_in[0:1, :], start=False,
                            stop=(a == 3))
        last.then_inc(s["scanned"], 1)
        t.wait_ge(s["states"], 1)
        t.wait_ge(s["hits"], 4)
        for k in range(2):
            last = t.matmul(c.bank[4 + k][:, :], c.half_ones[:],
                            self.hit[:, 2 * k:2 * k + 2, :].rearrange("p a t -> p (a t)"),
                            start=True, stop=True)
        last.then_inc(s["counted"], 1)
        self.norm.pe(t)
        t.wait_ge(s["picks"], 1)
        for b in range(B):
            h = slice(64 * (b % 2), 64 * (b % 2) + 64)
            self.norm.turn.wait(t, b // 2 + 1)
            if b >= 4:
                t.wait_ge(s["added"], 2 * (b - 4) + 2)
            for i in range(2):
                j = 2 * b + i
                out = c.bank[b % 4][:, i * D:(i + 1) * D]
                t.matmul(out, c.XT[:, j * P:(j + 1) * P], self.Wg[:], start=True, stop=False)
                last = t.matmul(out, self.pick[h, b // 2, i * P:(i + 1) * P], self.states[h, b // 2, :],
                                start=False, stop=True)
            last.then_inc(s["product"], 1)


class Routing:

    def __init__(self, c):
        self.c = c
        self.small = c.sb("routing_small", [P, 16, NT])
        self.wide = c.sb("routing_wide", [P, 8, NT, E])

    def rows(self, k):
        return self.small[:, k, :]

    def table(self, k):
        return self.wide[:, k, :, :]

    def first(self, v, own, values, biggest, onehot, index):
        c, shape, tmp = self.c, (P, NT, E), self.table(7)
        place = bc(c.expert_m8[:, None, :], shape)
        own.link(v, v.tensor_reduce(biggest, values, AX.X, ALU.max))
        own.link(v, v.tensor_tensor(tmp, values, bc(biggest[:, :, None], shape), ALU.is_ge))
        own.link(v, v.tensor_tensor(tmp, tmp, place, ALU.mult))
        own.link(v, v.tensor_reduce(index, tmp, AX.X, ALU.min))
        own.link(v, v.tensor_tensor(onehot, place, bc(index[:, :, None], shape), ALU.is_equal))

    def hide(self, v, own, values, onehot, left):
        own.link(v, v.scalar_tensor_tensor(left, onehot, -3.0e38, values, ALU.mult, ALU.add))


class Router:

    def __init__(self, c):
        c.routers += 1
        self.c, self.n = c, c.routers

    def pe(self, t, weights):
        c = self.c
        for j in range(NT):
            last = t.matmul(c.bank[0][:, j * E:(j + 1) * E], c.XT[:, j * P:(j + 1) * P], weights,
                            start=True, stop=True)
        last.then_inc(c.logits_done, 1)

    def logits(self, v):
        v.wait_ge(self.c.logits_done, self.n)
        return self.c.bank[0][:, 0:NT * E].rearrange("p (j e) -> p j e", e=E)

    def softmax(self, v, logits, prob, top):
        c, own, shape = self.c, self.c.dve_chain, (P, NT, E)
        own.link(v, v.tensor_reduce(top, logits, AX.X, ALU.max))
        v.tensor_tensor(prob, logits, bc(top[:, :, None], shape), ALU.subtract).then_inc(c.shift_done, 1)
        v.wait_ge(c.exp_done, self.n)
        own.link(v, v.tensor_reduce(top, prob, AX.X, ALU.add))
        own.link(v, v.reciprocal(top, top))
        own.link(v, v.tensor_tensor(prob, prob, bc(top[:, :, None], shape), ALU.mult))

    def act(self, a, values):
        a.wait_ge(self.c.shift_done, self.n)
        a.activation(values, values, ACT.Exp).then_inc(self.c.exp_done, 1)


class ExpertBias:

    def __init__(self, c, table, bias, arena):
        self.c, self.table, self.bias = c, table, bias
        self.turned = arena.take(P)
        self.rows = arena.take(NT * D).rearrange("p (j d) -> p j d", j=NT)
        self.before, self.products_before = 2 * c.spreads, NG * c.spreads
        c.spreads += 1

    def spread_pe(self, t):
        c = self.c
        t.matmul(c.bank[5][:, 0:D], c.spread8[:], self.bias, start=True, stop=True).then_inc(c.rows_turned, 1)

    def spread_act(self, a):
        c = self.c
        a.wait_ge(c.rows_turned, self.before + 1)
        for j in range(NT):
            last = a.activation(self.rows[:, j, :], c.bank[5][:, 0:D], ACT.Copy, scale=c.tile8[:, j:j + 1])
        last.then_inc(c.rows_copied, 1)

    def pe(self, t):
        c = self.c
        t.transpose(c.bank[4][:, 0:P], self.table.rearrange("p j e -> p (j e)"), c.ident[:]) \
            .then_inc(c.rows_turned, 1)
        t.wait_ge(c.rows_copied, self.before + 2)
        for q in range(NG):
            t.matmul(c.bank[q][:, :], self.turned, self.rows[:, GROUP * q:GROUP * q + GROUP, :]
                     .rearrange("p j d -> p (j d)"), start=True, stop=True).then_inc(c.bias_products, 1)

    def act(self, a):
        c = self.c
        a.wait_ge(c.rows_turned, self.before + 2)
        a.activation(self.turned, c.bank[4][:, 0:P], ACT.Copy).then_inc(c.rows_copied, 1)

    def dve(self, v, rows, done):
        c = self.c
        for q in range(NG):
            v.wait_ge(c.bias_products, self.products_before + q + 1)
            j = GROUP * q
            v.tensor_tensor(rows[:, j:j + GROUP, :], rows[:, j:j + GROUP, :],
                            c.bank[q][:, :].rearrange("p (j d) -> p j d", d=D), ALU.add).then_inc(done, 1)


class ExpertPairStage:

    def __init__(self, c):
        self.c = c
        sc, d = c.scratch(), c.d
        self.norm = Norm(c, c.X, c.XN, 1.0, EPS, c.XT)
        ar = Arena(c.arena_tensor, 10240)
        self.w1 = ar.take(E * 256).rearrange("p (e f) -> p e f", e=E)
        self.w2 = ar.take(E * 256).rearrange("p (e f) -> p e f", e=E)
        self.wg = ar.take(E * 512).rearrange("p (e k f) -> p e k f", e=E, k=2)
        self.w3 = ar.take(E * 256).rearrange("p (e k f) -> p e k f", e=E, k=2)
        self.gate_w = c.sb("b_gate_w", [P, E])
        self.gate_b = c.sb("b_gate_b", [P, E])
        self.bias = c.sb("b_bias", [P, 3, 2 * E])
        self.b3 = c.sb("b_b3", [E, D])
        self.all_added = NG + E * NT
        self.load = (Load(c, "b").add(self.gate_w[:], d["L0_ffn_gate_w"])
                     .add(self.gate_b[:], d["L0_ffn_gate_b"].partition_broadcast(P))
                     .add(self.bias[:, 0, :], d["L0_ffn_b1"]).add(self.bias[:, 1, :], d["L0_ffn_b2"])
                     .add(self.bias[:, 2, :], d["L0_ffn_bg"]).add(self.b3[:], d["L0_ffn_b3"]))
        self.expert_load = []
        for q in range(2):
            four = slice(4 * q, 4 * q + 4)
            load = (Load(c, f"b_experts{q}").add(self.w1[:, four], d["L0_ffn_w1"][four].rearrange("e h f -> h e f"))
                    .add(self.w2[:, four], d["L0_ffn_w2"][four].rearrange("e h f -> h e f")))
            for e in range(4 * q, 4 * q + 4):
                load.add(self.wg[:, e], d["L0_ffn_wg"][e].rearrange("(k h) f -> h k f", k=2))
                load.add(self.w3[:, e], d["L0_ffn_w3"][e].rearrange("(k h) f -> h k f", k=2))
            self.expert_load.append(load)
        self.x2 = sc.take(2 * 1024).rearrange("p (u k n) -> p u k n", u=2, k=2)
        self.z = sc.take(2 * 1024).rearrange("p (u k n) -> p u k n", u=2, k=2)
        self.act_out = sc.take(2 * 1024).rearrange("p (u k n) -> p u k n", u=2, k=2)
        self.own = c.dve_chain
        self.s = c.signals("b", "weights added second second_copied z third silu result")
        self.router = Router(c)
        self.bias_sum = ExpertBias(c, c.routing.table(2), self.b3[:], sc)

    def dve(self, v):
        c, s, own, r = self.c, self.s, self.own, self.c.routing
        self.norm.dve(v)
        products = self.router.logits(v)
        self.load.wait(v)
        logits, left, one, two = r.table(0), r.table(1), r.table(2), r.table(3)
        m1, m2, idx, gap, w1, w2 = (r.rows(k) for k in range(6))
        own.link(v, v.tensor_tensor(logits, products, bc(self.gate_b[:, None, :], (P, NT, E)), ALU.add))
        r.first(v, own, logits, m1, one, idx)
        r.hide(v, own, logits, one, left)
        r.first(v, own, left, m2, two, idx)
        v.tensor_tensor(gap, m2, m1, ALU.subtract).then_inc(c.shift_done, 1)
        v.wait_ge(c.exp_done, self.router.n)
        own.link(v, v.tensor_scalar(w1, gap, 1.0, None, ALU.add))
        own.link(v, v.reciprocal(w1, w1))
        own.link(v, v.tensor_tensor(w2, gap, w1, ALU.mult))
        own.link(v, v.tensor_tensor(one, one, bc(w1[:, :, None], (P, NT, E)), ALU.mult))
        own.link(v, v.tensor_tensor(two, two, bc(w2[:, :, None], (P, NT, E)), ALU.mult))
        own.link(v, v.tensor_tensor(one, one, two, ALU.add))
        v.tensor_scalar(one, one, c.gates[:, 4:5], None, ALU.mult).then_inc(s["weights"], 1)
        v.wait_ge(s["weights"], 1)
        self.bias_sum.dve(v, c.X, s["added"])

        def multiply(n):
            e = n // NG
            for k in range(2):
                v.wait_ge(s["second_copied"], 2 * n + k + 1)
                if n >= 2:
                    v.wait_ge(s["third"], n - 1)
                v.scalar_tensor_tensor(self.z[:, n % 2, k, :], c.bank[k][:, :],
                                       self.bias[:, 0, 2 * e + k:2 * e + k + 1], self.x2[:, n % 2, k, :],
                                       ALU.add, ALU.mult).then_inc(s["z"], 1)

        def add(n):
            e, q = n // NG, n % NG
            v.wait_ge(s["result"], n + 1)
            v.wait_ge(s["added"], NG + max(GROUP * (n - NG + 1), 0))
            for i in range(GROUP):
                j = GROUP * q + i
                v.scalar_tensor_tensor(c.X[:, j, :], c.bank[6 + n % 2][:, i * D:(i + 1) * D],
                                       one[:, j, e:e + 1], c.X[:, j, :], ALU.mult, ALU.add) \
                    .then_inc(s["added"], 1)
            if e == E - 1 and self.next is not None:
                v.wait_ge(s["added"], NG + GROUP * (n + 1))
                self.next.norm.stats(v, q)

        for n in range(E * NG):
            multiply(n)
            if n:
                add(n - 1)
        add(E * NG - 1)

    def pool(self, g):
        self.norm.pool(g)
        if self.next is not None:
            g.wait_ge(self.before.s["added"], self.before.all_added)
            self.next.prepare(g)

    def act(self, a):
        c, s = self.c, self.s
        self.norm.act(a)
        self.bias_sum.spread_act(a)
        self.router.act(a, c.routing.rows(3))
        self.bias_sum.act(a)
        self.load.wait(a)

        def copy_second(n):
            e = n // NG
            if n >= 2:
                a.wait_ge(s["z"], 2 * (n - 1))
            for k in range(2):
                a.wait_ge(s["second"], 2 * n + k + 1)
                a.activation(self.x2[:, n % 2, k, :], c.bank[2 + k][:, :], ACT.Identity,
                             bias=self.bias[:, 1, 2 * e + k:2 * e + k + 1]).then_inc(s["second_copied"], 1)

        def silu(n):
            e = n // NG
            if n >= 2:
                a.wait_ge(s["result"], n - 1)
            a.wait_ge(s["third"], n + 1)
            for k in range(2):
                a.activation(self.act_out[:, n % 2, k, :], c.bank[4 + k][:, :], ACT.Silu,
                             bias=self.bias[:, 2, 2 * e + k:2 * e + k + 1]).then_inc(s["silu"], 1)

        for n in range(E * NG):
            copy_second(n)
            silu(n)

    def pe(self, t):
        c, s = self.c, self.s
        self.norm.pe(t)
        self.load.wait(t)
        self.bias_sum.spread_pe(t)
        self.norm.turn.wait(t, NG)
        self.router.pe(t, self.gate_w[:])
        t.wait_ge(s["weights"], 1)
        self.bias_sum.pe(t)

        def project(n):
            e, x = n // NG, c.XT[:, (n % NG) * CHUNK:(n % NG + 1) * CHUNK]
            if n % (4 * NG) == 0:
                self.expert_load[e // 4].wait(t)
            if n == 0:
                t.wait_ge(s["added"], NG)
            else:
                t.wait_ge(s["z"], 2 * n)
            for k in range(2):
                t.matmul(c.bank[k][:, :], self.w1[:, e, k * P:(k + 1) * P], x, start=True, stop=True)
                t.matmul(c.bank[2 + k][:, :], self.w2[:, e, k * P:(k + 1) * P], x, start=True, stop=True) \
                    .then_inc(s["second"], 1)

        def third(n):
            e = n // NG
            t.wait_ge(s["z"], 2 * n + 2)
            if n:
                t.wait_ge(s["silu"], 2 * n)
            for k in range(2):
                for q in range(2):
                    last = t.matmul(c.bank[4 + k][:, :], self.wg[:, e, q, k * P:(k + 1) * P],
                                    self.z[:, n % 2, q, :], start=(q == 0), stop=(q == 1))
            last.then_inc(s["third"], 1)

        def last_product(n):
            e = n // NG
            t.wait_ge(s["silu"], 2 * n + 2)
            if n >= 2:
                t.wait_ge(s["added"], NG + GROUP * (n - 1))
            for i in range(GROUP):
                for k in range(2):
                    last = t.matmul(c.bank[6 + n % 2][:, i * D:(i + 1) * D],
                                    self.act_out[:, n % 2, k, i * P:(i + 1) * P], self.w3[:, e, k, :],
                                    start=(k == 0), stop=(k == 1))
            last.then_inc(s["result"], 1)

        project(0)
        for n in range(E * NG):
            third(n)
            if n + 1 < E * NG:
                project(n + 1)
            last_product(n)


class HeadsStage:

    H, DH = 16, 8
    SCALE = 8 ** -0.5
    KEYS = S + SC
    VW = 168

    def __init__(self, c):
        self.c, self.all_added = c, NT
        sc, d = c.scratch(), c.d
        self.norm = Norm(c, c.X, c.XN, 1.0, EPS, c.XT)
        self.Wqkv = c.sb("c_Wqkv", [P, 3 * D])
        self.Wproj = c.sb("c_Wproj", [P, D])
        self.b_proj = c.sb("c_b_proj", [P, D])
        self.load = (Load(c, "c").add(self.Wqkv[:], d["L1_xattn_w_qkv"]).add(self.Wproj[:], d["L1_xattn_w_proj"])
                     .add(self.b_proj[:], d["L1_xattn_b_proj"].partition_broadcast(P)))
        self.KM = sc.take(8 * self.KEYS).bitcast(BF16).rearrange("p (h t) -> p h t", h=16)
        more = sc.take(4 * 512)
        spare = c.XN[:, :, :].rearrange("p j n -> p (j n)")
        self.prob = [(spare if u < 4 else more)[:, (u % 4) * 512:(u % 4 + 1) * 512] for u in range(8)]
        self.prob_c = sc.take(2 * 512).rearrange("p (u n) -> p u n", u=2)
        self.QT = sc.take(1024).bitcast(BF16).rearrange("p (k t) -> p k t", k=8)
        self.AT = sc.take(512)
        self.O = sc.take(256).rearrange("p (i n) -> p i n", i=2)
        self.OT = sc.take(256)
        self.rest = sc.take(512).rearrange("p (k n c) -> p k n c", k=2, c=8)
        self.rest_c = sc.take(128)[0:64, :].rearrange("p (n c) -> p n c", c=8)
        assert sc.at >= 6 * 1024 + NT * P + P
        self.Q = sc.take(1024).bitcast(BF16).rearrange("p (n s c) -> p n s c", s=8, c=8)
        self.K = sc.take(1024).bitcast(BF16).rearrange("p (n s c) -> p n s c", s=8, c=8)
        self.KC = sc.take(512)[0:64, :].bitcast(BF16).rearrange("p (n s c) -> p n s c", s=8, c=8)
        self.V = sc.take(4 * self.VW).rearrange("p (u i n) -> p u i n", u=2, i=2)
        self.VC = sc.take(2 * self.VW).rearrange("p (u n) -> p u n", u=2)
        self.top = sc.take(32).rearrange("p (i h) -> p i h", i=2)
        self.rz = sc.take(16)
        self.s = c.signals("c", "ones_set values q_rows k_rows qkv split q_t k_t q_turned q_again masked "
                                "masked_v scores maxed st exp st_c exp_c av evac parts heads o_t o_turned product added")

    def v_rows(self, u, i):
        return self.V[:, u, i, 0:144].rearrange("p (h c) -> p h c", c=9)

    def vc_rows(self, half, u):
        return self.VC[64 * half:64 * half + 64, u, 0:144].rearrange("p (k a c) -> p k a c", a=2, c=9)[:, :, half, :]

    def split_keys(self, eng, own, rest, rows):
        n = rest.shape[1]
        for first, count in ((0, 3), (3, 2), (5, 1)):
            own.link(eng, eng.tensor_copy(rows[:, :, first:first + count, :],
                                          bc(rest[:, :, None, :], (rest.shape[0], n, count, 8))))
            if first < 5:
                own.link(eng, eng.tensor_tensor(rest, rest, rows[:, :, first, :], ALU.subtract))

    def prepare(self, g):
        c, s, own = self.c, self.s, self.c.pool_chain
        for t in (self.Q, self.K, self.KC, self.VC):
            own.link(g, g.memset(t, 0.0))
        own.link(g, g.memset(self.K[:, :, 6, 0:3], 1.0))
        own.link(g, g.memset(self.KC[:, :, 6, 0:3], 1.0))
        own.link(g, g.tensor_copy(c.ident16[:], c.ident[:]))
        for u in range(2):
            for half in range(2):
                own.link(g, g.memset(self.vc_rows(half, u)[:, :, 8], 1.0))
        g.memset(self.V, 1.0).then_inc(s["ones_set"], 1)
        g.wait_ge(s["ones_set"], 1)

    def pool(self, g):
        c, s, own = self.c, self.s, self.c.pool_chain
        self.norm.pool(g)
        c.c2_load.wait(g)
        for b in range(B):
            if b:
                g.wait_ge(s["k_t"], 2 * b)
            own.link(g, g.tensor_copy(self.rest_c, c.C2[0:64, b, 0:D].rearrange("p (h c) -> p h c", c=8)))
            self.split_keys(g, own, self.rest_c, self.KC)
            g.wait_ge(s["split"], 6 * b + 6)
            self.split_keys(g, own, self.rest[:, 1], self.K)
            g.memset(self.K[:, :, 6, 0:3], 1.0).then_inc(s["k_rows"], 1)
            g.wait_ge(s["k_rows"], b + 1)
            if b == 0:
                self.load.wait(g)
                own.link(g, g.tensor_scalar(self.b_proj[:], self.b_proj[:], c.gates[:, 1:2], None, ALU.mult))
                self.norm.wait_normed(g, NT)
                own.link(g, g.tensor_tensor(c.X[:, :, :], c.X[:, :, :], bc(self.b_proj[:, None, :], (P, NT, D)),
                                            ALU.add))
            if b >= 2:
                g.wait_ge(s["av"], 4 * (b - 1))
            for half in range(2):
                rows = c.C2[64 * half:64 * half + 64, b, D:2 * D].rearrange("p (k a c) -> p k a c", a=2, c=8)
                g.tensor_copy(self.vc_rows(half, b % 2)[:, :, 0:8], rows[:, :, half, :]).then_inc(s["values"], 1)
                g.wait_ge(s["values"], 2 * b + half + 1)

    def pe(self, t):
        c, s = self.c, self.s
        self.norm.pe(t)
        self.load.wait(t)
        bank = c.bank
        bank16 = [bank[k].bitcast(BF16) for k in range(8)]

        def project(b, i):
            self.norm.turn.wait(t, b // 2 + 1)
            if b >= 2:
                t.wait_ge(s["added"], 2 * (b - 1))
            elif b == 1:
                self.norm.turn.wait(t, NG)
            j = 2 * b + i
            t.matmul(bank[i + (6 if b else 0)][:, 0:3 * D], c.XT[:, j * P:(j + 1) * P], self.Wqkv[:],
                     start=True, stop=True).then_inc(s["qkv"], 1)

        def turn(rows, i, k, out):
            n = 16 * i + 2 * k
            return t.transpose(out, rows[:, n:n + 2, :, :].rearrange("p n s c -> p (n s c)"),
                               c.ident16[0:rows.shape[0], 0:rows.shape[0]])

        def turn_four(rows, g, out):
            for k in range(4):
                for i in range(2):
                    last = turn(rows, i, 4 * g + k, out[:, k * S + i * P:k * S + (i + 1) * P])
            return last

        def turn_context_keys(b):
            t.wait_ge(s["k_rows"], b + 1)
            if b:
                t.wait_ge(s["exp"], 16 * b - 3)
                t.wait_ge(s["exp_c"], 4 * b - 1)
            else:
                t.wait_ge(s["split"], 6)
            for k in range(8):
                turn(self.KC, 0, k, bank16[2][:, k * SC:(k + 1) * SC])
            turn_four(self.K, 0, bank16[0]).then_inc(s["k_t"], 1)

        def turn_rest(b):
            t.wait_ge(s["q_rows"], 3 * b + 1)
            if b:
                t.wait_ge(s["exp"], 16 * b - 2)
            turn_four(self.Q, 0, bank16[3]).then_inc(s["q_t"], 1)
            if b:
                t.wait_ge(s["exp_c"], 4 * b)
            turn_four(self.K, 1, bank16[1]).then_inc(s["k_t"], 1)
            if b:
                t.wait_ge(s["exp"], 16 * b - 1)
            turn_four(self.Q, 1, bank16[4]).then_inc(s["q_t"], 1)

        def scores(b, n):
            g, pair, i = n // 8, (n % 8) // 2, n % 2
            h = 8 * g + 2 * pair
            if n < 2:
                t.wait_ge(s["q_turned"], 2 * b + n + 1)
            if n == 1 and b:
                t.wait_ge(s["exp"], 16 * b)
            if n == 0:
                t.wait_ge(s["masked_v"], 2 * b + 2)
                t.wait_ge(s["masked"], 4 * b + 2)
            if n == 8:
                t.wait_ge(s["masked"], 4 * b + 4)
            if n >= 2:
                t.wait_ge(s["maxed"], 16 * b + n - 1)
            for q in range(2):
                last = t.matmul(bank[2 + 2 * (n % 2) + q][:, 0:self.KEYS], self.QT[:, 4 * g + pair, i * P:(i + 1) * P],
                                self.KM[:, h + q, :], start=True, stop=True)
            last.then_inc(s["scores"], 1)

        def turn_again(b, g):
            t.wait_ge(s["q_rows"], 3 * b + 2 + g)
            if g == 0:
                t.wait_ge(s["masked"], 4 * b + 4)
            turn_four(self.Q, g, bank16[g]).then_inc(s["q_t"], 1)

        def key_major_context(b, j):
            n = 4 * b + j
            if j >= 2:
                t.wait_ge(s["exp_c"], n - 1)
            else:
                t.wait_ge(s["q_again"], 2 * b + 2)
            for r in range(4):
                half = slice(64 * (r % 2), 64 * (r % 2) + 64)
                last = t.matmul(bank[j % 2][half, (r // 2) * S:(r // 2 + 1) * S],
                                self.KM[:, 4 * j + r, S:S + SC], self.QT[:, 2 * j + r // 2, :], start=True, stop=True)
            last.then_inc(s["st_c"], 1)

        def key_major(b, h):
            n, g = 16 * b + h, h // 8
            t.wait_ge(s["q_again"], 2 * b + 1 + g)
            if h >= 4:
                t.wait_ge(s["exp"], n - 3)
            else:
                t.wait_ge(s["maxed"], 16 * b + 16)
            for k in range(2):
                last = t.matmul(bank[2 + h % 4][:, k * S:(k + 1) * S], self.KM[:, h, k * P:(k + 1) * P],
                                self.QT[:, h // 2, :], start=True, stop=True)
            last.then_inc(s["st"], 1)

        def values(b, j):
            if j == 0:
                if b:
                    t.wait_ge(s["added"], 2 * b)
                if b + 1 < B:
                    t.wait_ge(s["split"], 6 * b + 12)
                t.wait_ge(s["values"], 2 * b + 2)
            t.wait_ge(s["exp_c"], 4 * b + j + 1)
            t.wait_ge(s["exp"], 16 * b + 4 * j + 4)
            for k in range(3):
                for r in range(4):
                    h = 4 * j + r
                    wide = slice(9 * h, 9 * h + 32)
                    out = bank[6 + j // 2][32 * r:32 * r + 32, (j % 2) * S:(j % 2 + 1) * S]
                    if k < 2:
                        t.matmul(out, self.V[:, b % 2, k, wide], self.prob[h % 8][:, k * S:(k + 1) * S],
                                 start=(k == 0), stop=False, tile_position=(0, 32 * r))
                    else:
                        last = t.matmul(out, self.VC[:, b % 2, wide],
                                        self.prob_c[:, j % 2, (r // 2) * S:(r // 2 + 1) * S],
                                        start=False, stop=True, tile_position=(0, 32 * r))
            last.then_inc(s["av"], 1)

        def turn_parts(b, half):
            t.wait_ge(s["evac"], 2 * b + half + 1)
            for n in range(4):
                last = t.transpose(bank[6 + half][:, n * P:(n + 1) * P], self.AT[:, n * P:(n + 1) * P], c.ident[:])
            last.then_inc(s["parts"], 1)

        def turn_out(b):
            t.wait_ge(s["heads"], 4 * b + 4)
            for i in range(2):
                last = t.transpose(bank[6][:, i * P:(i + 1) * P], self.O[:, i, :], c.ident[:])
            last.then_inc(s["o_t"], 1)

        def project_out(b):
            t.wait_ge(s["o_turned"], b + 1)
            for i in range(2):
                out = bank[6][:, S + i * P:S + (i + 1) * P]
                last = t.matmul(out, self.OT[:, i * P:(i + 1) * P], self.Wproj[:], start=True, stop=True)
            last.then_inc(s["product"], 1)

        t.wait_ge(s["ones_set"], 1)
        project(0, 0)
        project(0, 1)
        turn_context_keys(0)
        turn_rest(0)
        for b in range(B):
            for n in range(16):
                scores(b, n)
                if b and n == 0:
                    turn_parts(b - 1, 1)
                if b and n == 4:
                    turn_out(b - 1)
                if b and n == 6:
                    project_out(b - 1)
                if n in (10, 12) and b + 1 < B:
                    project(b + 1, (n - 10) // 2)
                if n == 13:
                    turn_again(b, 0)
            key_major(b, 0)
            key_major(b, 1)
            turn_again(b, 1)
            key_major(b, 2)
            key_major(b, 3)
            key_major_context(b, 0)
            for j in range(1, 4):
                for h in range(4 * j, 4 * j + 4):
                    key_major(b, h)
                key_major_context(b, j)
                values(b, j - 1)
            if b + 1 < B:
                turn_context_keys(b + 1)
            turn_parts(b, 0)
            if b + 1 < B:
                turn_rest(b + 1)
            values(b, 3)
        turn_parts(B - 1, 1)
        turn_out(B - 1)
        project_out(B - 1)

    def act(self, a):
        c, s = self.c, self.s
        self.norm.act(a)
        bank = c.bank
        a.wait_ge(s["ones_set"], 1)

        def split(b):
            for i in range(2):
                a.wait_ge(s["qkv"], 2 * b + i + 1)
                rows = [bank[i + (6 if b else 0)][:, k * D:(k + 1) * D].rearrange("p (h c) -> p h c", c=8)
                        for k in range(3)]
                a.activation(self.rest[:, 0, 16 * i:16 * i + 16, :], rows[0], ACT.Copy, scale=self.SCALE) \
                    .then_inc(s["split"], 1)
                a.activation(self.rest[:, 1, 16 * i:16 * i + 16, :], rows[1], ACT.Copy).then_inc(s["split"], 1)
                a.activation(self.v_rows(b % 2, i)[:, :, 0:8], rows[2], ACT.Copy).then_inc(s["split"], 1)

        def mask(b):
            a.wait_ge(s["k_t"], 2 * b + 1)
            for q in range(2):
                a.activation(self.KM[:, q:16:2, S:S + SC],
                             bank[2].bitcast(BF16)[:, 0:512].rearrange("p (k t) -> p k t", t=SC), ACT.Copy,
                             scale=c.parity[:, q:q + 1]).then_inc(s["masked"], 1)
            a.wait_ge(s["k_t"], 2 * b + 2)
            for q in range(2):
                a.activation(self.KM[:, 8 + q:16:2, 0:S],
                             bank[1].bitcast(BF16)[:, :].rearrange("p (k t) -> p k t", t=S), ACT.Copy,
                             scale=c.parity[:, q:q + 1]).then_inc(s["masked"], 1)

        def copy_again(b, g):
            a.wait_ge(s["q_t"], 4 * b + 3 + g)
            a.activation(self.QT[:, 4 * g:4 * g + 4, :],
                         bank[g].bitcast(BF16)[:, :].rearrange("p (k t) -> p k t", t=S), ACT.Copy) \
                .then_inc(s["q_again"], 1)

        def copy_out(b):
            a.wait_ge(s["o_t"], b + 1)
            a.activation(self.OT, bank[6][:, 0:S], ACT.Copy).then_inc(s["o_turned"], 1)

        def exp_context(b, j):
            n = 4 * b + j
            a.wait_ge(s["st_c"], n + 1)
            if n >= 2:
                a.wait_ge(s["av"], n - 1)
            a.activation(self.prob_c[:, n % 2, :], bank[j % 2][:, :], ACT.Exp).then_inc(s["exp_c"], 1)

        def exp_own(b, h):
            n = 16 * b + h
            a.wait_ge(s["st"], n + 1)
            if n >= 8:
                a.wait_ge(s["av"], n // 4 - 1)
            a.activation(self.prob[h % 8], bank[2 + h % 4][:, :], ACT.Exp).then_inc(s["exp"], 1)

        split(0)
        for b in range(B):
            mask(b)
            if b:
                copy_out(b - 1)
            if b + 1 < B:
                split(b + 1)
            copy_again(b, 0)
            copy_again(b, 1)
            for h in range(16):
                exp_own(b, h)
                if h % 4 == 3:
                    exp_context(b, h // 4)
        copy_out(B - 1)

    def dve(self, v):
        c, s = self.c, self.s
        self.norm.dve(v)
        bank, own = c.bank, c.dve_chain

        def split_queries(b):
            rest, rows = self.rest[:, 0], self.Q
            twice = bc(rest[:, :, None, :], (P, 32, 2, 8))
            v.wait_ge(s["split"], 6 * b + 6)
            if b:
                v.wait_ge(s["q_t"], 4 * b)
            own.link(v, v.tensor_copy(rows[:, :, 2:4, :], twice))
            own.link(v, v.tensor_copy(rows[:, :, 5, :], rest))
            own.link(v, v.tensor_tensor(rest, rest, rows[:, :, 2, :], ALU.subtract))
            own.link(v, v.tensor_copy(rows[:, :, 1:5:3, :], twice))
            own.link(v, v.tensor_tensor(rest, rest, rows[:, :, 1, :], ALU.subtract))
            own.link(v, v.tensor_copy(rows[:, :, 0, :], rest))
            v.memset(rows[:, :, 6, 0:3], 0.0).then_inc(s["q_rows"], 1)

        def next_stats(b):
            if b % 2 and self.next is not None:
                v.wait_ge(s["added"], 2 * b + 2)
                self.next.norm.stats(v, b // 2)

        def split_maxima(b, g, step):
            top = self.top[:, :, 8 * g:8 * g + 8]
            rows = self.Q[:, :, :, :].rearrange("p (i h) s c -> p i h (s c)", i=2)[:, :, 8 * g:8 * g + 8, :]
            part = rows[:, :, :, 48 + step // 2]
            if step == 0:
                v.wait_ge(s["maxed"], 16 * b + 8 * g + 8)
            else:
                v.wait_ge(own.sem, own.n)
            if step == 4:
                v.tensor_copy(part, top).then_inc(s["q_rows"], 1)
            elif step % 2 == 0:
                own.step(v.tensor_copy(part, top))
            else:
                own.step(v.tensor_tensor(top, top, part, ALU.subtract))

        def copy_queries(b):
            for g in range(2):
                if g == 1:
                    for q in range(2):
                        v.wait_ge(s["k_t"], 2 * b + 1)
                        v.tensor_scalar(self.KM[:, q:8:2, 0:S],
                                        bank[0].bitcast(BF16)[:, :].rearrange("p (k t) -> p k t", t=S),
                                        c.parity[:, q:q + 1], None, ALU.mult).then_inc(s["masked_v"], 1)
                v.wait_ge(s["q_t"], 4 * b + 1 + g)
                v.tensor_copy(self.QT[:, 4 * g:4 * g + 4, :],
                              bank[3 + g].bitcast(BF16)[:, :].rearrange("p (k t) -> p k t", t=S)) \
                    .then_inc(s["q_turned"], 1)

        def maxima(b, n):
            g, pair, i = n // 8, (n % 8) // 2, n % 2
            k, h = 2 + 2 * (n % 2), 8 * g + 2 * pair
            v.wait_ge(s["scores"], 16 * b + n + 1)
            v.tensor_reduce(self.top[:, i, h:h + 2], c.psum[:, k:k + 2, 0:self.KEYS], AX.X, ALU.max,
                            negate=True).then_inc(s["maxed"], 1)

        def take_parts(b, half):
            v.wait_ge(s["parts"], 2 * b + half + 1)
            turned = bank[6 + half]
            c.dve_chain.link(v, v.reciprocal(self.rz, turned.rearrange("p (n k) -> p n k", k=32)[:, :, 8]))
            if b and half == 0:
                v.wait_ge(s["o_t"], b)
            for j in range(2):
                parts = turned[:, j * S:(j + 1) * S].rearrange("p (i r k) -> p i r k", i=2, r=4)
                at = 64 * half + 32 * j
                rz = self.rz[:, 8 * j:8 * j + 8].rearrange("p (i r) -> p i r", i=2)
                v.tensor_tensor(self.O[:, :, at:at + 32].rearrange("p i (r k) -> p i r k", r=4), parts[:, :, :, 0:8],
                                bc(rz[:, :, :, None], (P, 2, 4, 8)), ALU.mult).then_inc(s["heads"], 1)

        def evacuate(b, half):
            v.wait_ge(s["av"], 4 * b + 2 * half + 2)
            if b or half:
                v.wait_ge(s["parts"], 2 * b + half)
            v.tensor_copy(self.AT, bank[6 + half][:, :]).then_inc(s["evac"], 1)

        def add(b):
            v.wait_ge(s["product"], b + 1)
            v.wait_ge(s["values"], 1)
            for i in range(2):
                j = 2 * b + i
                v.scalar_tensor_tensor(c.X[:, j, :], bank[6][:, S + i * P:S + (i + 1) * P],
                                       c.gates[:, 1:2], c.X[:, j, :], ALU.mult, ALU.add).then_inc(s["added"], 1)

        v.wait_ge(s["ones_set"], 1)
        split_queries(0)
        for b in range(B):
            copy_queries(b)
            if b:
                evacuate(b - 1, 1)
            for n in range(16):
                maxima(b, n)
                if b and n == 1:
                    take_parts(b - 1, 1)
                if b and n == 7:
                    add(b - 1)
                if 7 <= n < 12:
                    split_maxima(b, 0, n - 7)
            for step in range(5):
                split_maxima(b, 1, step)
            if b + 1 < B:
                split_queries(b + 1)
            evacuate(b, 0)
            take_parts(b, 0)
            if b:
                next_stats(b - 1)
        evacuate(B - 1, 1)
        take_parts(B - 1, 1)
        add(B - 1)
        next_stats(B - 1)


class AcrossStage:

    HEADS, DH, T = 16, 8, 8
    SCALE = 8 ** -0.5
    POOL_SCORES, POOL_VALUES = (0, 2, 4, 5, 7), (1, 4, 7)

    def __init__(self, c):
        self.c, self.all_added = c, NG
        sc, d = c.scratch(), c.d
        self.norm = Norm(c, c.X, c.XN, 1.0, EPS, c.XT)
        self.Win = c.sb("d_Win", [P, 3 * D])
        self.Wout = c.sb("d_Wout", [P, D])
        self.b_in = c.sb("d_b_in", [P, 3 * D])
        self.b_out = c.sb("d_b_out", [P, D])
        self.affine = c.sb("d_affine", [P, 4, D])
        self.router_w = c.sb("d_router_w", [P, E])
        self.router_b = c.sb("d_router_b", [P, E])
        self.b1 = c.sb("d_b1", [P, E])
        self.b2 = c.sb("d_b2", [E, D])
        self.w1 = c.late[:, 0:1024].rearrange("p (e n) -> p e n", e=E)
        self.w2 = c.late[:, 1024:2048].rearrange("p (e n) -> p e n", e=E)
        self.load = (Load(c, "d").add(self.Win[:], d["L1_ffn_in_proj_w"]).add(self.Wout[:], d["L1_ffn_out_w"])
                     .add(self.b_in[:], d["L1_ffn_in_proj_b"].partition_broadcast(P))
                     .add(self.b_out[:], d["L1_ffn_out_b"].partition_broadcast(P))
                     .add(self.affine[:, 0, :], d["L1_ffn_ln1_g"].partition_broadcast(P))
                     .add(self.affine[:, 1, :], d["L1_ffn_ln1_b"].partition_broadcast(P))
                     .add(self.affine[:, 2, :], d["L1_ffn_ln2_g"].partition_broadcast(P))
                     .add(self.affine[:, 3, :], d["L1_ffn_ln2_b"].partition_broadcast(P))
                     .add(self.router_w[:], d["L1_ffn_router_w"])
                     .add(self.router_b[:], d["L1_ffn_router_b"].partition_broadcast(P))
                     .add(self.b1[:], d["L1_ffn_b1"]).add(self.b2[:], d["L1_ffn_b2"])
                     .add(self.w1, d["L1_ffn_w1"]).add(self.w2, d["L1_ffn_w2"]))
        self.qkv = sc.take(16 * 384).rearrange("p (n k) -> p n k", n=16)
        self.prod = sc.take(4 * 1024).rearrange("p (u n) -> p u n", u=4)
        self.score = sc.take(2048).rearrange("p (m t s h) -> p m t s h", m=2, t=8, s=8)
        self.top = sc.take(256).rearrange("p (m t h) -> p m t h", m=2, t=8)
        sc2 = c.scratch()
        self.hidden = sc2.take(2 * 512).rearrange("p (u n) -> p u n", u=2)
        self.own = c.dve_chain
        self.dve_values = [t for t in range(8) if t not in self.POOL_VALUES]
        self.dve_order = [8 * m + t for m in range(2) for t in self.dve_values]
        self.s = c.signals("d", "qkv qkv_first copied prod scored shifted exp attn prod_v prod_w reduced out residual "
                                "h_affine pick "
                                "hidden gelu result moe added")
        self.ln1 = Norm(c, c.XN, c.XN)
        self.h_turn = Turn(c, c.XN, c.XT, self.s["h_affine"], 1)
        self.router = Router(c)
        self.bias_sum = ExpertBias(c, c.routing.table(2), self.b2[:], sc2)
        self.ln2 = Norm(c, c.XN, c.XN)

    def score_products(self, eng, m, t, u):
        q = bc(self.qkv[:, 8 * m + t, 0:D][:, None, :], (P, 8, D))
        return eng.tensor_tensor(self.prod[:, u, :].rearrange("p (s n) -> p s n", s=8), q,
                                 self.qkv[:, 8 * m:8 * m + 8, D:2 * D], ALU.mult)

    def value_products(self, eng, m, t, u):
        w = bc(self.score[:, m, t, :, :][:, :, :, None], (P, 8, 16, 8))
        return eng.tensor_tensor(self.prod[:, u, :].rearrange("p (s h c) -> p s h c", s=8, c=8), w,
                                 self.qkv[:, 8 * m:8 * m + 8, 2 * D:3 * D].rearrange("p s (h c) -> p s h c", c=8),
                                 ALU.mult)

    def pool(self, g):
        c, s = self.c, self.s
        self.norm.pool(g)
        self.load.wait(g)
        self.norm.turn.wait(g, NG)
        c.pool_chain.link(g, g.tensor_tensor(c.XN[:, :, :], c.XN[:, :, :], bc(self.b_out[:, None, :], (P, NT, D)),
                                             ALU.add))
        done = []
        for m in range(2):
            g.wait_ge(s["copied" if m else "qkv_first"], 8)
            for t in self.POOL_SCORES:
                if len(done) >= 2:
                    g.wait_ge(s["scored"], done[-2] + 1)
                self.score_products(g, m, t, len(done) % 2).then_inc(s["prod"], 1)
                done.append(8 * m + t)
        g.wait_ge(s["scored"], 16)
        done = []
        for m in range(2):
            g.wait_ge(s["attn"], m + 1)
            for t in self.POOL_VALUES:
                if len(done) >= 2:
                    g.wait_ge(s["reduced"], done[-2] + 1)
                self.value_products(g, m, t, len(done) % 2).then_inc(s["prod_v"], 1)
                done.append(8 * m + t)
        self.ln1.pool(g)
        g.wait_ge(s["reduced"], 16)
        if self.next is not None:
            self.next.prepare(g)
        shift = self.affine[:, 3, :]
        own = c.pool_chain
        own.link(g, g.tensor_scalar(shift, shift, c.gates[:, 5:6], None, ALU.mult))
        own.link(g, g.tensor_tensor(c.X[:, :, :], c.X[:, :, :], bc(shift[:, None, :], (P, NT, D)), ALU.add))
        self.ln2.pool(g)

    def dve(self, v):
        c, s, own, r = self.c, self.s, self.own, self.c.routing
        self.norm.dve(v)
        self.load.wait(v)
        for t in range(8):
            v.wait_ge(s["qkv"], t + 1)
            v.tensor_tensor(self.qkv[:, t, :], c.bank[t % 4][:, 0:3 * D], self.b_in[:, :], ALU.add) \
                .then_inc(s["qkv_first"], 1)
        own.link(v, v.tensor_scalar(self.affine[:, 2, :], self.affine[:, 2, :], c.gates[:, 5:6], None, ALU.mult))

        made = []

        def scores(m):
            for t in range(8):
                n = 8 * m + t
                if t in self.POOL_SCORES:
                    k = len(self.POOL_SCORES) * m + self.POOL_SCORES.index(t)
                    u = k % 2
                    v.wait_ge(s["prod"], k + 1)
                else:
                    u = 2 + len(made) % 2
                    if len(made) >= 2:
                        v.wait_ge(s["scored"], made[-2] + 1)
                    made.append(n)
                    own.link(v, self.score_products(v, m, t, u))
                v.tensor_reduce(self.score[:, m, t, :, :].rearrange("p s h -> p (s h)"),
                                self.prod[:, u, :].rearrange("p (n c) -> p n c", c=8), AX.X, ALU.add) \
                    .then_inc(s["scored"], 1)

        def parts(m):
            return (self.score[:, m], self.score[:, m].rearrange("p t s h -> p t h s"), self.top[:, m],
                    bc(self.top[:, m][:, :, None, :], (P, 8, 8, 16)))

        def shift(m):
            score, over_s, top, spread = parts(m)
            v.wait_ge(s["scored"], 8 * m + 8)
            own.link(v, v.tensor_reduce(top, over_s, AX.X, ALU.max))
            v.tensor_tensor(score, score, spread, ALU.subtract).then_inc(s["shifted"], 1)

        def divide(m):
            score, over_s, top, spread = parts(m)
            v.wait_ge(s["exp"], m + 1)
            own.link(v, v.tensor_reduce(top, over_s, AX.X, ALU.add))
            own.link(v, v.reciprocal(top, top))
            v.tensor_tensor(score, score, spread, ALU.mult).then_inc(s["attn"], 1)

        def values(m):
            v.wait_ge(s["attn"], m + 1)
            for t in self.dve_values:
                k = len(self.dve_values) * m + self.dve_values.index(t)
                if k >= 2:
                    v.wait_ge(s["reduced"], self.dve_order[k - 2] + 1)
                self.value_products(v, m, t, 2 + k % 2).then_inc(s["prod_w"], 1)

        scores(0)
        shift(0)
        v.wait_ge(s["copied"], 8)
        scores(1)
        divide(0)
        shift(1)
        values(0)
        divide(1)
        values(1)
        v.wait_ge(s["prod"], 1)
        for q in range(NG):
            v.wait_ge(s["out"], q + 1)
            tiles = c.XN[:, GROUP * q:GROUP * q + GROUP, :]
            v.tensor_tensor(tiles, tiles, c.bank[q][:, :].rearrange("p (j d) -> p j d", d=D), ALU.add) \
                .then_inc(s["residual"], 1)
            v.wait_ge(s["residual"], q + 1)
            self.ln1.stats(v, q)
        self.ln1.dve(v)
        self.scale_shift(v, self.ln1, 0, s["h_affine"])

        products = self.router.logits(v)
        logits, left, one, two = (r.table(k) for k in range(4))
        m1, m2, i1, i2 = (r.rows(k) for k in range(4))
        shape = (P, NT, E)
        own.link(v, v.tensor_tensor(logits, products, bc(self.router_b[:, None, :], shape), ALU.add))
        self.router.softmax(v, logits, logits, m1)
        r.first(v, own, logits, m1, one, i1)
        r.hide(v, own, logits, one, left)
        r.first(v, own, left, m2, two, i2)
        own.link(v, v.tensor_tensor(i1, i1, i2, ALU.max))
        v.tensor_tensor(one, bc(c.expert_m8[:, None, :], shape), bc(i1[:, :, None], shape), ALU.is_equal) \
            .then_inc(s["pick"], 1)
        v.wait_ge(s["pick"], 1)
        self.bias_sum.dve(v, c.XN, s["moe"])
        for n in range(E * NG):
            e, q = n // NG, n % NG
            v.wait_ge(s["result"], n + 1)
            v.wait_ge(s["moe"], NG + max(GROUP * (n - NG + 1), 0))
            for i in range(GROUP):
                j = GROUP * q + i
                v.scalar_tensor_tensor(c.XN[:, j, :], c.bank[2 + n % 2][:, i * D:(i + 1) * D],
                                       one[:, j, e:e + 1], c.XN[:, j, :], ALU.mult, ALU.add) \
                    .then_inc(s["moe"], 1)
            if e == E - 1:
                v.wait_ge(s["moe"], NG + GROUP * (n + 1))
                self.ln2.stats(v, q)
        for q in range(NG):
            self.ln2.add_to(v, q, self.affine[:, 2, :], c.X, s["added"])
            if self.next is not None:
                v.wait_ge(s["added"], q + 1)
                self.next.norm.stats(v, q)

    def scale_shift(self, v, norm, k, done):
        for q in range(NG):
            tiles = self.c.XN[:, GROUP * q:GROUP * q + GROUP, :]
            norm.wait_normed(v, GROUP * q + GROUP)
            self.own.link(v, v.tensor_tensor(tiles, tiles, bc(self.affine[:, k, :][:, None, :], (P, GROUP, D)),
                                             ALU.mult))
            v.tensor_tensor(tiles, tiles, bc(self.affine[:, k + 1, :][:, None, :], (P, GROUP, D)), ALU.add) \
                .then_inc(done, 1)

    def act(self, a):
        c, s = self.c, self.s
        self.norm.act(a)
        for n in range(8, 16):
            a.wait_ge(s["qkv"], n + 1)
            a.activation(self.qkv[:, n, :], c.bank[n % 4][:, 0:3 * D], ACT.Copy).then_inc(s["copied"], 1)
        for m in range(2):
            a.wait_ge(s["shifted"], m + 1)
            a.activation(self.score[:, m], self.score[:, m], ACT.Exp, scale=self.SCALE).then_inc(s["exp"], 1)
        for q in range(NG):
            a.wait_ge(s["reduced"], 8 + 2 * q + 2)
            a.activation(c.XT[:, q * CHUNK:(q + 1) * CHUNK], c.bank[4 + q][:, :], ACT.Copy) \
                .then_inc(s["copied"], 1)
        self.h_turn.act(a)
        self.bias_sum.spread_act(a)
        self.router.act(a, c.routing.table(0))
        self.bias_sum.act(a)
        for n in range(E * NG):
            if n >= 2:
                a.wait_ge(s["result"], n - 1)
            a.wait_ge(s["hidden"], n + 1)
            a.activation(self.hidden[:, n % 2, :], c.bank[4 + n % 2][:, :], ACT.Gelu,
                         bias=self.b1[:, n // NG:n // NG + 1]).then_inc(s["gelu"], 1)

    def pe(self, t):
        c, s = self.c, self.s
        self.norm.pe(t)
        self.load.wait(t)
        self.norm.turn.wait(t, NG)
        for n in range(NT):
            j, m = 2 * (n % 8) + n // 8, n // 8
            if 4 <= n < 12:
                t.wait_ge(s["qkv_first"], n - 3)
            elif n >= 12:
                t.wait_ge(s["copied"], n - 11)
            out = c.bank[n % 4][:, 0:3 * D]
            last = t.matmul(out, c.XT[:, j * P:(j + 1) * P], self.Win[:], start=True, stop=(m == 0))
            if m:
                last = t.matmul(out, c.ones[0:1, :], self.b_in[0:1, :], start=False, stop=True)
            last.then_inc(s["qkv"], 1)
        for m in range(2):
            for r in range(8):
                j = 2 * r + m
                if r in self.POOL_VALUES:
                    k = len(self.POOL_VALUES) * m + self.POOL_VALUES.index(r)
                    u = k % 2
                    t.wait_ge(s["prod_v"], k + 1)
                else:
                    k = len(self.dve_values) * m + self.dve_values.index(r)
                    u = 2 + k % 2
                    t.wait_ge(s["prod_w"], k + 1)
                for i in range(8):
                    last = t.matmul(c.bank[4 + j // 4][:, (j % 4) * P:(j % 4 + 1) * P],
                                    self.prod[:, u, i * D:(i + 1) * D], c.ident[:], start=(i == 0), stop=(i == 7))
                last.then_inc(s["reduced"], 1)
        t.wait_ge(s["copied"], 8)
        for j in range(NT):
            t.wait_ge(s["copied"], 8 + j // GROUP + 1)
            last = t.matmul(c.bank[j // 4][:, (j % 4) * D:(j % 4 + 1) * D], c.XT[:, j * P:(j + 1) * P],
                            self.Wout[:], start=True, stop=True)
            if j % 4 == 3:
                last.then_inc(s["out"], 1)
        self.h_turn.pe(t)
        self.bias_sum.spread_pe(t)
        self.h_turn.wait(t, NG)
        self.router.pe(t, self.router_w[:])
        t.wait_ge(s["pick"], 1)
        self.bias_sum.pe(t)

        def first(n):
            e, x = n // NG, c.XT[:, (n % NG) * CHUNK:(n % NG + 1) * CHUNK]
            if n >= 2:
                t.wait_ge(s["gelu"], n - 1)
            t.matmul(c.bank[4 + n % 2][:, :], self.w1[:, e, :], x, start=True, stop=True) \
                .then_inc(s["hidden"], 1)

        def second(n):
            e = n // NG
            t.wait_ge(s["gelu"], n + 1)
            t.wait_ge(s["moe"], NG + GROUP * max(n - 1, 0))
            for i in range(GROUP):
                last = t.matmul(c.bank[2 + n % 2][:, i * D:(i + 1) * D],
                                self.hidden[:, n % 2, i * P:(i + 1) * P], self.w2[:, e, :],
                                start=True, stop=True)
            last.then_inc(s["result"], 1)

        first(0)
        for n in range(E * NG):
            if n + 1 < E * NG:
                first(n + 1)
            second(n)


class MaskedStage:

    H, DH = 8, 16
    SCALE = 16 ** -0.5

    def __init__(self, c):
        self.c, self.all_added = c, NT
        sc, d = c.scratch(), c.d
        self.norm = Norm(c, c.X, c.XN, 1.0, EPS, c.XT)
        self.shift = c.sb("e_shift", [P, 1])
        self.mask_in = c.sb("e_mask_in", [P, B * SC], I32)
        self.load = (Load(c, "e").add(self.shift[:], d["L2_xattn_b"].partition_broadcast(P))
                     .add(self.mask_in[:], d["seq_mask"].partition_broadcast(P))
                     .add(c.CT[:], d["ctx_T"]))
        sc.take(3200)
        self.keys = sc.take(B * 512).rearrange("p (b h k) -> p b h k", b=B, h=8)
        self.vals = sc.take(B * 136).rearrange("p (b h n) -> p b h n", b=B, h=8)
        self.mask = sc.take(B * SC)
        self.prob = sc.take(3 * 512).rearrange("p (u n) -> p u n", u=3)
        self.probT = sc.take(2 * 512).rearrange("p (u n) -> p u n", u=2)
        self.top = sc.take(2 * 8).rearrange("p (u h) -> p u h", u=2)
        self.rz = sc.take(8)
        self.part = sc.take(D)
        self.head = sc.take(8)
        self.own, self.own_pool = c.dve_chain, c.pool_chain
        self.s = c.signals("e", "operands scores biased topped shifted exp p_t p_turned av added")

    @property
    def helped(self):
        return self.next.next if self.next is not None else None

    def pool(self, g):
        if self.helped is not None:
            g.wait_ge(self.before.s["added"], self.before.all_added)
            self.helped.zero_others(g, self.helped.kv_keys)
        self.norm.pool(g)

    def prepare(self, g):
        c, s, own = self.c, self.s, self.own_pool
        self.load.wait(g)
        c.c2_load.wait(g)
        own.link(g, g.tensor_scalar(self.head, c.head16[:], self.SCALE, None, ALU.mult))
        own.link(g, g.tensor_copy(self.mask, self.mask_in[:]))
        own.link(g, g.tensor_scalar(self.mask, self.mask, -1.0, 1.0e30, ALU.add, ALU.mult))
        for b in range(B):
            own.link(g, g.tensor_tensor(self.keys[:, b, :, :], bc(c.CT[:, 0, b * SC:(b + 1) * SC][:, None, :], (P, 8, SC)),
                                        bc(self.head[:, :, None], (P, 8, SC)), ALU.mult))
            own.link(g, g.tensor_tensor(self.vals[:, b, :, 0:16],
                                        c.C2[:, b, D:2 * D].rearrange("p (h n) -> p h n", h=8),
                                        bc(c.parity[:, :, None], (P, 8, 16)), ALU.mult))
            g.tensor_copy(self.vals[:, b, :, 16], c.parity[:]).then_inc(s["operands"], 1)

    def dve(self, v):
        c, s, own = self.c, self.s, self.own
        self.norm.dve(v)
        v.wait_ge(s["operands"], B)
        self.load.wait(v)

        def tile(j):
            return self.prob[:, j % 3, :].rearrange("p (h k) -> p h k", h=8)

        def bias(j):
            v.wait_ge(s["scores"], j + 1)
            if j >= 3:
                v.wait_ge(s["p_t"], j - 2)
            keys = slice(j // 2 * SC, (j // 2 + 1) * SC)
            v.scalar_tensor_tensor(tile(j), c.bank[j % 2][:, :].rearrange("p (h k) -> p h k", h=8),
                                   self.shift[:, 0:1], bc(self.mask[:, keys][:, None, :], (P, 8, SC)),
                                   ALU.add, ALU.add).then_inc(s["biased"], 1)

        def largest(j):
            v.wait_ge(s["biased"], j + 1)
            v.tensor_reduce(self.top[:, j % 2, :], tile(j), AX.X, ALU.max).then_inc(s["topped"], 1)

        def subtract(j):
            v.wait_ge(s["topped"], j + 1)
            v.tensor_tensor(tile(j), tile(j), bc(self.top[:, j % 2, :][:, :, None], (P, 8, SC)), ALU.subtract) \
                .then_inc(s["shifted"], 1)

        def invert(j):
            v.wait_ge(s["av"], j + 1)
            return own.step(v.reciprocal(self.rz, self.products(j)[:, :, 16]))

        def gate(inverted):
            v.wait_ge(own.sem, inverted)
            return own.step(v.tensor_scalar(self.rz, self.rz, c.gates[:, 2:3], None, ALU.mult))

        def divide(j, gated):
            v.wait_ge(own.sem, gated)
            return own.step(v.tensor_tensor(self.part.rearrange("p (h n) -> p h n", h=8), self.products(j)[:, :, 0:16],
                                            bc(self.rz[:, :, None], (P, 8, 16)), ALU.mult))

        def add(j, divided):
            v.wait_ge(own.sem, divided)
            v.tensor_tensor(c.X[:, j, :], c.X[:, j, :], self.part, ALU.add).then_inc(s["added"], 1)
            if j % GROUP == GROUP - 1 and self.next is not None:
                v.wait_ge(s["added"], j + 1)
                self.next.norm.stats(v, j // GROUP)

        for j in range(2):
            bias(j)
            largest(j)
            subtract(j)
        divided = None
        for j in range(NT + 1):
            soft, done = j + 2 < NT, j >= 1
            if soft:
                bias(j + 2)
            if divided is not None:
                add(j - 2, divided)
            if done:
                inverted = invert(j - 1)
            if soft:
                largest(j + 2)
            if done:
                gated = gate(inverted)
            if soft:
                subtract(j + 2)
            if done:
                divided = divide(j - 1, gated)
        add(NT - 1, divided)

    def products(self, j):
        return self.c.bank[4 + j % 2][:, 0:136].rearrange("p (h n) -> p h n", h=8)

    def act(self, a):
        c, s = self.c, self.s
        self.norm.act(a)

        def exponentials(j):
            a.wait_ge(s["shifted"], j + 1)
            a.activation(self.prob[:, j % 3, :], self.prob[:, j % 3, :], ACT.Exp).then_inc(s["exp"], 1)

        exponentials(0)
        for j in range(NT):
            u = j % 2
            if j + 1 < NT:
                exponentials(j + 1)
            a.wait_ge(s["p_t"], j + 1)
            if j >= 2:
                a.wait_ge(s["av"], j - 1)
            a.activation(self.probT[:, u, :], c.bank[2 + u][:, :], ACT.Copy).then_inc(s["p_turned"], 1)
            if self.helped is not None:
                self.helped.keys_act(a, j)

    def pe(self, t):
        c, s = self.c, self.s
        self.norm.pe(t)
        self.norm.turn.wait(t, NG)

        def scores(j):
            t.wait_ge(s["operands"], j // 2 + 1)
            if j >= 2:
                t.wait_ge(s["biased"], j - 1)
            t.matmul(c.bank[j % 2][:, :], c.XT[:, j * P:(j + 1) * P],
                     self.keys[:, j // 2, :, :].rearrange("p h k -> p (h k)"), start=True, stop=True) \
                .then_inc(s["scores"], 1)

        def turn(j):
            u = j % 2
            t.wait_ge(s["exp"], j + 1)
            if j >= 2:
                t.wait_ge(s["p_turned"], j - 1)
            for k in range(4):
                last = t.transpose(c.bank[2 + u][:, k * P:(k + 1) * P], self.prob[:, j % 3, k * P:(k + 1) * P],
                                   c.ident[:])
            last.then_inc(s["p_t"], 1)

        def values(j):
            u = j % 2
            t.wait_ge(s["p_turned"], j + 1)
            if j >= 2:
                t.wait_ge(s["added"], j - 1)
            for k in range(4):
                last = t.matmul(c.bank[4 + u][:, k * 34:(k + 1) * 34], self.probT[:, u, k * P:(k + 1) * P],
                                self.vals[:, j // 2, 2 * k:2 * k + 2, :].rearrange("p h n -> p (h n)"),
                                start=True, stop=True)
            last.then_inc(s["av"], 1)

        scores(0)
        scores(1)
        for j in range(NT):
            turn(j)
            if j + 2 < NT:
                scores(j + 2)
            if j:
                values(j - 1)
            if self.helped is not None:
                self.helped.keys_pe(t, j)
        values(NT - 1)
        if self.helped is not None:
            t.wait_ge(self.helped.s["copied_a"], NT)


class Ranks:

    def __init__(self, c, name):
        self.c = c
        self.counted = c.sem(name + "_rank_products")
        self.own = c.dve_chain

    def pe(self, t, chosen):
        c = self.c
        t.matmul(c.bank[1][:, 0:NT * E], c.before[:], chosen, start=True, stop=True)
        t.matmul(c.bank[2][:, 0:NT * E], c.ones[:], chosen, start=True, stop=True).then_inc(self.counted, 1)

    def dve(self, v, ranks, totals, running, zeros):
        c, own = self.c, self.own
        own.link(v, v.memset(zeros, 0.0))
        v.wait_ge(self.counted, 1)
        own.link(v, v.tensor_copy(totals, c.bank[2][:, 0:NT * E].rearrange("p (j e) -> p j e", e=E)))
        for e in range(E):
            last = v.tensor_tensor_scan(running[:, :, e], totals[:, :, e], zeros, 0.0, ALU.add, ALU.add)
        own.link(v, last)
        own.link(v, v.tensor_tensor(running, running, totals, ALU.subtract))
        own.link(v, v.tensor_tensor(ranks, c.bank[1][:, 0:NT * E].rearrange("p (j e) -> p j e", e=E), running,
                                    ALU.add))


class CapacityStage:

    CAPACITY = math.ceil(B * S / E * 1.25)

    def __init__(self, c):
        self.c, self.all_added = c, NT * E
        sc, d = c.scratch(), c.d
        self.norm = Norm(c, c.X, c.XN, 1.0, EPS, c.XT)
        self.router_w = c.sb("f_router_w", [P, E])
        self.w_gate = c.sb("f_w_gate", [P, 256])
        self.w_down = c.late[:, 2048:4096].rearrange("p (k n) -> p k n", k=2)
        self.load = (Load(c, "f").add(self.router_w[:], d["L2_ffn_w_router"]).add(self.w_gate[:], d["L2_ffn_w_gate"])
                     .add(self.w_down, d["L2_ffn_w_down"]))
        self.hidden = sc.take(2 * NT * P).rearrange("p (k n) -> p k n", k=2)
        self.own = c.dve_chain
        self.router = Router(c)
        self.ranks = Ranks(c, "f")
        self.s = c.signals("f", "chosen hidden_in hidden result combine added")

    def dve(self, v):
        c, s, own, r = self.c, self.s, self.own, self.c.routing
        self.norm.dve(v)
        shape = (P, NT, E)
        prob, left, one, two, chosen, ranks, totals, running = (r.table(k) for k in range(8))
        m1, m2, i1, i2, zeros, total = (r.rows(k) for k in range(6))
        self.router.softmax(v, self.router.logits(v), prob, m1)
        r.first(v, own, prob, m1, one, i1)
        r.hide(v, own, prob, one, left)
        r.first(v, own, left, m2, two, i2)
        v.tensor_tensor(chosen, one, two, ALU.add).then_inc(s["chosen"], 1)
        v.wait_ge(s["chosen"], 1)
        self.ranks.dve(v, ranks, totals, running, zeros)
        own.link(v, v.tensor_scalar(ranks, ranks, float(self.CAPACITY), None, ALU.is_lt))
        own.link(v, v.tensor_tensor(one, one, bc(m1[:, :, None], shape), ALU.mult))
        own.link(v, v.tensor_tensor(two, two, bc(m2[:, :, None], shape), ALU.mult))
        own.link(v, v.tensor_tensor(one, one, two, ALU.add))
        own.link(v, v.tensor_tensor(one, one, ranks, ALU.mult))
        own.link(v, v.tensor_reduce(total, one, AX.X, ALU.add))
        own.link(v, v.tensor_scalar(total, total, 1.0e-6, None, ALU.add))
        own.link(v, v.reciprocal(total, total))
        own.link(v, v.tensor_tensor(one, one, bc(total[:, :, None], shape), ALU.mult))
        v.tensor_scalar(one, one, c.gates[:, 6:7], None, ALU.mult).then_inc(s["combine"], 1)
        v.wait_ge(s["combine"], 1)
        n = 0
        for q in range(NT // 2):
            v.wait_ge(s["result"], q + 1)
            for e in range(E):
                for i in range(2):
                    j = 2 * q + i
                    if e:
                        v.wait_ge(s["added"], n - 1)
                    bank = c.bank[4 - 4 * (q % 2) + 2 * i + e // 4]
                    v.scalar_tensor_tensor(c.X[:, j, :], bank[:, (e % 4) * D:(e % 4 + 1) * D],
                                           one[:, j, e:e + 1], c.X[:, j, :], ALU.mult, ALU.add) \
                        .then_inc(s["added"], 1)
                    n += 1
            if q % 2 and self.next is not None:
                v.wait_ge(s["added"], n)
                self.next.norm.stats(v, q // 2)

    def pool(self, g):
        self.norm.pool(g)
        if self.next is not None:
            g.wait_ge(self.before.s["added"], self.before.all_added)
            self.next.prepare(g)

    def act(self, a):
        c, s = self.c, self.s
        self.norm.act(a)
        self.router.act(a, c.routing.table(0))
        for n in range(2 * NG):
            k, q = n % 2, n // 2
            a.wait_ge(s["hidden_in"], n + 1)
            a.activation(self.hidden[:, k, q * CHUNK:(q + 1) * CHUNK], c.bank[4 + n % 4][:, :], ACT.Silu) \
                .then_inc(s["hidden"], 1)

    def pe(self, t):
        c, s = self.c, self.s
        self.norm.pe(t)
        self.load.wait(t)
        self.norm.turn.wait(t, NG)
        self.router.pe(t, self.router_w[:])
        for n in range(2 * NG):
            k, q = n % 2, n // 2
            if n >= 4:
                t.wait_ge(s["hidden"], n - 3)
            t.matmul(c.bank[4 + n % 4][:, :], self.w_gate[:, k * P:(k + 1) * P],
                     c.XT[:, q * CHUNK:(q + 1) * CHUNK], start=True, stop=True).then_inc(s["hidden_in"], 1)
        t.wait_ge(s["hidden"], 2 * NG)
        for q in range(NT // 2):
            if q == 1:
                t.wait_ge(s["chosen"], 1)
                self.ranks.pe(t, c.routing.table(4).rearrange("p j e -> p (j e)"))
                t.wait_ge(s["combine"], 1)
            if q >= 2:
                t.wait_ge(s["added"], 2 * E * (q - 1))
            for i in range(2):
                j = 2 * q + i
                for half in range(2):
                    for k in range(2):
                        last = t.matmul(c.bank[4 - 4 * (q % 2) + 2 * i + half][:, :],
                                        self.hidden[:, k, j * P:(j + 1) * P],
                                        self.w_down[:, k, half * 512:(half + 1) * 512],
                                        start=(k == 0), stop=(k == 1))
            last.then_inc(s["result"], 1)


class NullStage:

    H, DH = 16, 64
    SCALE = 64 ** -0.5

    def __init__(self, c):
        self.c, self.all_added = c, NG
        sc, d = c.scratch(), c.d
        ar = Arena(c.arena_tensor, 10240)
        self.norm = Norm(c, c.X, c.XN, 1.0, EPS, c.XT)
        self.Wq = c.sb("g_Wq", [P, 8, D])
        self.Wkv = c.wide[:, :].rearrange("p (k n) -> p k n", k=2)
        self.Wout = c.sb("g_Wout", [P, 8, D])
        self.affine = c.sb("g_affine", [P, 2, D])
        self.null = c.sb("g_null", [P, 2])
        self.load = (Load(c, "g").add(self.Wq[:], d["L3_xattn_Wq"]).add(self.Wkv, d["L3_xattn_Wkv"])
                     .add(self.Wout[:], d["L3_xattn_Wout"])
                     .add(self.affine[:, 0, :], d["L3_xattn_ln_scale"].partition_broadcast(P))
                     .add(self.affine[:, 1, :], d["L3_xattn_ln_bias"].partition_broadcast(P))
                     .add(self.null[0:64, :], d["L3_xattn_null_kv"]).add(self.null[64:128, :], d["L3_xattn_null_kv"]))
        self.keys = ar.take(B * 1024).rearrange("p (b n) -> p b n", b=B)
        self.null_rows = ar.take(2 * 128).rearrange("p (k n) -> p k n", k=2)
        self.null_keys = ar.take(16)
        self.null_scores = ar.take(16 * NT)
        self.null_vals = ar.take(D)[0:16, :]
        self.null_probT = ar.take(2 * P)[0:16, :].rearrange("p (u n) -> p u n", u=2)
        self.top = ar.take(3 * 16).rearrange("p (u h) -> p u h", u=3)
        self.sums = ar.take(3 * 16).rearrange("p (u h) -> p u h", u=3)
        self.vals = sc.take(B * 1024).rearrange("p (b k d) -> p b k d", b=B, k=8)
        self.kv_keys = c.scratch().take(2048).rearrange("p (u b a n) -> p u b a n", u=2, b=B, a=2)
        room = sc.take(3 * 1040 + 1024)
        self.kv = room[:, 0:4096].rearrange("p (u b a n) -> p u b a n", u=4, b=B, a=2)
        self.prob = room[:, 0:3120].rearrange("p (u n) -> p u n", u=3)
        self.probT = room[:, 3120:4144]
        self.own, self.zeros = c.dve_chain, 0
        self.post = Norm(c, c.XN, c.XN, 1.0, 1.0e-6)
        self.s = c.signals("g", "zeroed null_set nulls nulls_copied kv kv_even kv_odd folded copied_a copied_b "
                                "scores null_scores shifted exp summed divided p_t p_turned out "
                                "out_copied added")

    def prepare(self, g):
        c, s = self.c, self.s
        self.load.wait(g)
        g.memset(self.null_rows, 0.0).then_inc(s["zeroed"], 1)
        self.zeros += 1
        g.wait_ge(s["zeroed"], self.zeros)
        self.zero_others(g, self.kv)
        for k in range(2):
            g.tensor_copy(self.null_rows[0:64, k, 0:P:18], bc(self.null[0:64, k:k + 1], (64, 8))) \
                .then_inc(s["null_set"], 1)
            g.tensor_copy(self.null_rows[64:128, k, 1:P:18], bc(self.null[64:128, k:k + 1], (64, 8))) \
                .then_inc(s["null_set"], 1)
        g.wait_ge(s["null_set"], 4)

    def zero_others(self, g, kv):
        for half in range(2):
            rows = slice(64 * (1 - half), 64 * (1 - half) + 64)
            g.memset(kv[rows, :, :, half, :], 0.0).then_inc(self.s["zeroed"], 1)
            self.zeros += 1
            g.wait_ge(self.s["zeroed"], self.zeros)

    def keys_pe(self, t, j):
        c, s, k = self.c, self.s, j // 2
        if j == 0:
            self.load.wait(t)
            t.wait_ge(s["zeroed"], 2)
        if j % 2 == 0:
            if k:
                t.wait_ge(s["copied_a"], 2 * k)
            for i in range(2):
                last = t.matmul(c.bank[6][:, :], self.Wkv[:, i, k * P:(k + 1) * P], c.CT[:, i, :],
                                start=(i == 0), stop=(i == 1))
            last.then_inc(s["kv"], 1)
        else:
            t.wait_ge(s["kv_even"], 2 * k + 2)
            for q in range(2):
                t.matmul(c.bank[7 - q][:, :], self.Wq[:, k, :],
                         self.kv_keys[:, k % 2, 4 * q:4 * q + 4, :, :].rearrange("p b a n -> p (b a n)"),
                         start=True, stop=True).then_inc(s["folded"], 1)

    def keys_act(self, a, j):
        c, s, k = self.c, self.s, j // 2
        if j == 0:
            a.wait_ge(s["zeroed"], 2)
        if j % 2 == 0:
            a.wait_ge(s["kv"], k + 1)
            for half in range(2):
                rows = slice(64 * half, 64 * half + 64)
                a.activation(self.kv_keys[rows, k % 2, :, half, :],
                             c.bank[6][rows, :].rearrange("p (b n) -> p b n", b=B), ACT.Copy) \
                    .then_inc(s["kv_even"], 1)
        else:
            for q in range(2):
                a.wait_ge(s["folded"], 2 * k + q + 1)
                a.activation(self.keys[:, 4 * q:4 * q + 4, 128 * k:128 * k + 128],
                             c.bank[7 - q][:, :].rearrange("p (b n) -> p b n", b=4), ACT.Copy,
                             scale=self.SCALE).then_inc(s["copied_a"], 1)

    def pool(self, g):
        c, s = self.c, self.s
        self.norm.pool(g)
        shift = self.affine[:, 1, :]
        c.pool_chain.link(g, g.tensor_scalar(shift, shift, c.gates[:, 3:4], None, ALU.mult))
        self.norm.wait_normed(g, NT)
        for j in range(NT):
            g.wait_ge(s["summed"], 2 * (j + 1))
            main = self.prob[:, j % 3, 0:1024].rearrange("p (h k) -> p h k", h=16)
            g.tensor_tensor(main, main, bc(self.sums[:, j % 3, :][:, :, None], (P, 16, 64)), ALU.mult) \
                .then_inc(s["divided"], 1)
            g.tensor_tensor(self.prob[:, j % 3, 1024:1040], self.prob[:, j % 3, 1024:1040],
                            self.sums[:, j % 3, :], ALU.mult).then_inc(s["divided"], 1)
            if j % 2 and j < 2 * NG:
                tiles = c.X[:, GROUP * (j // 2):GROUP * (j // 2) + GROUP, :]
                c.pool_chain.link(g, g.tensor_tensor(tiles, tiles, bc(shift[:, None, :], (P, GROUP, D)), ALU.add))
        self.post.pool(g)

    def pe(self, t):
        c, s, bank = self.c, self.s, self.c.bank
        self.load.wait(t)
        t.wait_ge(self.before.s["added"], self.before.all_added)
        t.wait_ge(s["null_set"], 4)
        for k in range(8):
            t.matmul(bank[0][:, 0:16], self.Wq[:, k, :], self.null_rows[:, 0, 16 * k:16 * k + 16],
                     start=(k == 0), stop=(k == 7))
        for k in range(8):
            last = t.matmul(bank[1][0:16, 0:D], self.null_rows[:, 1, 16 * k:16 * k + 16], self.Wout[:, k, :],
                            start=(k == 0), stop=(k == 7))
        last.then_inc(s["nulls"], 1)

        def project(n):
            if n >= 2:
                t.wait_ge(s["kv_even"], 16 + n - 1)
                t.wait_ge(s["kv_odd"], n - 1)
            for k in range(2):
                last = t.matmul(bank[2 + n % 2][:, :], self.Wkv[:, k, (8 + n) * P:(9 + n) * P], c.CT[:, k, :],
                                start=(k == 0), stop=(k == 1))
            last.then_inc(s["kv"], 1)

        def fold(n):
            t.wait_ge(s["kv_even"], 16 + n + 1)
            t.wait_ge(s["kv_odd"], n + 1)
            for q in range(2):
                m = 2 * n + q
                if m >= 4 and q == 0:
                    t.wait_ge(s["copied_a"], 16 + n - 1)
                elif m >= 4:
                    t.wait_ge(s["copied_b"], n - 1)
                for b in range(4):
                    last = t.matmul(bank[4 + m % 4][:, b * D:(b + 1) * D],
                                    self.kv[:, n % 4, 4 * q + b, :, :].rearrange("p a n -> p (a n)"),
                                    self.Wout[:, n, :], start=True, stop=True)
                last.then_inc(s["folded"], 1)

        t.wait_ge(s["zeroed"], 5)
        project(0)
        project(1)
        for n in range(8):
            if n + 2 < 8:
                project(n + 2)
            fold(n)
        t.wait_ge(s["copied_a"], 24)
        t.wait_ge(s["copied_b"], 8)
        self.norm.pe(t)
        self.norm.turn.wait(t, NG)
        t.wait_ge(s["nulls_copied"], 2)

        def scores(j):
            if j >= 2:
                t.wait_ge(s["shifted"], 2 * (j - 1))
            for half in range(2):
                last = t.matmul(bank[2 * (j % 2) + half][:, :], c.XT[:, j * P:(j + 1) * P],
                                self.keys[:, j // 2, half * 512:(half + 1) * 512], start=True, stop=True)
            last.then_inc(s["scores"], 1)

        for j in range(NT):
            last = t.matmul(bank[5][:, 16 * j:16 * j + 16], c.XT[:, j * P:(j + 1) * P], self.null_keys,
                            start=True, stop=True)
        last.then_inc(s["null_scores"], 1)

        def turn(j):
            t.wait_ge(s["divided"], 2 * j + 2)
            if j:
                t.wait_ge(s["p_turned"], 3 * j)
            if j >= 2:
                t.wait_ge(s["out_copied"], j - 1)
            if j == 0:
                t.wait_ge(s["shifted"], 2)
            for k in range(8):
                last = t.transpose(bank[6 + k // 4][:, (k % 4) * P:(k % 4 + 1) * P],
                                   self.prob[:, j % 3, k * P:(k + 1) * P], c.ident[:])
                if k == 3:
                    last.then_inc(s["p_t"], 1)
            last.then_inc(s["p_t"], 1)
            t.transpose(bank[4 + j % 2][0:16, P:2 * P], self.prob[:, j % 3, 1024:1040], c.ident[:]) \
                .then_inc(s["p_t"], 1)

        def values(j):
            t.wait_ge(s["p_turned"], 3 * j + 3)
            out = bank[4 + j % 2][:, 256:256 + D]
            for k in range(8):
                t.matmul(out, self.probT[:, k * P:(k + 1) * P], self.vals[:, j // 2, k, :], start=(k == 0),
                         stop=False)
            t.matmul(out, self.null_probT[:, j % 2, :], self.null_vals, start=False, stop=True) \
                .then_inc(s["out"], 1)

        scores(0)
        scores(1)
        scores(2)
        for j in range(NT):
            turn(j)
            if j + 3 < NT:
                scores(j + 3)
            values(j)

    def act(self, a):
        c, s, bank = self.c, self.s, self.c.bank
        a.wait_ge(s["nulls"], 1)
        a.activation(self.null_keys, bank[0][:, 0:16], ACT.Copy, scale=self.SCALE).then_inc(s["nulls_copied"], 1)
        a.activation(self.null_vals, bank[1][0:16, 0:D], ACT.Copy).then_inc(s["nulls_copied"], 1)

        def take_half(n):
            a.wait_ge(s["kv"], 8 + n + 1)
            if n >= 4:
                a.wait_ge(s["folded"], 16 + 2 * (n - 3))
            a.activation(self.kv[0:64, n % 4, :, 0, :], bank[2 + n % 2][0:64, :].rearrange("p (b n) -> p b n", b=B),
                         ACT.Copy).then_inc(s["kv_even"], 1)

        def take_fold(n):
            a.wait_ge(s["folded"], 16 + 2 * n + 1)
            a.activation(self.vals[:, 0:4, n, :], bank[4 + 2 * (n % 2)][:, :].rearrange("p (b n) -> p b n", b=4),
                         ACT.Copy).then_inc(s["copied_a"], 1)

        a.wait_ge(s["zeroed"], 5)
        take_half(0)
        take_half(1)
        for n in range(8):
            if n + 2 < 8:
                take_half(n + 2)
            take_fold(n)
        self.norm.act(a)

        def exponentials(j):
            a.wait_ge(s["shifted"], 2 * j + 2)
            a.activation(self.prob[:, j % 3, :], self.prob[:, j % 3, :], ACT.Exp).then_inc(s["exp"], 1)

        def copy_turned(j):
            for k in range(2):
                a.wait_ge(s["p_t"], 3 * j + k + 1)
                if j:
                    a.wait_ge(s["out"], j)
                a.activation(self.probT[:, k * 512:(k + 1) * 512], bank[6 + k][:, :], ACT.Copy) \
                    .then_inc(s["p_turned"], 1)
            a.wait_ge(s["p_t"], 3 * j + 3)
            a.activation(self.null_probT[:, j % 2, :], bank[4 + j % 2][0:16, P:2 * P], ACT.Copy) \
                .then_inc(s["p_turned"], 1)

        def copy_result(j):
            a.wait_ge(s["out"], j + 1)
            a.activation(c.XN[:, j, :], bank[4 + j % 2][:, 256:256 + D], ACT.Copy).then_inc(s["out_copied"], 1)

        exponentials(0)
        exponentials(1)
        for j in range(NT):
            copy_turned(j)
            if j + 2 < NT:
                exponentials(j + 2)
            copy_result(j)

    def dve(self, v):
        c, s, own, bank = self.c, self.s, self.own, self.c.bank

        def take_half(n):
            v.wait_ge(s["kv"], 8 + n + 1)
            if n >= 4:
                v.wait_ge(s["folded"], 16 + 2 * (n - 3))
            v.tensor_copy(self.kv[64:128, n % 4, :, 1, :],
                          bank[2 + n % 2][64:128, :].rearrange("p (b n) -> p b n", b=B)).then_inc(s["kv_odd"], 1)

        def take_fold(n):
            v.wait_ge(s["folded"], 16 + 2 * n + 2)
            v.tensor_copy(self.vals[:, 4:8, n, :],
                          bank[5 + 2 * (n % 2)][:, :].rearrange("p (b n) -> p b n", b=4)).then_inc(s["copied_b"], 1)

        v.wait_ge(s["zeroed"], 5)
        take_half(0)
        take_half(1)
        for n in range(8):
            if n + 2 < 8:
                take_half(n + 2)
            take_fold(n)
        self.norm.dve(v)

        own.link(v, v.tensor_scalar(self.affine[:, 0, :], self.affine[:, 0, :], c.gates[:, 3:4], None, ALU.mult))

        def softmax(j):
            u = j % 3
            main_in = c.psum[:, 2 * (j % 2):2 * (j % 2) + 2, :].rearrange("p k (h n) -> p (k h) n", n=64)
            null_in = self.null_scores[:, 16 * j:16 * j + 16]
            main = self.prob[:, u, 0:1024].rearrange("p (h n) -> p h n", n=64)
            null = self.prob[:, u, 1024:1040]
            top, sums = self.top[:, u, :], self.sums[:, u, :]
            v.wait_ge(s["scores"], j + 1)
            own.link(v, v.tensor_reduce(top, main_in, AX.X, ALU.max))
            own.link(v, v.tensor_tensor(top, null_in, top, ALU.max))
            if j >= 3:
                v.wait_ge(s["p_t"], 3 * (j - 2))
            v.tensor_tensor(main, main_in, bc(top[:, :, None], (P, 16, 64)), ALU.subtract) \
                .then_inc(s["shifted"], 1)
            v.tensor_tensor(null, null_in, top, ALU.subtract).then_inc(s["shifted"], 1)

        def sums(j):
            u = j % 3
            total = self.sums[:, u, :]
            main = self.prob[:, u, 0:1024].rearrange("p (h n) -> p h n", n=64)
            v.wait_ge(s["exp"], j + 1)
            if j >= 3:
                v.wait_ge(s["divided"], 2 * (j - 2))
            own.link(v, v.tensor_reduce(total, main, AX.X, ALU.add))
            v.tensor_tensor(total, total, self.prob[:, u, 1024:1040], ALU.add).then_inc(s["summed"], 1)
            v.wait_ge(s["summed"], 2 * j + 1)
            v.reciprocal(total, total).then_inc(s["summed"], 1)

        v.wait_ge(s["null_scores"], 1)
        own.link(v, v.tensor_copy(self.null_scores, bank[5][:, 0:256]))
        softmax(0)
        softmax(1)
        sums(0)
        for j in range(NT):
            if j + 2 < NT:
                softmax(j + 2)
            if j + 1 < NT:
                sums(j + 1)
            if j % GROUP == 1 and j > GROUP:
                self.post.stats(v, j // GROUP - 1, s["out_copied"])
        for q in range(self.post.at, NG):
            self.post.stats(v, q, s["out_copied"])
        for q in range(NG):
            self.post.add_to(v, q, self.affine[:, 0, :], c.X, s["added"])
            if self.next is not None:
                v.wait_ge(s["added"], q + 1)
                self.next.norm.stats(v, q)


class DispatchStage:

    CAPACITY = math.ceil(B * S * 1.0 / E)
    SLOTS = E * CAPACITY
    TILES = CAPACITY // P

    def __init__(self, c):
        self.c, self.all_added = c, NT
        sc, d = c.scratch(), c.d
        assert self.CAPACITY == self.TILES * P
        self.norm = Norm(c, c.X, c.XN, 1.0, EPS, c.XT)
        self.router_w = c.sb("h_router_w", [P, E])
        self.w1 = c.wide[:, :].rearrange("p (e n) -> p e n", e=E)
        self.w2 = c.late[:, :].rearrange("p (e k d) -> p e k d", e=E, k=4)
        self.load = Load(c, "h").add(self.router_w[:], d["L3_ffn_Wr"])
        self.expert_load = Load(c, "h_experts").add(self.w1, d["L3_ffn_W1"].rearrange("e d f -> d e f"))
        for e in range(E):
            self.expert_load.add(self.w2[:, e], d["L3_ffn_W2"][e].rearrange("(k f) d -> f k d", k=4))
        self.taken = c.nc.dram_tensor("slots_in", (self.SLOTS, D), F32).ap()
        self.given = c.nc.dram_tensor("slots_out", (self.SLOTS, D), F32).ap()
        self.rows = sc.take(NT * D).rearrange("p (j d) -> p j d", j=NT)
        self.hidden = sc.take(2 * 1024).rearrange("p (u k n) -> p u k n", u=2, k=4)
        self.results = sc.take(NT * D).rearrange("p (j d) -> p j d", j=NT)
        self.scatter_at = c.sb("h_scatter_at", [P, NT], I32)
        self.gather_at = c.sb("h_gather_at", [P, NT], I32)
        self.own = c.dve_chain
        self.router = Router(c)
        self.ranks = Ranks(c, "h")
        self.s = c.signals("h", "cleared chosen slots scattered fetched hidden_in hidden_a "
                                "hidden_v result copied stored gathered0 gathered1 gathered2 gathered3 added")
        self.gathered = [self.s["gathered%d" % q] for q in range(NG)]
        self.slot_turn = Turn(c, self.rows, c.XT, self.s["fetched"], 0, 16 * NG)

    def clear(self, sp):
        c = self.c
        sp.wait_ge(c.zeroed, 1)
        for j in range(NT):
            sp.dma_start(self.taken[j * P:(j + 1) * P, :], c.zero_tile[:]).then_inc(self.s["cleared"], 16)

    def pool(self, g):
        c, s = self.c, self.s
        self.norm.pool(g)
        g.wait_ge(s["slots"], 1)
        g.wait_ge(s["cleared"], 16 * NT)
        for j in range(NT):
            g.indirect_dma_start(self.taken, bass.IndirectOffsetOnAxis(ap=self.scatter_at[:, j:j + 1], axis=0),
                                 c.XN[:, j, :], None, bounds_check=self.SLOTS - 1, oob_is_err=False) \
                .then_inc(s["scattered"], 16)
        g.wait_ge(s["stored"], 16 * E)
        for j in range(NT):
            g.indirect_dma_start(self.rows[:, j, :], None, self.given,
                                 bass.IndirectOffsetOnAxis(ap=self.gather_at[:, j:j + 1], axis=0),
                                 bounds_check=self.SLOTS - 1, oob_is_err=False) \
                .then_inc(self.gathered[j // GROUP], 16)

    def sync(self, sp):
        s = self.s
        sp.wait_ge(s["scattered"], 16 * NT)
        for q in range(NG):
            sp.dma_start(self.rows[:, GROUP * q:GROUP * q + GROUP, :],
                         self.taken.rearrange("(j p) d -> p j d", p=P)[:, GROUP * q:GROUP * q + GROUP, :]) \
                .then_inc(s["fetched"], 16)
        for e in range(E):
            j = self.TILES * e
            sp.wait_ge(s["copied"], e + 1)
            sp.dma_start(self.given.rearrange("(j p) d -> p j d", p=P)[:, j:j + self.TILES, :],
                         self.results[:, j:j + self.TILES, :]).then_inc(s["stored"], 16)

    def dve(self, v):
        c, s, own, r = self.c, self.s, self.own, self.c.routing
        self.norm.dve(v)
        shape = (P, NT, E)
        prob, tmp, one, chosen_at, ranks, totals, running = (r.table(k) for k in range(7))
        m1, i1, zeros, rank, kept, slot, weight = (r.rows(k) for k in range(7))
        self.router.softmax(v, self.router.logits(v), prob, m1)
        r.first(v, own, prob, m1, one, i1)
        v.tensor_copy(chosen_at, one).then_inc(s["chosen"], 1)
        self.ranks.dve(v, ranks, totals, running, zeros)
        own.link(v, v.tensor_tensor(ranks, ranks, one, ALU.mult))
        own.link(v, v.tensor_reduce(rank, ranks, AX.X, ALU.add))
        own.link(v, v.tensor_scalar(kept, rank, float(self.CAPACITY), None, ALU.is_lt))
        own.link(v, v.tensor_scalar(slot, i1, float(E), float(self.CAPACITY), ALU.add, ALU.mult))
        own.link(v, v.tensor_tensor(slot, slot, rank, ALU.add))
        own.link(v, v.tensor_tensor(slot, slot, kept, ALU.mult))
        own.link(v, v.tensor_copy(self.gather_at[:], slot))
        own.link(v, v.tensor_scalar(rank, kept, -float(2 * self.SLOTS), float(2 * self.SLOTS), ALU.mult, ALU.add))
        own.link(v, v.tensor_tensor(slot, slot, rank, ALU.add))
        own.link(v, v.tensor_tensor(weight, m1, kept, ALU.mult))
        own.link(v, v.tensor_scalar(weight, weight, c.gates[:, 7:8], None, ALU.mult))
        v.tensor_copy(self.scatter_at[:], slot).then_inc(s["slots"], 1)
        for e in range(E):
            v.wait_ge(s["hidden_in"], 2 * e + 2)
            if e >= 2:
                v.wait_ge(s["result"], e - 1)
            v.tensor_scalar(self.hidden[:, e % 2, 2:4, :].rearrange("p k n -> p (k n)"),
                            c.bank[2 * (e % 2) + 1][:, :], 0.0, None, ALU.max).then_inc(s["hidden_v"], 1)
        for j in range(NT):
            v.wait_ge(self.gathered[j // GROUP], 16 * GROUP)
            v.scalar_tensor_tensor(c.X[:, j, :], self.rows[:, j, :], weight[:, j:j + 1], c.X[:, j, :],
                                   ALU.mult, ALU.add).then_inc(s["added"], 1)

    def act(self, a):
        c, s = self.c, self.s
        self.norm.act(a)
        self.router.act(a, c.routing.table(0))
        self.slot_turn.act(a)

        def copy(e):
            a.wait_ge(s["result"], e + 1)
            a.activation(self.results[:, self.TILES * e:self.TILES * (e + 1), :].rearrange("p j d -> p (j d)"),
                         c.bank[4 + e % 2][:, 0:self.TILES * D], ACT.Copy).then_inc(s["copied"], 1)

        for e in range(E):
            a.wait_ge(s["hidden_in"], 2 * e + 1)
            if e >= 2:
                a.wait_ge(s["result"], e - 1)
            a.activation(self.hidden[:, e % 2, 0:2, :].rearrange("p k n -> p (k n)"),
                         c.bank[2 * (e % 2)][:, :], ACT.Relu).then_inc(s["hidden_a"], 1)
            if e:
                copy(e - 1)
        copy(E - 1)

    def pe(self, t):
        c, s = self.c, self.s
        self.norm.pe(t)
        self.load.wait(t)
        self.norm.turn.wait(t, NG)
        self.router.pe(t, self.router_w[:])
        t.wait_ge(s["chosen"], 1)
        self.ranks.pe(t, c.routing.table(3).rearrange("p j e -> p (j e)"))
        self.slot_turn.pe(t)
        self.expert_load.wait(t)
        t.wait_ge(s["slots"], 1)
        n = self.CAPACITY

        def first(e):
            self.slot_turn.wait(t, e // 2 + 1)
            if e >= 2:
                t.wait_ge(s["hidden_a"], e - 1)
                t.wait_ge(s["hidden_v"], e - 1)
            for k in range(4):
                last = t.matmul(c.bank[2 * (e % 2) + k // 2][:, (k % 2) * n:(k % 2 + 1) * n],
                                self.w1[:, e, k * P:(k + 1) * P], c.XT[:, e * n:(e + 1) * n], start=True, stop=True)
                if k % 2:
                    last.then_inc(s["hidden_in"], 1)

        def second(e):
            t.wait_ge(s["hidden_a"], e + 1)
            t.wait_ge(s["hidden_v"], e + 1)
            if e >= 2:
                t.wait_ge(s["copied"], e - 1)
            for i in range(self.TILES):
                for k in range(4):
                    last = t.matmul(c.bank[4 + e % 2][:, i * D:(i + 1) * D],
                                    self.hidden[:, e % 2, k, i * P:(i + 1) * P], self.w2[:, e, k, :],
                                    start=(k == 0), stop=(k == 3))
            last.then_inc(s["result"], 1)

        first(0)
        for e in range(E):
            if e + 1 < E:
                first(e + 1)
            second(e)


KINDS = (DepoolStage, ExpertPairStage, HeadsStage, AcrossStage, MaskedStage, CapacityStage, NullStage, DispatchStage,)


STAGES = 8


def build(nc, d, out):
    with ExitStack() as ctx:
        c = Core(nc, ctx, d)
        constants = Constants(c)
        c.arena_tensor = c.sb("arena", [P, 10240])
        c.late = c.sb("late", [P, 4096])
        c.wide = c.sb("wide", [P, 4096])
        c.routing = Routing(c)
        c.gates_in = c.sb("gates_in", [P, 8])
        c.gates_done = c.sem("gates_done")
        c.gate_load = (Load(c, "gates").add(c.gates_in[:, 0:4], d["g_xattn"].partition_broadcast(P))
                       .add(c.gates_in[:, 4:8], d["g_ffn"].partition_broadcast(P)))
        x_tiles = d["x"].rearrange("b (i p) d -> p (b i) d", p=P)
        x_load = Load(c, "x")
        for g in range(2):
            x_load.add(c.X[:, 8 * g:8 * g + 8, :], x_tiles[:, 8 * g:8 * g + 8, :])
        c2_load = (Load(c, "context").add(c.C2[0:64], d["ctx_2048"].rearrange("b s d -> s b d"))
                   .add(c.C2[64:128], d["ctx_2048"].rearrange("b s d -> s b d")))
        c.c2_load = c2_load
        stored = c.sem("stored")
        c.zero_tile, c.zeroed = c.sb("zero_tile", [P, D]), c.sem("zero_tile")
        stages = []
        for kind in KINDS[:STAGES]:
            stages.append(kind(c))
            stages[-1].before = stages[-2] if len(stages) > 1 else None
            stages[-1].next = None
            if len(stages) > 1:
                stages[-2].next = stages[-1]
        block = ctx.enter_context(nc.Block())

        dispatch = [st for st in stages if isinstance(st, DispatchStage)]

        @block.sync
        def _(sp):
            c.gate_load.issue(sp)
            x_load.issue(sp)
            for n, st in enumerate(stages):
                if n == 2:
                    c2_load.issue(sp)
                st.load.issue(sp)
                if isinstance(st, ExpertPairStage):
                    for load in st.expert_load:
                        load.issue(sp)
            for st in dispatch:
                st.clear(sp)
                if st.before is not None:
                    sp.wait_ge(st.before.before.s["result"], NT // 2)
                    sp.wait_ge(st.before.s["kv"], 16)
                st.expert_load.issue(sp)
                st.sync(sp)
            for g in range(NG):
                last = stages[-1]
                sp.wait_ge(last.s["added"], last.all_added * (g + 1) // NG)
                sp.dma_start(out.rearrange("b (i p) d -> p (b i) d", p=P)[:, GROUP * g:GROUP * g + GROUP, :],
                             c.X[:, GROUP * g:GROUP * g + GROUP, :]).then_inc(stored, 16)
            sp.wait_ge(stored, 16 * NG)

        @block.gpsimd
        def _(g):
            constants.pool(g)
            g.wait_ge(c.constants_done, 1)
            g.memset(c.zero_tile[:], 0.0).then_inc(c.zeroed, 1)
            for st in stages:
                st.pool(g)

        @block.scalar
        def _(a):
            for st in stages:
                st.act(a)

        @block.vector
        def _(v):
            x_load.wait(v)
            v.wait_ge(c.gates_done, 1)
            for n, st in enumerate(stages):
                if n:
                    v.wait_ge(stages[n - 1].s["added"], stages[n - 1].all_added)
                st.dve(v)

        @block.tensor
        def _(t):
            for st in stages:
                if st.before is not None:
                    t.wait_ge(st.before.s["added"], st.before.all_added)
                st.pe(t)


def kernel(**inputs):
    import numpy as np
    import concourse.bacc as bacc
    from concourse.bass_utils import run_bass_kernel_spmd

    given = {n: np.asarray(a) for n, a in inputs.items()}
    T = lambda n: given[n].T
    lay = {
        "x": given["x"],
        "ctx_pairs": given["ctx_2048"].reshape(4, 2, SC, DC).transpose(1, 2, 0, 3).reshape(P, 4, DC),
        "ctx_T": given["ctx_2048"].reshape(B * SC, 2, P).transpose(2, 1, 0),
        "ctx_2048": given["ctx_2048"],
        "patch_lens": given["mask_BxS2_if0"].reshape(4, P).T,
        "seq_mask": given["mask_BxS2_ik0"].reshape(B * SC),
        "g_xattn": given["g_xattn"], "g_ffn": given["g_ffn"],
        "L0_xattn_g_res": given["L0_xattn_g_res"].reshape(D, 1),
        "L0_xattn_W_in": T("L0_xattn_W_in"),
        "L0_ffn_b1": given["L0_ffn_b1"].reshape(2 * E, P).T,
        "L0_ffn_b2": given["L0_ffn_b2"].reshape(2 * E, P).T,
        "L0_ffn_bg": given["L0_ffn_bg"].reshape(2 * E, P).T,
        "L1_xattn_w_qkv": T("L1_xattn_w_qkv"), "L1_xattn_w_proj": T("L1_xattn_w_proj"),
        "L1_ffn_in_proj_w": T("L1_ffn_in_proj_w"), "L1_ffn_out_w": T("L1_ffn_out_w"),
        "L1_ffn_router_w": T("L1_ffn_router_w"), "L1_ffn_b1": T("L1_ffn_b1"),
        "L1_ffn_w1": given["L1_ffn_w1"].transpose(2, 0, 1), "L1_ffn_w2": given["L1_ffn_w2"].transpose(2, 0, 1),
        "L2_ffn_w_router": T("L2_ffn_w_router"), "L2_ffn_w_gate": T("L2_ffn_w_gate"),
        "L2_ffn_w_down": given["L2_ffn_w_down"].transpose(2, 0, 1).reshape(2, P, E * D).transpose(1, 0, 2),
        "L3_xattn_null_kv": T("L3_xattn_null_kv"),
        "L3_xattn_Wq": given["L3_xattn_Wq"].T.reshape(8, P, D).transpose(1, 0, 2),
        "L3_xattn_Wkv": given["L3_xattn_Wkv"].reshape(2, P, 2048).transpose(1, 0, 2),
        "L3_xattn_Wout": given["L3_xattn_Wout"].reshape(8, P, D).transpose(1, 0, 2),
    }
    for n in ("L0_xattn_b_in L0_xattn_g_init L0_ffn_gate_w L0_ffn_gate_b L0_ffn_w1 L0_ffn_w2 "
              "L0_ffn_wg L0_ffn_w3 L0_ffn_b3 L1_xattn_b_proj L1_ffn_in_proj_b L1_ffn_out_b L1_ffn_ln1_g "
              "L1_ffn_ln1_b L1_ffn_router_b L1_ffn_b2 L1_ffn_ln2_g L1_ffn_ln2_b L2_xattn_b "
              "L3_xattn_ln_scale L3_xattn_ln_bias L3_ffn_Wr L3_ffn_W1 L3_ffn_W2").split():
        lay[n] = given[n]
    nc = bacc.Bacc("TRN2", target_bir_lowering=False, num_devices=1)
    arrays, d = {}, {}
    for n, a in lay.items():
        a = np.ascontiguousarray(a)
        arrays["in_" + n] = a
        d[n] = nc.dram_tensor("in_" + n, a.shape, mybir.dt.from_np(a.dtype), kind="ExternalInput").ap()
    out = nc.dram_tensor("out_x", (B, S, D), F32, kind="ExternalOutput").ap()
    build(nc, d, out)
    r = run_bass_kernel_spmd(nc, [arrays], core_ids=[0])
    return r.results[0]["out_x"]
```
